# Optimizing a Trainium2 kernel written in Bass

```python
import numpy as np
import jax
import jax.numpy as jnp

def _softmax(x, axis=-1):
    return jax.nn.softmax(x, axis=axis)

def _gelu(x):
    return jax.nn.gelu(x, approximate=True)

def _silu(x):
    return jax.nn.silu(x)

def _sigmoid(x):
    return jax.nn.sigmoid(x)

def _layernorm(x, axis=-1, eps=1e-05):
    m = jnp.mean(x, axis=axis, keepdims=True)
    v = jnp.var(x, axis=axis, keepdims=True)
    return (x - m) / jnp.sqrt(v + eps)

def _scatter_add(tgt, idx, src, axis=0):
    return tgt.at[idx].add(src)

def _segment_sum(src, seg, n):
    return jax.ops.segment_sum(src, seg, n)
kernel_name = 'mk_early_fusion_d1_tok_img768_r4_32cb4b'

def setup_inputs(seed: int=0):
    np.random.seed(seed)
    _w = jnp.asarray

    def _rec_inputs():
        import jax
        import jax.numpy as jnp
        _rk = jax.random.key(seed)
        x = -0.000356955 + 1 * jax.random.normal(jax.random.fold_in(_rk, 1), (64, 3, 224, 224), jnp.float32)
        txt = 0.323316 + 0.855 * jax.random.normal(jax.random.fold_in(_rk, 2), (64, 32, 192), jnp.float32)
        return (x, txt)
    x, txt = _rec_inputs()

    def _L0_tok_setup():
        import jax, jax.numpy as jnp
        import numpy as np
        CHW = (3, 224, 224)
        N_PATCHES = 14
        HIDDEN_D = 192
        BATCH = 128
        PATCH = CHW[1] // N_PATCHES
        INPUT_D = CHW[0] * PATCH * PATCH
        SEQ = N_PATCHES * N_PATCHES + 1

        def get_positional_embeddings(seq, d):
            i = np.arange(seq)[:, None].astype(np.float32)
            j = np.arange(d)[None, :]
            even = j % 2 == 0
            exp = np.where(even, j, j - 1).astype(np.float32) / d
            angle = i / np.power(10000.0, exp)
            out = np.where(even, np.sin(angle), np.cos(angle)).astype(np.float32)
            return jnp.asarray(out)

        def patchify(images, n_patches):
            n, c, h, w = images.shape
            ps = h // n_patches
            x = images.reshape(n, c, n_patches, ps, n_patches, ps)
            x = x.transpose(0, 2, 4, 1, 3, 5)
            return x.reshape(n, n_patches * n_patches, c * ps * ps)
        key = jax.random.key(seed)
        k1, k2, k3, k4 = jax.random.split(key, 4)
        images = jax.random.normal(k1, (BATCH,) + CHW, dtype=jnp.float32)
        bound = 1.0 / np.sqrt(INPUT_D)
        W = jax.random.uniform(k2, (HIDDEN_D, INPUT_D), minval=-bound, maxval=bound, dtype=jnp.float32)
        b = jax.random.uniform(k3, (HIDDEN_D,), minval=-bound, maxval=bound, dtype=jnp.float32)
        class_token = jax.random.uniform(k4, (1, HIDDEN_D), dtype=jnp.float32)
        pos_embed = get_positional_embeddings(SEQ, HIDDEN_D)
        return {'images': images, 'W': W, 'b': b, 'class_token': class_token, 'pos_embed': pos_embed}
    _L0_tok_all = _L0_tok_setup()
    _L0_tok_in = {k: v for k, v in _L0_tok_all.items() if k in ('W', 'b', 'class_token', 'pos_embed')}
    del _L0_tok_all

    def _L0_attn_setup():
        import jax, jax.numpy as jnp
        import numpy as np
        D_MODEL = 192
        H = 6
        DQK = 128
        DV = 64
        SCALE_BASE = 512.0

        def _xpos(x, sign):
            B, T, Hn, d = x.shape
            half = d // 2
            pos = jnp.arange(T, dtype=jnp.float32)
            inv_freq = 1.0 / 10000.0 ** (jnp.arange(half, dtype=jnp.float32) / half)
            angles = pos[:, None] * inv_freq[None, :]
            zeta = (jnp.arange(half, dtype=jnp.float32) + half) / d
            decay = zeta[None, :] ** (sign * pos[:, None] / SCALE_BASE)
            cos_a = (jnp.cos(angles) * decay)[None, :, None, :]
            sin_a = (jnp.sin(angles) * decay)[None, :, None, :]
            x1, x2 = (x[..., :half], x[..., half:])
            return jnp.concatenate([x1 * cos_a - x2 * sin_a, x1 * sin_a + x2 * cos_a], axis=-1)

        def _decay_mask(T):
            gammas = jnp.array([1.0 - 2.0 ** (-(5 + h)) for h in range(H)], dtype=jnp.float32)
            i = jnp.arange(T, dtype=jnp.float32)
            diff = i[:, None] - i[None, :]
            causal = (diff >= 0).astype(jnp.float32)
            D = gammas[:, None, None] ** jnp.clip(diff, 0.0)[None] * causal[None]
            row = jnp.clip(jnp.sum(D, axis=-1, keepdims=True), 1e-06)
            return D / jnp.sqrt(row)
        key = jax.random.key(seed)
        ks = jax.random.split(key, 6)
        B, T = (2, 512)

        def xavier(k, shape):
            lim = float(np.sqrt(6.0 / (shape[0] + shape[1])))
            return jax.random.uniform(k, shape, jnp.float32, -lim, lim)
        return {'x': jax.random.normal(ks[0], (B, T, D_MODEL), jnp.float32), 'Wq': xavier(ks[1], (D_MODEL, H * DQK)), 'Wk': xavier(ks[2], (D_MODEL, H * DQK)), 'Wv': xavier(ks[3], (D_MODEL, H * DV)), 'Wg': xavier(ks[4], (D_MODEL, H * DV)), 'Wo': xavier(ks[5], (H * DV, D_MODEL)), 'gn_weight': jnp.ones((H * DV,), jnp.float32), 'gn_bias': jnp.zeros((H * DV,), jnp.float32)}
    _L0_attn_all = _L0_attn_setup()
    _L0_attn_in = {k: v for k, v in _L0_attn_all.items() if k in ('Wq', 'Wk', 'Wv', 'Wg', 'Wo', 'gn_weight', 'gn_bias')}
    del _L0_attn_all

    def _L0_ffn_setup():
        import jax, jax.numpy as jnp
        import numpy as np
        B, S, D = (2, 256, 192)
        I = 96
        E = 8
        G = 4
        TOPK_GROUPS = 2
        K = 2
        ROUTE_SCALE = 1.0
        ALPHA, LIMIT = (1.702, 7.0)

        def swiglu(h):
            xg = jnp.minimum(h[..., ::2], LIMIT)
            xl = jnp.clip(h[..., 1::2], -LIMIT, LIMIT)
            return xg * jax.nn.sigmoid(ALPHA * xg) * (xl + 1.0)

        def gate(x, gate_w, gate_b):
            scores = jax.nn.softmax(jnp.einsum('td,ed->te', x, gate_w).astype(jnp.float32), axis=-1)
            original_scores = scores
            s = scores + gate_b
            T = x.shape[0]
            sg = s.reshape(T, G, E // G)
            group_scores = jnp.sum(jax.lax.top_k(sg, 2)[0], axis=-1)
            _, gidx = jax.lax.top_k(group_scores, TOPK_GROUPS)
            keep = jnp.any(jax.nn.one_hot(gidx, G, dtype=jnp.bool_), axis=1)
            sg = jnp.where(keep[:, :, None], sg, -jnp.inf)
            s = sg.reshape(T, E)
            _, idx = jax.lax.top_k(s, K)
            w = jnp.take_along_axis(original_scores, idx, axis=1) * ROUTE_SCALE
            return (w.astype(x.dtype), idx)

        def expert_ffn(x, W1, B1, W3, B3, W2, B2):
            h1 = jnp.einsum('td,edh->teh', x, W1) + B1
            h3 = jnp.einsum('td,edh->teh', x, W3) + B3
            g = swiglu(h1 * h3)
            return jnp.einsum('tei,eid->ted', g, W2) + B2

        def shared_ffn(x, Ws1, Bs1, Ws3, Bs3, Ws2, Bs2):
            h = (x @ Ws1 + Bs1) * (x @ Ws3 + Bs3)
            return swiglu(h) @ Ws2 + Bs2
        key = jax.random.key(seed)
        ks = jax.random.split(key, 16)
        sc = 0.02
        inp = {'x': jax.random.normal(ks[0], (B, S, D), jnp.float32), 'gate_w': jax.random.normal(ks[1], (E, D), jnp.float32) * sc, 'gate_b': jax.random.normal(ks[2], (E,), jnp.float32) * sc, 'W1': jax.random.normal(ks[3], (E, D, 2 * I), jnp.float32) * sc, 'B1': jax.random.normal(ks[4], (E, 2 * I), jnp.float32) * sc, 'W3': jax.random.normal(ks[5], (E, D, 2 * I), jnp.float32) * sc, 'B3': jax.random.normal(ks[6], (E, 2 * I), jnp.float32) * sc, 'W2': jax.random.normal(ks[7], (E, I, D), jnp.float32) * sc, 'B2': jax.random.normal(ks[8], (E, D), jnp.float32) * sc, 'Ws1': jax.random.normal(ks[9], (D, 2 * I), jnp.float32) * sc, 'Bs1': jax.random.normal(ks[10], (2 * I,), jnp.float32) * sc, 'Ws3': jax.random.normal(ks[11], (D, 2 * I), jnp.float32) * sc, 'Bs3': jax.random.normal(ks[12], (2 * I,), jnp.float32) * sc, 'Ws2': jax.random.normal(ks[13], (I, D), jnp.float32) * sc, 'Bs2': jax.random.normal(ks[14], (D,), jnp.float32) * sc}
        return inp
    _L0_ffn_all = _L0_ffn_setup()
    _L0_ffn_in = {k: v for k, v in _L0_ffn_all.items() if k in ('gate_w', 'gate_b', 'W1', 'B1', 'W3', 'B3', 'W2', 'B2', 'Ws1', 'Bs1', 'Ws3', 'Bs3', 'Ws2', 'Bs2')}
    del _L0_ffn_all
    return {'x': x, 'txt': txt, 'L0_tok_W': _L0_tok_in['W'], 'L0_tok_b': _L0_tok_in['b'], 'L0_tok_class_token': _L0_tok_in['class_token'], 'L0_tok_pos_embed': _L0_tok_in['pos_embed'], 'L0_attn_Wq': _L0_attn_in['Wq'], 'L0_attn_Wk': _L0_attn_in['Wk'], 'L0_attn_Wv': _L0_attn_in['Wv'], 'L0_attn_Wg': _L0_attn_in['Wg'], 'L0_attn_Wo': _L0_attn_in['Wo'], 'L0_attn_gn_weight': _L0_attn_in['gn_weight'], 'L0_attn_gn_bias': _L0_attn_in['gn_bias'], 'L0_ffn_gate_w': _L0_ffn_in['gate_w'], 'L0_ffn_gate_b': _L0_ffn_in['gate_b'], 'L0_ffn_W1': _L0_ffn_in['W1'], 'L0_ffn_B1': _L0_ffn_in['B1'], 'L0_ffn_W3': _L0_ffn_in['W3'], 'L0_ffn_B3': _L0_ffn_in['B3'], 'L0_ffn_W2': _L0_ffn_in['W2'], 'L0_ffn_B2': _L0_ffn_in['B2'], 'L0_ffn_Ws1': _L0_ffn_in['Ws1'], 'L0_ffn_Bs1': _L0_ffn_in['Bs1'], 'L0_ffn_Ws3': _L0_ffn_in['Ws3'], 'L0_ffn_Bs3': _L0_ffn_in['Bs3'], 'L0_ffn_Ws2': _L0_ffn_in['Ws2'], 'L0_ffn_Bs2': _L0_ffn_in['Bs2']}

def reference(x, txt, L0_tok_W, L0_tok_b, L0_tok_class_token, L0_tok_pos_embed, L0_attn_Wq, L0_attn_Wk, L0_attn_Wv, L0_attn_Wg, L0_attn_Wo, L0_attn_gn_weight, L0_attn_gn_bias, L0_ffn_gate_w, L0_ffn_gate_b, L0_ffn_W1, L0_ffn_B1, L0_ffn_W3, L0_ffn_B3, L0_ffn_W2, L0_ffn_B2, L0_ffn_Ws1, L0_ffn_Bs1, L0_ffn_Ws3, L0_ffn_Bs3, L0_ffn_Ws2, L0_ffn_Bs2):
    import jax
    import jax.numpy as jnp

    def _L0_tok_ref(images, W, b, class_token, pos_embed):
        import jax, jax.numpy as jnp
        import numpy as np
        CHW = (3, 224, 224)
        N_PATCHES = 14
        HIDDEN_D = 192
        BATCH = 128
        PATCH = CHW[1] // N_PATCHES
        INPUT_D = CHW[0] * PATCH * PATCH
        SEQ = N_PATCHES * N_PATCHES + 1

        def get_positional_embeddings(seq, d):
            i = np.arange(seq)[:, None].astype(np.float32)
            j = np.arange(d)[None, :]
            even = j % 2 == 0
            exp = np.where(even, j, j - 1).astype(np.float32) / d
            angle = i / np.power(10000.0, exp)
            out = np.where(even, np.sin(angle), np.cos(angle)).astype(np.float32)
            return jnp.asarray(out)

        def patchify(images, n_patches):
            n, c, h, w = images.shape
            ps = h // n_patches
            x = images.reshape(n, c, n_patches, ps, n_patches, ps)
            x = x.transpose(0, 2, 4, 1, 3, 5)
            return x.reshape(n, n_patches * n_patches, c * ps * ps)
        patches = patchify(images, N_PATCHES)
        tokens = jnp.einsum('bpd,hd->bph', patches, W) + b
        cls = jnp.broadcast_to(class_token[None], (tokens.shape[0], 1, HIDDEN_D))
        tokens = jnp.concatenate([cls, tokens], axis=1)
        return tokens + pos_embed

    def _L0_attn_ref(x, Wq, Wk, Wv, Wg, Wo, gn_weight, gn_bias):
        import jax, jax.numpy as jnp
        import numpy as np
        D_MODEL = 192
        H = 6
        DQK = 128
        DV = 64
        SCALE_BASE = 512.0

        def _xpos(x, sign):
            B, T, Hn, d = x.shape
            half = d // 2
            pos = jnp.arange(T, dtype=jnp.float32)
            inv_freq = 1.0 / 10000.0 ** (jnp.arange(half, dtype=jnp.float32) / half)
            angles = pos[:, None] * inv_freq[None, :]
            zeta = (jnp.arange(half, dtype=jnp.float32) + half) / d
            decay = zeta[None, :] ** (sign * pos[:, None] / SCALE_BASE)
            cos_a = (jnp.cos(angles) * decay)[None, :, None, :]
            sin_a = (jnp.sin(angles) * decay)[None, :, None, :]
            x1, x2 = (x[..., :half], x[..., half:])
            return jnp.concatenate([x1 * cos_a - x2 * sin_a, x1 * sin_a + x2 * cos_a], axis=-1)

        def _decay_mask(T):
            gammas = jnp.array([1.0 - 2.0 ** (-(5 + h)) for h in range(H)], dtype=jnp.float32)
            i = jnp.arange(T, dtype=jnp.float32)
            diff = i[:, None] - i[None, :]
            causal = (diff >= 0).astype(jnp.float32)
            D = gammas[:, None, None] ** jnp.clip(diff, 0.0)[None] * causal[None]
            row = jnp.clip(jnp.sum(D, axis=-1, keepdims=True), 1e-06)
            return D / jnp.sqrt(row)
        B, T, _ = x.shape
        Q = (x @ Wq).reshape(B, T, H, DQK)
        K = (x @ Wk).reshape(B, T, H, DQK)
        V = (x @ Wv).reshape(B, T, H, DV)
        Q = _xpos(Q, 1.0)
        K = _xpos(K, -1.0)
        scores = jnp.einsum('bihd,bjhd->bhij', Q, K) * DQK ** (-0.5)
        scores = scores * _decay_mask(T)[None]
        out = jnp.einsum('bhij,bjhv->bihv', scores, V)
        concat = out.reshape(B, T, H * DV)
        g = concat.transpose(0, 2, 1).reshape(B, H, DV, T)
        mean = jnp.mean(g, axis=(2, 3), keepdims=True)
        var = jnp.var(g, axis=(2, 3), keepdims=True)
        g = (g - mean) / jnp.sqrt(var + 1e-05)
        g = g.reshape(B, H * DV, T) * gn_weight[None, :, None] + gn_bias[None, :, None]
        normed = g.transpose(0, 2, 1)
        gate = jax.nn.silu(x @ Wg)
        return normed * gate @ Wo

    def _L0_ffn_ref(x, gate_w, gate_b, W1, B1, W3, B3, W2, B2, Ws1, Bs1, Ws3, Bs3, Ws2, Bs2):
        import jax, jax.numpy as jnp
        import numpy as np
        B, S, D = (2, 256, 192)
        I = 96
        E = 8
        G = 4
        TOPK_GROUPS = 2
        K = 2
        ROUTE_SCALE = 1.0
        ALPHA, LIMIT = (1.702, 7.0)

        def swiglu(h):
            xg = jnp.minimum(h[..., ::2], LIMIT)
            xl = jnp.clip(h[..., 1::2], -LIMIT, LIMIT)
            return xg * jax.nn.sigmoid(ALPHA * xg) * (xl + 1.0)

        def gate(x, gate_w, gate_b):
            scores = jax.nn.softmax(jnp.einsum('td,ed->te', x, gate_w).astype(jnp.float32), axis=-1)
            original_scores = scores
            s = scores + gate_b
            T = x.shape[0]
            sg = s.reshape(T, G, E // G)
            group_scores = jnp.sum(jax.lax.top_k(sg, 2)[0], axis=-1)
            _, gidx = jax.lax.top_k(group_scores, TOPK_GROUPS)
            keep = jnp.any(jax.nn.one_hot(gidx, G, dtype=jnp.bool_), axis=1)
            sg = jnp.where(keep[:, :, None], sg, -jnp.inf)
            s = sg.reshape(T, E)
            _, idx = jax.lax.top_k(s, K)
            w = jnp.take_along_axis(original_scores, idx, axis=1) * ROUTE_SCALE
            return (w.astype(x.dtype), idx)

        def expert_ffn(x, W1, B1, W3, B3, W2, B2):
            h1 = jnp.einsum('td,edh->teh', x, W1) + B1
            h3 = jnp.einsum('td,edh->teh', x, W3) + B3
            g = swiglu(h1 * h3)
            return jnp.einsum('tei,eid->ted', g, W2) + B2

        def shared_ffn(x, Ws1, Bs1, Ws3, Bs3, Ws2, Bs2):
            h = (x @ Ws1 + Bs1) * (x @ Ws3 + Bs3)
            return swiglu(h) @ Ws2 + Bs2
        inp_shape = x.shape
        xt = x.reshape(-1, D)
        w, idx = gate(xt, gate_w, gate_b)
        combine = jnp.einsum('tk,tke->te', w, jax.nn.one_hot(idx, E, dtype=w.dtype))
        per_expert = expert_ffn(xt, W1, B1, W3, B3, W2, B2)
        routed = jnp.einsum('ted,te->td', per_expert, combine)
        out = routed + shared_ffn(xt, Ws1, Bs1, Ws3, Bs3, Ws2, Bs2)
        return out.reshape(inp_shape)
    h = _L0_tok_ref(x, L0_tok_W, L0_tok_b, L0_tok_class_token, L0_tok_pos_embed)
    h = jnp.concatenate([h, txt], axis=1)
    h = h + _L0_attn_ref(_layernorm(h, axis=-1), L0_attn_Wq, L0_attn_Wk, L0_attn_Wv, L0_attn_Wg, L0_attn_Wo, L0_attn_gn_weight, L0_attn_gn_bias)
    h = h + _L0_ffn_ref(_layernorm(h, axis=-1), L0_ffn_gate_w, L0_ffn_gate_b, L0_ffn_W1, L0_ffn_B1, L0_ffn_W3, L0_ffn_B3, L0_ffn_W2, L0_ffn_B2, L0_ffn_Ws1, L0_ffn_Bs1, L0_ffn_Ws3, L0_ffn_Bs3, L0_ffn_Ws2, L0_ffn_Bs2)
    return h

_drawn_inputs = setup_inputs


def setup_inputs(seed=0):
    import zlib

    import numpy as np

    out = dict(_drawn_inputs(seed))
    spreads = {'L0_attn_gn_weight': (1.0, 0.2), 'L0_attn_gn_bias': (0.0, 0.1)}
    factors = {'L0_ffn_gate_w': 8.0,
     'L0_ffn_gate_b': 8.0,
     'L0_ffn_W1': 8.0,
     'L0_ffn_B1': 8.0,
     'L0_ffn_W3': 8.0,
     'L0_ffn_B3': 8.0,
     'L0_ffn_W2': 8.0,
     'L0_ffn_B2': 64.0,
     'L0_ffn_Ws1': 7.713,
     'L0_ffn_Bs1': 8.0,
     'L0_ffn_Ws3': 7.881,
     'L0_ffn_Bs3': 8.0,
     'L0_ffn_Ws2': 7.619,
     'L0_ffn_Bs2': 25.04}
    for name, (base, spread) in spreads.items():
        noise = np.random.default_rng([zlib.crc32(name.encode()), seed]).standard_normal(out[name].shape)
        drawn = base * np.exp(spread * noise) if base else spread * noise
        out[name] = jnp.asarray(drawn.astype(out[name].dtype))
    for name, factor in factors.items():
        out[name] = (out[name] * factor).astype(out[name].dtype)
    return out
```

```python
from contextlib import ExitStack

import concourse.bass as bass
from concourse import mybir

P = 128
F32 = mybir.dt.float32
F32R = mybir.dt.float32r
ALU = mybir.AluOpType
ACT = mybir.ActivationFunctionType
AX_X = mybir.AxisListType.X

IMAGES = 64
PAIRS = IMAGES // 2
D = 192
DB = D - P
PATCHES = 196
PDIM = 768
PCH = PDIM // P
TXT = 32
T = PATCHES + 1 + TXT
TT = 2 * T
SECOND = T - P
CH = 4
IMG_ROWS1 = P - TXT
H = 6
DQK = 128
DV = 64
HV = H * DV
HVC = HV // P
SC = T + (T - P)
E = 8
G = 4
I = 96
E1 = E + 1
HID = E1 * I
FC = -(-HID // P)
LAST = HID - (FC - 1) * P
LIMIT = 7.0
ALPHA = 1.702
EPS = 1e-5
BIG = 1e30
LO_ROW = 32

W_V = 2 * H * DQK
W_G = W_V + HV
W_F = W_G + HV


def ffn_rows(c):
    return P if c < FC - 1 else LAST


SPLIT = W_F + 4 * P
W_R = SPLIT
W_UP = SPLIT + E


def ffn_col(c, part):
    base = W_F if c == 0 else W_UP + (c - 1) * 4 * P
    return base + part * ffn_rows(c)


WCOLS = W_UP + 4 * (HID - P)
UPC = WCOLS - W_UP
PIECES = [(0, W_UP // 2), (W_UP // 2, W_UP), (W_UP, W_UP + UPC // 2), (W_UP + UPC // 2, WCOLS)]


def row_col(c):
    return (c // 2) * T + (c % 2) * SECOND


def fusion_kernel(nc, a):
    ctx = ExitStack()
    with ctx:
        def sb(name, shape, dt=F32):
            return ctx.enter_context(nc.sbuf_tensor(name, shape, dt))

        def sem(name):
            return ctx.enter_context(nc.semaphore(name))

        wA_hi = sb("wA_hi", [P, WCOLS], F32R)
        wA_lo = sb("wA_lo", [P, WCOLS], F32R)
        wB_hi = sb("wB_hi", [P, WCOLS], F32R)
        wB_lo = sb("wB_lo", [P, UPC], F32R)
        w_tok = sb("w_tok", [P, PCH, D])
        w_o = sb("w_o", [P, HVC, D])
        w_2 = sb("w_2", [P, FC, D])
        b_13 = sb("b_13", [P, FC, 4])
        ident = sb("ident", [P, P])
        heads64 = sb("heads64", [P, P])
        rot_tab = sb("rot_tab", [P, 4, T])
        mask = sb("mask", [P, H, SC])
        sel = sb("sel", [P, FC, P], F32R)
        tie_g = sb("tie_g", [P, G * G])
        tie_e = sb("tie_e", [P, E * E])
        embed = sb("embed", [P, 2, D])
        b_2f = sb("b_2f", [LO_ROW + E1, D])
        b_2hi = sb("b_2hi", [LO_ROW + E1, D], F32R)
        b_2lo = sb("b_2lo", [LO_ROW + E1, D], F32R)
        gate_b = sb("gate_b", [P, E])
        gn_w = sb("gn_w", [P, HVC])
        gn_b = sb("gn_b", [P, HVC])
        neg_half = sb("neg_half", [P, 2 * H])

        patch = sb("patch", [P, PCH * 2, 1 + PATCHES])
        hid = sb("hid", [P, CH, D])
        normed = sb("normed", [P, CH, D])
        hid2 = sb("hid2", [P, CH, D])
        outp = sb("outp", [P, CH, D])
        bn1 = sb("bn1", [P, CH, 6])
        mv1 = sb("mv1", [P, CH, 2])
        rstd1 = sb("rstd1", [P, CH])
        bn2 = sb("bn2", [P, CH, 6])
        mv2 = sb("mv2", [P, CH, 2])
        rstd2 = sb("rstd2", [P, CH])
        x1A_hi = sb("x1A_hi", [P, TT], F32R)
        x1A_lo = sb("x1A_lo", [P, TT], F32R)
        x1B = sb("x1B", [P, TT], F32R)
        x2A_hi = sb("x2A_hi", [P, TT], F32R)
        x2A_lo = sb("x2A_lo", [P, TT], F32R)
        x2B = sb("x2B", [P, TT], F32R)
        x2B_up = sb("x2B_up", [P, TT], F32R)
        swap = sb("swap", [P, 2, TT])
        qk = sb("qk", [P, 2 * H, TT])
        val = sb("val", [P, CH, HV])
        prob = sb("prob", [P, 2, SC])
        rbn = sb("rbn", [P, 2 * HVC, 6])
        rmv = sb("rmv", [P, 2 * HVC, 2])
        gn = sb("gn", [P, 8, 2 * HVC])
        lg = sb("lg", [P, 5, CH * E])
        few = sb("few", [P, 6, CH * G])
        cmp_a = sb("cmp_a", [P, CH * E * E])
        cmp_b = sb("cmp_b", [P, CH * E * E])
        comb = sb("comb", [P, CH, E1])
        combR = sb("combR", [64, TT], F32R)
        gT = sb("gT", [P, FC, TT])
        glu = sb("glu", [P, 2, 2, TT])
        th = sb("th", [P, TT])
        stage = [gT[:, :, :].rearrange("p c t -> p (c t)")[:, i * (UPC // 2):(i + 1) * (UPC // 2)] for i in range(2)]
        sel_in = qk[:, 0:2, :].rearrange("p a t -> p (a t)")[:, 0:FC * P]
        GN_IN, GN_MEAN, GN_SQ, GN_RSTD, GN_SCALE, GN_T, GN_SHIFT = range(7)

        def ret(c):
            return qk[:, 4 * c, :]

        def gate(c):
            return qk[:, 4 * c + 1, :]

        psA = ctx.enter_context(nc.psum_tensor("psA", [P, 4, 512], F32))
        psF = ctx.enter_context(nc.psum_tensor("psF", [P, 4, 512], F32))

        s_const = sem("s_const")
        s_stage = [sem("s_stage0"), sem("s_stage1")]
        s_whi = sem("s_whi")
        s_wlo = sem("s_wlo")
        s_zero = sem("s_zero")
        s_set = sem("s_set")
        s_sel = sem("s_sel")
        s_patch = sem("s_patch")
        s_txt = sem("s_txt")
        s_tok = sem("s_tok")
        s_hid = sem("s_hid")
        s_ln1 = sem("s_ln1")
        s_rstd1 = sem("s_rstd1")
        s_norm1 = sem("s_norm1")
        s_x1T = sem("s_x1T")
        s_x1hi = sem("s_x1hi")
        s_x1lo = sem("s_x1lo")
        s_proj = sem("s_proj")
        s_swap = sem("s_swap")
        s_cos = sem("s_cos")
        s_sin = sem("s_sin")
        s_rot = sem("s_rot")
        s_val = sem("s_val")
        s_gproj = sem("s_gproj")
        s_tanh = sem("s_tanh")
        s_gate = sem("s_gate")
        s_score = sem("s_score")
        s_prob = sem("s_prob")
        s_pv = sem("s_pv")
        s_ret = sem("s_ret")
        s_gn = sem("s_gn")
        s_gnsum = sem("s_gnsum")
        s_gnrstd = sem("s_gnrstd")
        s_scaled = sem("s_scaled")
        s_gated = sem("s_gated")
        s_wo = sem("s_wo")
        s_hid2 = sem("s_hid2")
        s_res = sem("s_res")
        s_ln2 = sem("s_ln2")
        s_rstd2 = sem("s_rstd2")
        s_norm2 = sem("s_norm2")
        s_x2T = sem("s_x2T")
        s_x2hi = sem("s_x2hi")
        s_x2lo = sem("s_x2lo")
        s_logit = sem("s_logit")
        s_top = sem("s_top")
        s_exp = sem("s_exp")
        s_combT = sem("s_combT")
        s_combhi = sem("s_combhi")
        s_comblo = sem("s_comblo")
        s_spread = sem("s_spread")
        s_weight = sem("s_weight")
        s_up = sem("s_up")
        s_up1 = sem("s_up1")
        s_prod = sem("s_prod")
        s_clip = sem("s_clip")
        s_lin = sem("s_lin")
        s_sig = sem("s_sig")
        s_glu = sem("s_glu")
        s_exout = sem("s_exout")
        s_down = sem("s_down")
        s_out = sem("s_out")
        s_store = sem("s_store")

        QKV = 2 * H + CH
        LN_OPS = 2 * CH + 1
        GN_OPS = 16
        TOP_OPS = 20
        CONSTS = 21
        SET_B2 = 1
        SET_ALL = 7

        def nth(per_pair, p, k):
            return per_pair * p + (k + 1)

        def later(p):
            return not isinstance(p, int) or p > 0

        def body(steps, p):
            ahead = not isinstance(p, int) or p < PAIRS - 1

            def do(name, *args):
                if name in steps:
                    steps[name](*args)

            def ex(name, *args):
                if later(p):
                    do(name, p - 1, *args)

            def nxt(name):
                if ahead:
                    do(name, p + 1)

            nxt("load")
            ex("norm2")
            for n in range(QKV):
                do("project", p, n)
                if n == 2:
                    ex("split2")
                if n == 4:
                    ex("route")
                if n == 8:
                    ex("combine")
                if n >= 9:
                    ex("spread", n - 9)
            for h in range(H + 1):
                if h < H:
                    do("score", p, h)
                if h < 4:
                    ex("expert", h)
                if h > 0:
                    do("mix", p, h - 1)
            do("group_norm", p)
            do("attn_gate", p)
            ex("expert", 4)
            do("attn_scale", p)
            do("attn_out", p)
            nxt("embed")
            ex("expert", 5)
            nxt("norm1")
            ex("expert", 6)
            nxt("split1")
            ex("down")

        def program(eng, steps):
            for name in ("load", "embed", "norm1", "split1"):
                if name in steps:
                    steps[name](0)
            body(steps, 0)
            body(steps, 1)
            with eng.Fori(2, PAIRS - 1) as p:
                body(steps, p)
            body(steps, PAIRS - 1)
            for name, args in ([("norm2", ()), ("split2", ()), ("route", ()), ("combine", ())]
                               + [("spread", (c,)) for c in range(FC)]
                               + [("expert", (c,)) for c in range(FC)] + [("down", ())]):
                if name in steps:
                    steps[name](PAIRS - 1, *args)

        block = ctx.enter_context(nc.Block())

        @block.sync
        def _(sp):
            n = [0]

            def const(dst, src):
                n[0] += 1
                sp.dma_start(dst, src).then_inc(s_const, 16)

            for i in range(2 * len(PIECES)):
                lo, hi = PIECES[i // 2]
                st = stage[i % 2][:, 0:hi - lo]
                if i >= 2:
                    sp.wait_ge(s_wlo, i - 1)
                if i % 2 == 0:
                    sp.dma_start(st, a["w_stack"][0:P, lo:hi]).then_inc(s_stage[0], 16)
                else:
                    sp.dma_start(st[0:DB, :], a["w_stack"][P:D, lo:hi]).then_inc(s_stage[1], 16)
                    sp.dma_start(st[DB:P, :], a["w_stack"][P:D, lo:hi]).then_inc(s_stage[1], 16)
                if i == 1:
                    const(w_tok[:, :, :], a["w_tok"])
                    const(ident[:, :], a["c_ident"])
                    const(embed[:, 0, :], a["pos"][0:P, :])
                    const(embed[0:IMG_ROWS1, 1, :], a["pos"][SECOND:SECOND + IMG_ROWS1, :])
                    const(hid[0:1, 0, :], a["cls"])
                    const(hid[1:P, 0, :], a["tok_b"].to_broadcast([P - 1, D]))
                    const(hid[0:IMG_ROWS1, 1, :], a["tok_b"].to_broadcast([IMG_ROWS1, D]))
                    const(w_o[:, :, :], a["w_o"])
                    const(w_2[:, 0:FC - 1, :], a["w_2"][0:(FC - 1) * P, :].rearrange("(c p) d -> p c d", p=P))
                    const(w_2[0:LAST, FC - 1, :], a["w_2"][(FC - 1) * P:HID, :])
                    sp.wait_ge(s_set, SET_B2)
                    const(b_2f[0:E1, :], a["b_2"])
                    const(b_2f[LO_ROW:LO_ROW + E1, :], a["b_2"])
                    const(b_13[:, :, :], a["b_13"])
                    const(rot_tab[:, :, :], a["c_rot"])
                    const(mask[:, :, :], a["c_mask"])
                    const(heads64[:, :], a["c_heads"])
                    const(sel_in, a["c_sel"])
                    const(tie_g[:, :], a["c_tie_g"].to_broadcast([P, G * G]))
                    const(tie_e[:, :], a["c_tie_e"].to_broadcast([P, E * E]))
                    const(gate_b[:, :], a["gate_b"].to_broadcast([P, E]))
                    const(gn[:, GN_IN, :], a["gn_wb"])
            assert n[0] == CONSTS

            def load(p):
                if later(p):
                    sp.wait_ge(s_tok, nth(1, p, -1))
                else:
                    sp.wait_ge(s_zero, 1)
                sp.dma_start(patch[:, :, 1:1 + PATCHES], a["patches"][bass.ds(p, 1), :, :, :].rearrange(
                    "a p c t -> (a p) c t")).then_inc(s_patch, 16)

            def embed_text(p):
                if later(p):
                    sp.wait_ge(s_hid2, nth(2, p, -1))
                for b in range(2):
                    sp.dma_start(hid[IMG_ROWS1:P, 2 * b + 1, :], a["txt"][bass.ds(p * 2 + b, 1), :, :].rearrange(
                        "b t d -> (b t) d")).then_inc(s_txt, 16)

            def down(p):
                for b in range(2):
                    sp.wait_ge(s_out, nth(2, p, b))
                    img = a["out"][bass.ds(p * 2 + b, 1), :, :].rearrange("a t d -> (a t) d")
                    sp.dma_start(img[0:P, :], outp[:, 2 * b, :]).then_inc(s_store, 16)
                    sp.dma_start(img[P:T, :], outp[P - SECOND:P, 2 * b + 1, :]).then_inc(s_store, 16)

            program(sp, {"load": load, "embed": embed_text, "down": down})
            sp.wait_ge(s_store, 64 * PAIRS)

        @block.gpsimd
        def _(pool):
            nc.gpsimd.memset(patch[:, :, 0:1], 0.0).then_inc(s_zero, 1)
            nc.gpsimd.memset(comb[:, :, E:E1], 1.0).then_inc(s_zero, 1)
            nc.gpsimd.memset(neg_half[:, :], -0.5).then_inc(s_zero, 1)
            pool.wait_ge(s_zero, 3)

            def norm1(p):
                pool.wait_ge(s_ln1, nth(LN_OPS, p, LN_OPS - 1))
                nc.gpsimd.tensor_tensor(rstd1[:, :], rstd1[:, :], neg_half[:, 0:CH], ALU.pow).then_inc(s_rstd1, 1)

            def project(p, n):
                if n < 2 * H:
                    pool.wait_ge(s_swap, 2 * nth(2 * H, p, n))
                    s = swap[:, n % 2, :].rearrange("p (b t) -> p b t", b=2)
                    k = 2 * (n % 2) + 1
                    nc.gpsimd.tensor_tensor(s, s, rot_tab[:, k:k + 1, :].to_broadcast([P, 2, T]),
                                            ALU.mult).then_inc(s_sin, 1)

            def group_norm(p):
                pool.wait_ge(s_gn, nth(GN_OPS, p, 12))
                nc.gpsimd.tensor_tensor(gn[:, GN_RSTD, :], gn[:, GN_RSTD, :], neg_half[:, 0:2 * HVC],
                                        ALU.pow).then_inc(s_gnrstd, 1)

            def attn_scale(p):
                for c in range(HVC):
                    pool.wait_ge(s_scaled, nth(2 * HVC, p, 2 * c + 1))
                    pool.wait_ge(s_gate, nth(HVC, p, c))
                    nc.gpsimd.tensor_tensor(ret(c), ret(c), gate(c), ALU.mult).then_inc(s_gated, 1)

            def norm2(p):
                if later(p):
                    pool.wait_ge(s_store, 64 * nth(1, p, -1))
                pool.wait_ge(s_ln2, nth(LN_OPS, p, LN_OPS - 1))
                nc.gpsimd.tensor_tensor(rstd2[:, :], rstd2[:, :], neg_half[:, 0:CH], ALU.pow).then_inc(s_rstd2, 1)
                nc.gpsimd.tensor_copy(outp[:, :, :], hid2[:, :, :]).then_inc(s_res, 1)

            def expert(p, c):
                r = ffn_rows(c)
                pool.wait_ge(s_glu, nth(FC, p, c))
                pool.wait_ge(s_weight, nth(FC, p, c))
                nc.gpsimd.tensor_tensor(gT[0:r, c, :], gT[0:r, c, :], glu[0:r, c % 2, 1, :],
                                        ALU.mult).then_inc(s_exout, 1)

            program(pool, {"norm1": norm1, "project": project, "group_norm": group_norm,
                           "attn_scale": attn_scale, "norm2": norm2, "expert": expert})

        @block.scalar
        def _(act):
            for i in range(2 * len(PIECES)):
                lo, hi = PIECES[i // 2]
                dst = (wA_hi if i % 2 == 0 else wB_hi)[:, lo:hi]
                act.wait_ge(s_stage[i % 2], (16 if i % 2 == 0 else 32) * (i // 2 + 1))
                nc.scalar.activation(dst, stage[i % 2][:, 0:hi - lo], ACT.Copy).then_inc(s_whi, 1)
            act.wait_ge(s_const, 16 * CONSTS)
            act.wait_ge(s_set, SET_B2)
            nc.scalar.activation(b_2hi[:, :], b_2f[:, :], ACT.Copy).then_inc(s_sel, 1)
            nc.scalar.activation(sel[:, :, :].rearrange("p c r -> p (c r)"), sel_in, ACT.Copy).then_inc(s_sel, 1)

            def split1(p):
                act.wait_ge(s_x1T, nth(2, p, 0))
                if later(p):
                    act.wait_ge(s_gproj, nth(HVC, p, -1))
                nc.scalar.activation(x1A_hi[:, :], psA[:, 2, 0:TT], ACT.Copy).then_inc(s_x1hi, 1)
                act.wait_ge(s_x1T, nth(2, p, 1))
                nc.scalar.activation(x1B[0:DB, :], psA[0:DB, 3, 0:TT], ACT.Copy).then_inc(s_x1hi, 1)

            def project(p, n):
                bank = psA[:, n % 4, :]
                act.wait_ge(s_proj, nth(QKV, p, n))
                if n < 2 * H:
                    if n >= 2 or later(p):
                        act.wait_ge(s_rot, nth(2 * H, p, n - 2))
                    nc.scalar.activation(swap[0:64, n % 2, :], bank[64:P, 0:TT], ACT.Copy).then_inc(s_swap, 1)
                    nc.scalar.activation(swap[64:P, n % 2, :], bank[0:64, 0:TT], ACT.Copy).then_inc(s_swap, 1)
                else:
                    if n == 2 * H and later(p):
                        act.wait_ge(s_pv, nth(2 * H, p, -1))
                    nc.scalar.activation(val[:, n - 2 * H, :], bank[:, 0:HV], ACT.Copy).then_inc(s_val, 1)

            def mix(p, h):
                if h % 2 == 1:
                    c = h // 2
                    act.wait_ge(s_pv, nth(2 * H, p, 2 * h + 1))
                    nc.scalar.activation(ret(c), psA[:, 3 - c % 2, 0:TT], ACT.Copy).then_inc(s_ret, 1)

            def attn_gate(p):
                for c in range(HVC):
                    act.wait_ge(s_gproj, nth(HVC, p, c))
                    nc.scalar.activation(gate(c), psA[:, c, 0:TT], ACT.Tanh, scale=0.5).then_inc(s_tanh, 1)

            def split2(p):
                act.wait_ge(s_x2T, nth(2, p, 0))
                if later(p):
                    act.wait_ge(s_up, nth(4 * FC, p, -1))
                nc.scalar.activation(x2A_hi[:, :], psF[:, 0, 0:TT], ACT.Copy).then_inc(s_x2hi, 1)
                act.wait_ge(s_x2T, nth(2, p, 1))
                nc.scalar.activation(x2B[0:DB, :], psF[0:DB, 1, 0:TT], ACT.Copy).then_inc(s_x2hi, 1)
                nc.scalar.activation(x2B_up[DB:P, :], psF[0:DB, 1, 0:TT], ACT.Copy).then_inc(s_x2hi, 1)

            def route(p):
                act.wait_ge(s_top, nth(TOP_OPS, p, 1))
                nc.scalar.activation(lg[:, 1, :], lg[:, 0, :], ACT.Exp).then_inc(s_exp, 1)

            def combine(p):
                act.wait_ge(s_combT, nth(1, p, 0))
                if later(p):
                    act.wait_ge(s_down, nth(2, p, -1))
                nc.scalar.activation(combR[0:E1, :], psF[0:E1, 3, 0:TT], ACT.Copy).then_inc(s_combhi, 1)

            def spread(p, c):
                r = ffn_rows(c)
                act.wait_ge(s_spread, nth(FC, p, c))
                nc.scalar.activation(gT[0:r, c, :], psF[0:r, c % 4, 0:TT], ACT.Copy).then_inc(s_weight, 1)

            def expert(p, c):
                r = ffn_rows(c)
                if c >= 2 or later(p):
                    act.wait_ge(s_exout, nth(FC, p, c - 2))
                for part in range(2):
                    act.wait_ge(s_up, nth(4 * FC, p, 4 * c + part))
                    nc.scalar.activation(glu[0:r, c % 2, part, :], psF[0:r, part, 0:TT], ACT.Identity,
                                         bias=b_13[0:r, c, part:part + 1]).then_inc(s_up1, 1)
                act.wait_ge(s_clip, nth(2 * FC, p, 2 * c))
                if c >= 1 or later(p):
                    act.wait_ge(s_glu, nth(FC, p, c - 1))
                nc.scalar.activation(th[0:r, :], glu[0:r, c % 2, 0, :], ACT.Tanh, scale=ALPHA / 2).then_inc(s_sig, 1)

            program(act, {"split1": split1, "project": project, "mix": mix, "attn_gate": attn_gate,
                          "split2": split2, "route": route, "combine": combine, "spread": spread,
                          "expert": expert})

        @block.vector
        def _(dve):
            nc.vector.memset(b_2f[:, :], 0.0).then_inc(s_set, 1)
            nc.vector.memset(combR[:, :].bitcast(mybir.dt.uint32), 0).then_inc(s_set, 1)
            for i in range(2 * len(PIECES)):
                lo, hi = PIECES[i // 2]
                st = stage[i % 2][:, 0:hi - lo]
                dve.wait_ge(s_whi, i + 1)
                if i % 2 == 0:
                    nc.vector.tensor_tensor(wA_lo[:, lo:hi], st, wA_hi[:, lo:hi].bitcast(F32),
                                            ALU.subtract).then_inc(s_wlo, 1)
                else:
                    r, off = (0, 0) if hi <= W_UP else (DB, W_UP)
                    nc.vector.tensor_tensor(wB_lo[r:r + DB, lo - off:hi - off], st[r:r + DB, :],
                                            wB_hi[r:r + DB, lo:hi].bitcast(F32), ALU.subtract).then_inc(s_wlo, 1)
            dve.wait_ge(s_const, 16 * CONSTS)
            nc.vector.tensor_tensor(embed[:, 0, :], embed[:, 0, :], hid[:, 0, :], ALU.add).then_inc(s_set, 1)
            nc.vector.tensor_tensor(embed[0:IMG_ROWS1, 1, :], embed[0:IMG_ROWS1, 1, :], hid[0:IMG_ROWS1, 1, :],
                                    ALU.add).then_inc(s_set, 1)
            nc.vector.tensor_scalar(gn_w[:, :], gn[:, GN_IN, 0:HVC], 0.5, None, ALU.mult).then_inc(s_set, 1)
            nc.vector.tensor_scalar(gn_b[:, :], gn[:, GN_IN, HVC:2 * HVC], 0.5, None, ALU.mult).then_inc(s_set, 1)
            dve.wait_ge(s_sel, 1)
            nc.vector.tensor_tensor(b_2lo[:, :], b_2f[:, :], b_2hi[:, :].bitcast(F32), ALU.subtract).then_inc(s_set, 1)
            dve.wait_ge(s_set, SET_ALL)

            hid4 = hid[:, :, :].rearrange("p (b k) d -> p b k d", k=2)

            def embed_image(p):
                dve.wait_ge(s_tok, nth(1, p, 0))
                nc.vector.tensor_tensor(hid4[:, :, 0, :], psA[:, 0:2, 0:D],
                                        embed[:, 0:1, :].to_broadcast([P, 2, D]), ALU.add).then_inc(s_hid, 1)
                nc.vector.tensor_tensor(hid4[0:IMG_ROWS1, :, 1, :], psA[0:IMG_ROWS1, 0:2, D:2 * D],
                                        embed[0:IMG_ROWS1, 1:2, :].to_broadcast([IMG_ROWS1, 2, D]),
                                        ALU.add).then_inc(s_hid, 1)

            def layer_norm(p, src, bn, mv, rstd, s_stat, s_rstd, s_done):
                for c in range(CH):
                    nc.vector.bn_stats(bn[:, c, :], src[:, c, :]).then_inc(s_stat, 1)
                dve.wait_ge(s_stat, nth(LN_OPS, p, CH - 1))
                nc.vector.memset(rstd[:, :], EPS)
                for c in range(CH):
                    nc.vector.bn_aggr(mv[:, c, :], bn[:, c, :]).then_inc(s_stat, 1)
                dve.wait_ge(s_stat, nth(LN_OPS, p, 2 * CH - 1))
                nc.vector.tensor_tensor(rstd[:, :], mv[:, :, 1], rstd[:, :], ALU.add).then_inc(s_stat, 1)
                dve.wait_ge(s_rstd, nth(1, p, 0))
                for c in range(CH):
                    nc.vector.tensor_scalar(normed[:, c, :], src[:, c, :], mv[:, c, 0:1], rstd[:, c:c + 1],
                                            ALU.subtract, ALU.mult).then_inc(s_done, 1)

            def norm1(p):
                dve.wait_ge(s_hid, nth(2, p, 1))
                dve.wait_ge(s_txt, 32 * nth(1, p, 0))
                if not isinstance(p, int) or p > 1:
                    dve.wait_ge(s_x2T, nth(2, p - 2, 1))
                layer_norm(p, hid, bn1, mv1, rstd1, s_ln1, s_rstd1, s_norm1)

            def norm2(p):
                if not isinstance(p, int) or p < PAIRS - 1:
                    dve.wait_ge(s_x1T, nth(2, p + 1, 1))
                dve.wait_ge(s_hid2, nth(2, p, 1))
                layer_norm(p, hid2, bn2, mv2, rstd2, s_ln2, s_rstd2, s_norm2)

            def split1(p):
                dve.wait_ge(s_x1hi, nth(2, p, 0))
                nc.vector.tensor_tensor(x1A_lo[:, :], psA[:, 2, 0:TT], x1A_hi[:, :].bitcast(F32),
                                        ALU.subtract).then_inc(s_x1lo, 1)
                dve.wait_ge(s_x1hi, nth(2, p, 1))
                nc.vector.tensor_tensor(x1B[DB:P, :], psA[0:DB, 3, 0:TT], x1B[0:DB, :].bitcast(F32),
                                        ALU.subtract).then_inc(s_x1lo, 1)

            def split2(p):
                dve.wait_ge(s_x2hi, nth(3, p, 0))
                nc.vector.tensor_tensor(x2A_lo[:, :], psF[:, 0, 0:TT], x2A_hi[:, :].bitcast(F32),
                                        ALU.subtract).then_inc(s_x2lo, 1)
                dve.wait_ge(s_x2hi, nth(3, p, 2))
                nc.vector.tensor_tensor(x2B[DB:P, :], psF[0:DB, 1, 0:TT], x2B[0:DB, :].bitcast(F32),
                                        ALU.subtract).then_inc(s_x2lo, 1)

            def add_sin(p, n):
                dve.wait_ge(s_cos, nth(2 * H, p, n))
                dve.wait_ge(s_sin, nth(2 * H, p, n))
                nc.vector.tensor_tensor(qk[:, n, :], qk[:, n, :], swap[:, n % 2, :], ALU.add).then_inc(s_rot, 1)

            def project(p, n):
                if n < 2 * H:
                    dve.wait_ge(s_swap, 2 * nth(2 * H, p, n))
                    if n == 0 and later(p):
                        dve.wait_ge(s_wo, nth(2, p, -1))
                    k = 2 * (n % 2)
                    nc.vector.tensor_tensor(qk[:, n, :].rearrange("p (b t) -> p b t", b=2),
                                            psA[:, n % 4, 0:TT].rearrange("p (b t) -> p b t", b=2),
                                            rot_tab[:, k:k + 1, :].to_broadcast([P, 2, T]),
                                            ALU.mult).then_inc(s_cos, 1)
                if 1 <= n <= 2 * H:
                    add_sin(p, n - 1)

            def score(p, h):
                for b in range(2):
                    n = 2 * h + b
                    dve.wait_ge(s_score, nth(2 * H, p, n))
                    if h > 0 or later(p):
                        dve.wait_ge(s_pv, nth(2 * H, p, n - 2))
                    nc.vector.tensor_tensor(prob[:, b, :], psA[:, b, 0:SC], mask[:, h, :], ALU.mult).then_inc(s_prob, 1)

            def mix(p, h):
                if h % 2 == 1:
                    c = h // 2
                    dve.wait_ge(s_ret, nth(HVC, p, c))
                    for b in range(2):
                        nc.vector.bn_stats(rbn[:, 2 * c + b, :], ret(c)[:, b * T:(b + 1) * T]).then_inc(s_gn, 1)

            def group_norm(p):
                k = [2 * HVC]

                def link(ins):
                    k[0] += 1
                    ins.then_inc(s_gn, 1)
                    dve.wait_ge(s_gn, nth(GN_OPS, p, k[0] - 1))

                dve.wait_ge(s_gn, nth(GN_OPS, p, 2 * HVC - 1))
                nc.vector.memset(gn[:, GN_RSTD, :], EPS)
                for i in range(2 * HVC):
                    last = nc.vector.bn_aggr(rmv[:, i, :], rbn[:, i, :])
                link(last)
                link(nc.vector.tensor_tensor(gn[:, GN_T, :], rmv[:, :, 0], rmv[:, :, 0], ALU.mult))
                link(nc.vector.tensor_tensor(rmv[:, :, 1], rmv[:, :, 1], gn[:, GN_T, :], ALU.add))
                dve.wait_ge(s_gnsum, nth(1, p, 0))
                link(nc.vector.tensor_copy(gn[:, GN_MEAN:GN_SQ + 1, :],
                                           psA[:, 3, 0:4 * HVC].rearrange("p (i s) -> p s i", s=2)))
                link(nc.vector.tensor_tensor(gn[:, GN_T, :], gn[:, GN_MEAN, :], gn[:, GN_MEAN, :], ALU.mult))
                link(nc.vector.tensor_tensor(gn[:, GN_SQ, :], gn[:, GN_SQ, :], gn[:, GN_T, :], ALU.subtract))
                link(nc.vector.tensor_tensor(gn[:, GN_RSTD, :], gn[:, GN_SQ, :], gn[:, GN_RSTD, :], ALU.add))
                assert k[0] == 13

            def attn_gate(p):
                for c in range(HVC):
                    dve.wait_ge(s_tanh, nth(HVC, p, c))
                    nc.vector.scalar_tensor_tensor(gate(c), gate(c), 1.0, psA[:, c, 0:TT],
                                                   ALU.add, ALU.mult).then_inc(s_gate, 1)

            def attn_scale(p):
                def by_chunk(row):
                    return gn[:, row, :].rearrange("p (c b) -> p c b", b=2)

                dve.wait_ge(s_gnrstd, nth(1, p, 0))
                nc.vector.tensor_tensor(by_chunk(GN_SCALE), by_chunk(GN_RSTD), gn_w[:, :, None].to_broadcast([P, HVC, 2]),
                                        ALU.mult).then_inc(s_gn, 1)
                dve.wait_ge(s_gn, nth(GN_OPS, p, 13))
                nc.vector.tensor_tensor(gn[:, GN_T, :], gn[:, GN_MEAN, :], gn[:, GN_SCALE, :], ALU.mult).then_inc(s_gn, 1)
                dve.wait_ge(s_gn, nth(GN_OPS, p, 14))
                nc.vector.tensor_tensor(by_chunk(GN_SHIFT), gn_b[:, :, None].to_broadcast([P, HVC, 2]), by_chunk(GN_T),
                                        ALU.subtract).then_inc(s_gn, 1)
                dve.wait_ge(s_gn, nth(GN_OPS, p, 15))
                for i in range(2 * HVC):
                    x = ret(i // 2)[:, (i % 2) * T:(i % 2 + 1) * T]
                    nc.vector.tensor_scalar(x, x, gn[:, GN_SCALE, i:i + 1], gn[:, GN_SHIFT, i:i + 1],
                                            ALU.mult, ALU.add).then_inc(s_scaled, 1)

            def attn_out(p):
                for b in range(2):
                    dve.wait_ge(s_wo, nth(2, p, b))
                    if b == 0 and later(p):
                        dve.wait_ge(s_res, nth(1, p, -1))
                    nc.vector.tensor_tensor(hid2[:, 2 * b:2 * b + 2, :],
                                            psA[:, b, 0:2 * D].rearrange("p (k d) -> p k d", k=2),
                                            hid[:, 2 * b:2 * b + 2, :], ALU.add).then_inc(s_hid2, 1)

            def route(p):
                k = [0]

                def link(ins):
                    k[0] += 1
                    ins.then_inc(s_top, 1)
                    dve.wait_ge(s_top, nth(TOP_OPS, p, k[0] - 1))

                def by_row(x, n):
                    return x.rearrange("p (c n) -> p c n", n=n)

                def rank(values, n, ties, out):
                    v = by_row(values, n)
                    other = v[:, :, None, :].to_broadcast([P, CH, n, n])
                    own = v[:, :, :, None].to_broadcast([P, CH, n, n])
                    a_ = cmp_a[:, 0:CH * n * n]
                    b_ = cmp_b[:, 0:CH * n * n]
                    a4 = a_.rearrange("p (c i j) -> p c i j", i=n, j=n)
                    b4 = b_.rearrange("p (c i j) -> p c i j", i=n, j=n)
                    link(nc.vector.tensor_tensor(a4, other, own, ALU.is_gt))
                    link(nc.vector.tensor_tensor(b4, other, own, ALU.is_equal))
                    link(nc.vector.tensor_tensor(by_row(b_, n * n), by_row(b_, n * n),
                                                 ties[:, None, :].to_broadcast([P, CH, n * n]), ALU.mult))
                    link(nc.vector.tensor_tensor(a_, a_, b_, ALU.add))
                    link(nc.vector.reduce_sum(out, a_.rearrange("p (i j) -> p i j", j=n), axis=AX_X))

                logits = psF[:, 2, 0:CH * E]
                dve.wait_ge(s_logit, nth(1, p, 0))
                link(nc.vector.reduce_max(few[:, 0, 0:CH], by_row(logits, E), axis=AX_X))
                link(nc.vector.tensor_tensor(by_row(lg[:, 0, :], E), by_row(logits, E),
                                             few[:, 0, 0:CH, None].to_broadcast([P, CH, E]), ALU.subtract))
                dve.wait_ge(s_exp, nth(1, p, 0))
                link(nc.vector.reduce_sum(few[:, 1, 0:CH], by_row(lg[:, 1, :], E), axis=AX_X))
                link(nc.vector.reciprocal(few[:, 2, 0:CH], few[:, 1, 0:CH]))
                link(nc.vector.tensor_tensor(by_row(lg[:, 2, :], E), by_row(lg[:, 1, :], E),
                                             few[:, 2, 0:CH, None].to_broadcast([P, CH, E]), ALU.mult))
                link(nc.vector.tensor_tensor(by_row(lg[:, 3, :], E), by_row(lg[:, 2, :], E),
                                             gate_b[:, None, :].to_broadcast([P, CH, E]), ALU.add))
                pairs = lg[:, 3, :].rearrange("p (m two) -> p m two", two=2)
                link(nc.vector.tensor_tensor(few[:, 3, :], pairs[:, :, 0], pairs[:, :, 1], ALU.add))
                rank(few[:, 3, :], G, tie_g[:, :], few[:, 4, :])
                link(nc.vector.tensor_scalar(few[:, 5, :], few[:, 4, :], 2.0, -BIG, ALU.is_ge, ALU.mult))
                link(nc.vector.tensor_tensor(lg[:, 4, :].rearrange("p (m two) -> p m two", two=2), pairs,
                                             few[:, 5, :, None].to_broadcast([P, CH * G, 2]), ALU.add))
                rank(lg[:, 4, :], E, tie_e[:, :], lg[:, 0, :])
                if later(p):
                    dve.wait_ge(s_combT, nth(1, p, -1))
                nc.vector.scalar_tensor_tensor(comb[:, :, 0:E], by_row(lg[:, 0, :], E), 2.0, by_row(lg[:, 2, :], E),
                                               ALU.is_lt, ALU.mult).then_inc(s_top, 1)
                assert k[0] + 1 == TOP_OPS, k[0]

            def combine(p):
                dve.wait_ge(s_combhi, nth(1, p, 0))
                nc.vector.tensor_tensor(combR[LO_ROW:LO_ROW + E1, :], psF[0:E1, 3, 0:TT],
                                        combR[0:E1, :].bitcast(F32), ALU.subtract).then_inc(s_comblo, 1)

            def expert_glu(p, c):
                r = ffn_rows(c)
                odd = glu[0:r, c % 2, 1, :]
                dve.wait_ge(s_sig, nth(FC, p, c))
                dve.wait_ge(s_lin, nth(FC, p, c))
                nc.vector.scalar_tensor_tensor(odd, th[0:r, :], 1.0, odd, ALU.add, ALU.mult).then_inc(s_glu, 1)

            def expert(p, c):
                r = ffn_rows(c)
                even, odd = glu[0:r, c % 2, 0, :], glu[0:r, c % 2, 1, :]
                for part in range(2):
                    x = glu[0:r, c % 2, part, :]
                    dve.wait_ge(s_up, nth(4 * FC, p, 4 * c + 2 + part))
                    dve.wait_ge(s_up1, nth(2 * FC, p, 2 * c + part))
                    nc.vector.scalar_tensor_tensor(x, psF[0:r, 2 + part, 0:TT], b_13[0:r, c, 2 + part:3 + part], x,
                                                   ALU.add, ALU.mult).then_inc(s_prod, 1)
                dve.wait_ge(s_prod, nth(2 * FC, p, 2 * c))
                nc.vector.tensor_scalar(even, even, LIMIT, None, ALU.min).then_inc(s_clip, 1)
                dve.wait_ge(s_prod, nth(2 * FC, p, 2 * c + 1))
                nc.vector.tensor_scalar(odd, odd, LIMIT, -LIMIT, ALU.min, ALU.max).then_inc(s_clip, 1)
                dve.wait_ge(s_clip, nth(2 * FC, p, 2 * c + 1))
                nc.vector.scalar_tensor_tensor(odd, odd, 1.0, even, ALU.add, ALU.mult).then_inc(s_lin, 1)
                expert_glu(p, c)

            def down(p):
                for b in range(2):
                    dve.wait_ge(s_down, nth(2, p, b))
                    if b == 0:
                        dve.wait_ge(s_res, nth(1, p, 0))
                    rows = outp[:, 2 * b:2 * b + 2, :]
                    nc.vector.tensor_tensor(rows, psF[:, b, 0:2 * D].rearrange("p (k d) -> p k d", k=2), rows,
                                            ALU.add).then_inc(s_out, 1)

            program(dve, {"embed": embed_image, "norm1": norm1, "split1": split1, "project": project,
                          "score": score, "mix": mix, "group_norm": group_norm, "attn_gate": attn_gate,
                          "attn_scale": attn_scale, "attn_out": attn_out, "norm2": norm2, "split2": split2,
                          "route": route, "combine": combine, "expert": expert, "down": down})

        @block.tensor
        def _(pe):
            pe.wait_ge(s_const, 16 * CONSTS)
            pe.wait_ge(s_zero, 3)
            pe.wait_ge(s_wlo, 2 * len(PIECES))
            pe.wait_ge(s_set, SET_ALL)
            pe.wait_ge(s_sel, 2)

            def low_b(w0, w1):
                if w0 < W_UP:
                    return wB_lo[0:DB, w0:w1], slice(0, DB)
                return wB_lo[DB:P, w0 - W_UP:w1 - W_UP], slice(DB, P)

            def weights_by_tokens(out, w0, m, xA_hi, xA_lo, xB, xB_up):
                w = slice(w0, w0 + m)
                wlo, rows = low_b(w0, w0 + m)
                xlo = (xB if rows.start == 0 else xB_up)[rows, :]
                nc.tensor.matmul(out, wA_hi[:, w], xA_hi[:, :], start=True, stop=False)
                nc.tensor.matmul(out, wA_lo[:, w], xA_hi[:, :], start=False, stop=False)
                nc.tensor.matmul(out, wA_hi[:, w], xA_lo[:, :], start=False, stop=False)
                nc.tensor.matmul(out, wB_hi[:, w], xB[:, :], start=False, stop=False)
                return nc.tensor.matmul(out, wlo, xlo, start=False, stop=True)

            def tokens_by_weights(out, c, w0, m, xA_hi, xA_lo, xB):
                w = slice(w0, w0 + m)
                t = slice(row_col(c), row_col(c) + P)
                nc.tensor.matmul(out, xA_hi[:, t], wA_hi[:, w], start=True, stop=False)
                nc.tensor.matmul(out, xA_hi[:, t], wA_lo[:, w], start=False, stop=False)
                nc.tensor.matmul(out, xA_lo[:, t], wA_hi[:, w], start=False, stop=False)
                nc.tensor.matmul(out, xB[:, t], wB_hi[:, w], start=False, stop=False)
                return nc.tensor.matmul(out, xB[0:DB, t], wB_lo[0:DB, w], start=False, stop=True)

            def embed_(p):
                pe.wait_ge(s_patch, 16 * nth(1, p, 0))
                if later(p):
                    pe.wait_ge(s_hid2, nth(2, p, -1))
                for b in range(2):
                    for k in range(2):
                        m, t0 = (P, 0) if k == 0 else (IMG_ROWS1, SECOND)
                        for c in range(PCH):
                            last = nc.tensor.matmul(psA[0:m, b, k * D:(k + 1) * D], patch[:, 2 * c + b, t0:t0 + m],
                                                    w_tok[:, c, :], start=(c == 0), stop=(c == PCH - 1))
                last.then_inc(s_tok, 1)

            def to_columns(bankA, bankB, s_done):
                for c in range(CH):
                    t = slice(row_col(c), row_col(c) + P)
                    last = nc.tensor.transpose(bankA[:, t], normed[:, c, 0:P], ident[:, :])
                last.then_inc(s_done, 1)
                for c in range(CH):
                    t = slice(row_col(c), row_col(c) + P)
                    last = nc.tensor.transpose(bankB[0:DB, t], normed[:, c, P:D], ident[:, :])
                last.then_inc(s_done, 1)

            def split1(p):
                pe.wait_ge(s_norm1, nth(CH, p, CH - 1))
                if later(p):
                    pe.wait_ge(s_gate, nth(HVC, p, -1))
                    pe.wait_ge(s_gn, nth(GN_OPS, p - 1, 9))
                to_columns(psA[:, 2, :], psA[:, 3, :], s_x1T)

            def project(p, n):
                bank = psA[:, n % 4, :]
                if n == 0:
                    pe.wait_ge(s_x1lo, nth(2, p, 1))
                    pe.wait_ge(s_hid, nth(2, p, 1))
                elif n >= 4:
                    pe.wait_ge(s_swap, 2 * nth(2 * H, p, n - 4))
                    pe.wait_ge(s_cos, nth(2 * H, p, n - 4))
                if n < 2 * H:
                    head, k = n // 2, n % 2
                    w0 = k * H * DQK + head * DQK
                    last = weights_by_tokens(bank[:, 0:TT], w0, P, x1A_hi, x1A_lo, x1B, None)
                else:
                    last = tokens_by_weights(bank[:, 0:HV], n - 2 * H, W_V, HV, x1A_hi, x1A_lo, x1B)
                last.then_inc(s_proj, 1)

            def score(p, h):
                pe.wait_ge(s_rot, nth(2 * H, p, 2 * h + 1))
                for b in range(2):
                    if h == 0:
                        pe.wait_ge(s_val, nth(CH, p, b))
                    else:
                        pe.wait_ge(s_prob, nth(2 * H, p, 2 * h - 2 + b))
                    t0 = b * T
                    q, k = qk[:, 2 * h, :], qk[:, 2 * h + 1, :]
                    nc.tensor.matmul(psA[:, b, 0:T], k[:, t0:t0 + P], q[:, t0:t0 + T], start=True, stop=True)
                    nc.tensor.matmul(psA[:, b, T:SC], k[:, t0 + SECOND:t0 + T], q[:, t0 + P:t0 + T],
                                     start=True, stop=True).then_inc(s_score, 1)

            def mix(p, h):
                c = h // 2
                bank = psA[:, 3 - c % 2, :]
                rows = slice(64 * (h % 2), 64 * (h % 2) + 64)
                v = slice(h * DV, (h + 1) * DV)
                if h % 2 == 0:
                    if c < 2:
                        pe.wait_ge(s_val, nth(CH, p, CH - 1))
                    else:
                        pe.wait_ge(s_ret, nth(HVC, p, c - 2))
                for b in range(2):
                    pe.wait_ge(s_prob, nth(2 * H, p, 2 * h + b))
                    nc.tensor.matmul(bank[rows, b * T:(b + 1) * T], val[:, 2 * b, v], prob[:, b, 0:T],
                                     start=True, stop=False)
                    nc.tensor.matmul(bank[rows, b * T + P:(b + 1) * T], val[:, 2 * b + 1, v], prob[:, b, T:SC],
                                     start=False, stop=True).then_inc(s_pv, 1)

            def group_norm(p):
                pe.wait_ge(s_ret, nth(HVC, p, HVC - 1))
                pe.wait_ge(s_gn, nth(GN_OPS, p, 8))
                nc.tensor.matmul(psA[:, 3, 0:4 * HVC], heads64[:, :], rmv[:, :, :].rearrange("p i s -> p (i s)"),
                                 start=True, stop=True).then_inc(s_gnsum, 1)

            def attn_gate(p):
                for c in range(HVC):
                    if c < 2:
                        pe.wait_ge(s_prob, nth(2 * H, p, 2 * H - 2 + c))
                    weights_by_tokens(psA[:, c, 0:TT], W_G + c * P, P, x1A_hi, x1A_lo, x1B, None).then_inc(s_gproj, 1)

            def attn_out(p):
                pe.wait_ge(s_gated, nth(HVC, p, HVC - 1))
                for b in range(2):
                    for k in range(2):
                        t0 = row_col(2 * b + k)
                        for c in range(HVC):
                            last = nc.tensor.matmul(psA[:, b, k * D:(k + 1) * D], ret(c)[:, t0:t0 + P], w_o[:, c, :],
                                                    start=(c == 0), stop=(c == HVC - 1))
                    last.then_inc(s_wo, 1)

            def split2(p):
                pe.wait_ge(s_norm2, nth(CH, p, CH - 1))
                if later(p):
                    pe.wait_ge(s_out, nth(2, p, -1))
                to_columns(psF[:, 0, :], psF[:, 1, :], s_x2T)

            def route(p):
                pe.wait_ge(s_x2lo, nth(2, p, 1))
                for c in range(CH):
                    last = tokens_by_weights(psF[:, 2, c * E:(c + 1) * E], c, W_R, E, x2A_hi, x2A_lo, x2B)
                last.then_inc(s_logit, 1)

            def combine(p):
                pe.wait_ge(s_top, nth(TOP_OPS, p, TOP_OPS - 1))
                for c in range(CH):
                    last = nc.tensor.transpose(psF[0:E1, 3, row_col(c):row_col(c) + P], comb[:, c, :], ident[:, :])
                last.then_inc(s_combT, 1)

            def spread(p, c):
                r = ffn_rows(c)
                if c == 0:
                    pe.wait_ge(s_comblo, nth(1, p, 0))
                    pe.wait_ge(s_x2hi, nth(3, p, 2))
                elif c >= 4:
                    pe.wait_ge(s_weight, nth(FC, p, c - 4))
                nc.tensor.matmul(psF[0:r, c % 4, 0:TT], sel[0:LO_ROW + E1, c, 0:r], combR[0:LO_ROW + E1, :],
                                 start=True, stop=True).then_inc(s_spread, 1)

            def expert(p, c):
                r = ffn_rows(c)
                for part in range(4):
                    if c == 0:
                        pe.wait_ge(s_weight, nth(FC, p, FC - 1)) if part == 0 else None
                    elif part < 2:
                        pe.wait_ge(s_up1, nth(2 * FC, p, 2 * (c - 1) + part))
                    else:
                        pe.wait_ge(s_prod, nth(2 * FC, p, 2 * (c - 1) + part - 2))
                    weights_by_tokens(psF[0:r, part, 0:TT], ffn_col(c, part), r, x2A_hi, x2A_lo, x2B,
                                      x2B_up).then_inc(s_up, 1)

            def down(p):
                for b in range(2):
                    pe.wait_ge(s_up1, nth(2 * FC, p, 2 * FC - 2 + b))
                    for k in range(2):
                        t0 = row_col(2 * b + k)
                        out = psF[:, b, k * D:(k + 1) * D]
                        cw = combR[0:LO_ROW + E1, t0:t0 + P]
                        nc.tensor.matmul(out, cw, b_2hi[:, :], start=True, stop=False)
                        nc.tensor.matmul(out, cw, b_2lo[:, :], start=False, stop=False)
                        for c in range(FC):
                            r = ffn_rows(c)
                            if b == 0 and k == 0:
                                pe.wait_ge(s_exout, nth(FC, p, c))
                            last = nc.tensor.matmul(out, gT[0:r, c, t0:t0 + P], w_2[0:r, c, :],
                                                    start=False, stop=(c == FC - 1))
                    last.then_inc(s_down, 1)

            program(pe, {"embed": embed_, "split1": split1, "project": project, "score": score, "mix": mix,
                         "group_norm": group_norm, "attn_gate": attn_gate, "attn_out": attn_out,
                         "split2": split2, "route": route, "combine": combine, "spread": spread,
                         "expert": expert, "down": down})


def _tables():
    import numpy as np
    half = DQK // 2
    pos = np.arange(T, dtype=np.float32)
    inv_freq = np.float32(1.0) / np.float32(10000.0) ** (np.arange(half, dtype=np.float32) / np.float32(half))
    angles = (inv_freq[:, None] * pos[None, :]).astype(np.float32).astype(np.float64)
    zeta = (np.arange(half, dtype=np.float64) + half) / DQK
    rot = np.zeros((P, 4, T), np.float32)
    for i, sign in enumerate((1.0, -1.0)):
        decay = zeta[:, None] ** (sign * pos[None, :].astype(np.float64) / 512.0)
        cos, sin = np.cos(angles) * decay, np.sin(angles) * decay
        rot[:, 2 * i] = np.concatenate([cos, cos])
        rot[:, 2 * i + 1] = np.concatenate([-sin, sin])
    t = np.arange(T)
    diff = t[None, :] - t[:, None]
    mask = np.zeros((P, H, SC), np.float32)
    for h in range(H):
        gamma = 1.0 - 2.0 ** (-(5 + h))
        d = np.where(diff >= 0, gamma ** np.maximum(diff, 0), 0.0)
        d = d / np.sqrt(np.maximum(d.sum(axis=0, keepdims=True), 1e-6)) * DQK ** -0.5
        mask[:, h, 0:T] = d[0:P]
        mask[P - SECOND:, h, T:] = d[P:, P:]
    heads = np.kron(np.eye(2), np.full((64, 64), 1.0 / 64)).astype(np.float32)
    sel = np.zeros((P, FC * P), np.float32)
    for r in range(HID):
        sel[r // I, r] = sel[LO_ROW + r // I, r] = 0.5
    return {
        "c_ident": np.eye(P, dtype=np.float32), "c_rot": rot, "c_mask": mask, "c_heads": heads, "c_sel": sel,
        "c_tie_g": np.tril(np.ones((G, G), np.float32), -1).reshape(1, -1),
        "c_tie_e": np.tril(np.ones((E, E), np.float32), -1).reshape(1, -1),
    }


def kernel(x, txt, L0_tok_W, L0_tok_b, L0_tok_class_token, L0_tok_pos_embed, L0_attn_Wq, L0_attn_Wk, L0_attn_Wv,
           L0_attn_Wg, L0_attn_Wo, L0_attn_gn_weight, L0_attn_gn_bias, L0_ffn_gate_w, L0_ffn_gate_b, L0_ffn_W1,
           L0_ffn_B1, L0_ffn_W3, L0_ffn_B3, L0_ffn_W2, L0_ffn_B2, L0_ffn_Ws1, L0_ffn_Bs1, L0_ffn_Ws3, L0_ffn_Bs3,
           L0_ffn_Ws2, L0_ffn_Bs2):
    import numpy as np
    import concourse.bacc as bacc
    from concourse import mybir as _mybir
    from concourse.bass_utils import run_bass_kernel_spmd

    def f(v):
        return np.asarray(v)

    def experts(w, ws):
        return np.concatenate([f(w), f(ws)[None]]).transpose(1, 0, 2).reshape(D, HID, 2)

    up1, up3 = experts(L0_ffn_W1, L0_ffn_Ws1), experts(L0_ffn_W3, L0_ffn_Ws3)
    bias1 = np.concatenate([f(L0_ffn_B1), f(L0_ffn_Bs1)[None]]).reshape(HID, 2)
    bias3 = np.concatenate([f(L0_ffn_B3), f(L0_ffn_Bs3)[None]]).reshape(HID, 2)
    cols = [f(L0_attn_Wq), f(L0_attn_Wk), f(L0_attn_Wv), f(L0_attn_Wg)]
    b_13 = np.zeros((P, FC, 4), np.float32)
    for c in range(FC):
        r = slice(c * P, c * P + ffn_rows(c))
        cols += [up1[:, r, 0], up1[:, r, 1], up3[:, r, 0], up3[:, r, 1]]
        if c == 0:
            cols.append(f(L0_ffn_gate_w).T)
        b_13[0:ffn_rows(c), c, 0:2] = bias1[r]
        b_13[0:ffn_rows(c), c, 2:4] = bias3[r]
    n = 14
    ps = 16
    patches = f(x).reshape(PAIRS, 2, 3, n, ps, n, ps).transpose(0, 2, 4, 6, 1, 3, 5)
    patches = patches.reshape(PAIRS, PCH, P, 2, PATCHES).transpose(0, 2, 1, 3, 4).reshape(PAIRS, P, PCH * 2, PATCHES)
    ins = {
        "patches": patches,
        "txt": f(txt),
        "w_stack": np.concatenate(cols, axis=1),
        "w_tok": f(L0_tok_W).T.reshape(PCH, P, D).transpose(1, 0, 2),
        "tok_b": f(L0_tok_b).reshape(1, D),
        "cls": f(L0_tok_class_token),
        "pos": f(L0_tok_pos_embed),
        "w_o": f(L0_attn_Wo).reshape(HVC, P, D).transpose(1, 0, 2),
        "gn_wb": np.concatenate([f(L0_attn_gn_weight).reshape(HVC, P).T, f(L0_attn_gn_bias).reshape(HVC, P).T], axis=1),
        "gate_b": f(L0_ffn_gate_b).reshape(1, E),
        "w_2": np.concatenate([f(L0_ffn_W2).reshape(E * I, D), f(L0_ffn_Ws2)]),
        "b_2": np.concatenate([f(L0_ffn_B2), f(L0_ffn_Bs2).reshape(1, D)]),
        "b_13": b_13,
        **_tables(),
    }
    ins = {k: np.ascontiguousarray(v) for k, v in ins.items()}
    nc = bacc.Bacc("TRN2", target_bir_lowering=False, num_devices=1)
    aps = {k: nc.dram_tensor("in_" + k, v.shape, _mybir.dt.from_np(v.dtype), kind="ExternalInput").ap() for k, v in ins.items()}
    aps["out"] = nc.dram_tensor("out", (IMAGES, T, D), F32, kind="ExternalOutput").ap()
    fusion_kernel(nc, aps)
    r = run_bass_kernel_spmd(nc, [{"in_" + k: v for k, v in ins.items()}], core_ids=[0])
    return r.results[0]["out"]
```

```python
from contextlib import ExitStack

import concourse.bass as bass
from concourse import mybir

P = 128
F32 = mybir.dt.float32
F32R = mybir.dt.float32r
ALU = mybir.AluOpType
ACT = mybir.ActivationFunctionType
AX_X = mybir.AxisListType.X

IMAGES = 64
PAIRS = IMAGES // 2
D = 192
DB = D - P
PATCHES = 196
PDIM = 768
PCH = PDIM // P
TXT = 32
T = PATCHES + 1 + TXT
TT = 2 * T
SECOND = T - P
CH = 4
IMG_ROWS1 = P - TXT
H = 6
DQK = 128
DV = 64
HV = H * DV
HVC = HV // P
SC = T + (T - P)
E = 8
G = 4
I = 96
E1 = E + 1
HID = E1 * I
FC = -(-HID // P)
LAST = HID - (FC - 1) * P
LIMIT = 7.0
ALPHA = 1.702
EPS = 1e-5
BIG = 1e30
LO_ROW = 32

W_V = 2 * H * DQK
W_G = W_V + HV
W_F = W_G + HV


def ffn_rows(c):
    return P if c < FC - 1 else LAST


W_R = W_F
W_UP = W_R + E
WCOLS = W_UP + 4 * HID
FFC = WCOLS - W_F
PIECES = ([(i * W_F // 2, (i + 1) * W_F // 2) for i in range(2)]
          + [(W_F + i * 1156, min(W_F + (i + 1) * 1156, WCOLS)) for i in range(3)])
PIECE = max(b - a for a, b in PIECES)


def up_col(c, part):
    return W_UP + c * 4 * P + part * ffn_rows(c)


ROUND = ([("logits",)] + [("up", 0, part) for part in range(4)] + [("route",)] + [("up", 1, part) for part in range(4)]
         + [("combine",), ("spread", 0), ("spread", 1)]
         + [x for c in range(2, FC) for x in [("up", c, part) for part in range(4)] + [("spread", c)]])


def bank_of(*item):
    return ROUND.index(item) % 4


def row_col(c):
    return (c // 2) * T + (c % 2) * SECOND


def fusion_kernel(nc, a):
    ctx = ExitStack()
    with ctx:
        def sb(name, shape, dt=F32):
            return ctx.enter_context(nc.sbuf_tensor(name, shape, dt))

        def sem(name):
            return ctx.enter_context(nc.semaphore(name))

        wA_hi = sb("wA_hi", [P, WCOLS], F32R)
        wA_lo = sb("wA_lo", [P, WCOLS], F32R)
        wB_hi = sb("wB_hi", [P, WCOLS], F32R)
        wB_lo = sb("wB_lo", [P, FFC], F32R)
        w_tok = sb("w_tok", [P, PCH, D])
        w_o = sb("w_o", [P, HVC, D])
        w_2 = sb("w_2", [P, FC, D])
        b_13 = sb("b_13", [P, FC, 4])
        ident = sb("ident", [P, P])
        heads64 = sb("heads64", [P, P])
        rot_tab = sb("rot_tab", [P, 4, T])
        mask = sb("mask", [P, H, SC])
        sel = sb("sel", [P, FC, P], F32R)
        tie_g = sb("tie_g", [P, G * G])
        tie_e = sb("tie_e", [P, E * E])
        embed = sb("embed", [P, 2, D])
        b_2hi = sb("b_2hi", [LO_ROW + E1, D], F32R)
        b_2lo = sb("b_2lo", [LO_ROW + E1, D], F32R)
        gate_b = sb("gate_b", [P, E])
        gn_w = sb("gn_w", [P, HVC])
        gn_b = sb("gn_b", [P, HVC])
        neg_half = sb("neg_half", [P, 2 * H])
        zeros = sb("zeros", [P, 1, 1])

        patch = sb("patch", [P, PCH * 2, 1 + PATCHES])
        hid = sb("hid", [P, CH, D])
        normed = sb("normed", [P, CH, D])
        hid2 = sb("hid2", [P, CH, D])
        outp = sb("outp", [P, CH, D])
        bn1 = sb("bn1", [P, CH, 6])
        mv1 = sb("mv1", [P, CH, 2])
        rstd1 = sb("rstd1", [P, CH])
        bn2 = sb("bn2", [P, CH, 6])
        mv2 = sb("mv2", [P, CH, 2])
        rstd2 = sb("rstd2", [P, CH])
        x1A_hi = sb("x1A_hi", [P, TT], F32R)
        x1A_lo = sb("x1A_lo", [P, TT], F32R)
        x1B = sb("x1B", [P, TT], F32R)
        x1B_z = sb("x1B_z", [P, TT], F32R)
        x2A_hi = sb("x2A_hi", [P, TT], F32R)
        x2A_lo = sb("x2A_lo", [P, TT], F32R)
        x2B = sb("x2B", [P, TT], F32R)
        x2B_z = sb("x2B_z", [P, TT], F32R)
        swap = sb("swap", [P, 2, TT])
        qk = sb("qk", [P, 2 * H, TT])
        val = sb("val", [P, CH, HV])
        prob = sb("prob", [P, 2, SC])
        rbn = sb("rbn", [P, 2 * HVC, 6])
        rmv = sb("rmv", [P, 2 * HVC, 2])
        gn = sb("gn", [P, 8, 2 * HVC])
        lg = sb("lg", [P, 5, CH * E])
        few = sb("few", [P, 6, CH * G])
        flat = prob[:, :, :].rearrange("p b s -> p (b s)")
        cmp_a, cmp_b = flat[:, 0:CH * E * E], flat[:, CH * E * E:2 * CH * E * E]
        comb = sb("comb", [P, CH, E1])
        combR = sb("combR", [64, TT], F32R)
        gT = sb("gT", [P, FC, TT])
        glu = sb("glu", [P, 2, 2, TT])
        th = sb("th", [P, TT])
        stage = [gT[:, :, :].rearrange("p c t -> p (c t)")[:, i * PIECE:(i + 1) * PIECE] for i in range(2)]
        b_2f = prob[0:LO_ROW + E1, 0, 0:D]
        sel_in = qk[:, 0:2, :].rearrange("p a t -> p (a t)")[:, 0:FC * P]
        GN_IN, GN_MEAN, GN_SQ, GN_RSTD, GN_SCALE, GN_T, GN_SHIFT = range(7)

        def ret(c):
            return qk[:, 4 * c, :]

        def gate(c):
            return qk[:, 4 * c + 1, :]

        psA = ctx.enter_context(nc.psum_tensor("psA", [P, 4, 512], F32))
        psF = ctx.enter_context(nc.psum_tensor("psF", [P, 4, 512], F32))

        s_const = sem("s_const")
        s_stage = [sem("s_stage0"), sem("s_stage1")]
        s_whi = sem("s_whi")
        s_wlo = sem("s_wlo")
        s_zero = sem("s_zero")
        s_set = sem("s_set")
        s_sel = sem("s_sel")
        s_patch = sem("s_patch")
        s_txt = sem("s_txt")
        s_tok = sem("s_tok")
        s_hid = sem("s_hid")
        s_ln1 = sem("s_ln1")
        s_rstd1 = sem("s_rstd1")
        s_norm1 = sem("s_norm1")
        s_x1T = sem("s_x1T")
        s_x1hi = sem("s_x1hi")
        s_x1lo = sem("s_x1lo")
        s_proj = sem("s_proj")
        s_swap = sem("s_swap")
        s_cos = sem("s_cos")
        s_sin = sem("s_sin")
        s_rot = sem("s_rot")
        s_val = sem("s_val")
        s_gproj = sem("s_gproj")
        s_tanh = sem("s_tanh")
        s_gate = sem("s_gate")
        s_score = sem("s_score")
        s_prob = sem("s_prob")
        s_pv = sem("s_pv")
        s_ret = sem("s_ret")
        s_gn = sem("s_gn")
        s_gnsum = sem("s_gnsum")
        s_gnrstd = sem("s_gnrstd")
        s_scaled = sem("s_scaled")
        s_gated = sem("s_gated")
        s_wo = sem("s_wo")
        s_hid2 = sem("s_hid2")
        s_res = sem("s_res")
        s_ln2 = sem("s_ln2")
        s_rstd2 = sem("s_rstd2")
        s_norm2 = sem("s_norm2")
        s_x2T = sem("s_x2T")
        s_x2hi = sem("s_x2hi")
        s_x2lo = sem("s_x2lo")
        s_logit = sem("s_logit")
        s_lgcol = sem("s_lgcol")
        s_lgrow = sem("s_lgrow")
        s_top = sem("s_top")
        s_exp = sem("s_exp")
        s_combT = sem("s_combT")
        s_combhi = sem("s_combhi")
        s_comblo = sem("s_comblo")
        s_spread = sem("s_spread")
        s_weight = sem("s_weight")
        s_up = sem("s_up")
        s_up1 = sem("s_up1")
        s_prod = sem("s_prod")
        s_clip = sem("s_clip")
        s_lin = sem("s_lin")
        s_sig = sem("s_sig")
        s_glu = sem("s_glu")
        s_exout = sem("s_exout")
        s_down = sem("s_down")
        s_out = sem("s_out")
        s_store = sem("s_store")

        QKV = 2 * H + CH
        LN_OPS = 2 * CH + 1
        GN_OPS = 16
        TOP_OPS = 20
        CONSTS = 21
        SET_B2 = 1
        SET_ALL = 10

        def nth(per_pair, p, k):
            return per_pair * p + (k + 1)

        def later(p):
            return not isinstance(p, int) or p > 0

        def body(steps, p):
            ahead = not isinstance(p, int) or p < PAIRS - 1

            def do(name, *args):
                if name in steps:
                    steps[name](*args)

            def ex(name, *args):
                if later(p):
                    do(name, p - 1, *args)

            def nxt(name):
                if ahead:
                    do(name, p + 1)

            nxt("load")
            ex("logits")
            ex("up", 0)
            ex("act", 0)
            do("project", p, 0)
            ex("route")
            do("project", p, 1)
            ex("tanh", 0)
            ex("glu", 0)
            ex("up", 1)
            ex("act", 1)
            do("project", p, 2)
            do("project", p, 3)
            ex("combine")
            ex("tanh", 1)
            ex("glu", 1)
            do("project", p, 4)
            do("project", p, 5)
            do("project", p, 6)
            ex("spread", 0)
            ex("spread", 1)
            ex("weigh", 0)
            ex("weigh", 1)
            ex("residual")
            for c, first in ((2, 7), (3, 10)):
                do("project", p, first)
                ex("up", c)
                ex("act", c)
                do("project", p, first + 1)
                ex("spread", c)
                ex("tanh", c)
                do("project", p, first + 2)
                ex("glu", c)
                ex("weigh", c)
            do("project", p, 13)
            do("score", p, 0)
            do("project", p, 14)
            do("project", p, 15)
            do("score", p, 1)
            do("mix", p, 0)
            for c, h in ((4, 2), (5, 4)):
                ex("up", c)
                ex("act", c)
                do("score", p, h)
                ex("spread", c)
                ex("tanh", c)
                do("mix", p, h - 1)
                do("score", p, h + 1)
                ex("glu", c)
                ex("weigh", c)
                do("mix", p, h)
            do("attn_gate", p, 0)
            do("mix", p, H - 1)
            do("group_norm", p)
            do("attn_gate", p, 1)
            do("attn_gate", p, 2)
            do("head_sums", p)
            ex("up", 6)
            do("attn_scale", p)
            ex("act", 6)
            ex("spread", 6)
            ex("tanh", 6)
            do("attn_out", p)
            ex("glu", 6)
            ex("weigh", 6)
            ex("down", 0)
            do("norm2", p)
            nxt("embed")
            ex("finish", 0)
            do("split2", p)
            nxt("norm1")
            ex("down", 1)
            ex("finish", 1)
            nxt("split1")

        def program(eng, steps):
            for name in ("load", "embed", "norm1", "split1"):
                if name in steps:
                    steps[name](0)
            body(steps, 0)
            body(steps, 1)
            with eng.Fori(2, PAIRS - 1) as p:
                body(steps, p)
            body(steps, PAIRS - 1)
            for name, *args in ([("logits",), ("up", 0), ("act", 0), ("route",), ("tanh", 0),
                                 ("glu", 0), ("up", 1), ("act", 1), ("tanh", 1),
                                 ("glu", 1), ("combine",), ("spread", 0), ("spread", 1), ("weigh", 0), ("weigh", 1), ("residual",)]
                                + [(s, c) for c in range(2, FC) for s in ("up", "act", "spread", "tanh", "glu", "weigh")]
                                + [(s, b) for b in range(2) for s in ("down", "finish")]):
                if name in steps:
                    steps[name](PAIRS - 1, *args)

        block = ctx.enter_context(nc.Block())

        @block.sync
        def _(sp):
            n = [0]

            def const(dst, src):
                n[0] += 1
                sp.dma_start(dst, src).then_inc(s_const, 16)

            for i in range(2 * len(PIECES)):
                lo, hi = PIECES[i // 2]
                st = stage[i % 2][:, 0:hi - lo]
                if i >= 2:
                    sp.wait_ge(s_wlo, i - 1)
                if i % 2 == 0:
                    sp.dma_start(st, a["w_stack"][0:P, lo:hi]).then_inc(s_stage[0], 16)
                else:
                    sp.dma_start(st[0:DB, :], a["w_stack"][P:D, lo:hi]).then_inc(s_stage[1], 16)
                    sp.dma_start(st[DB:P, :], a["w_stack"][P:D, lo:hi]).then_inc(s_stage[1], 16)
                if i == 1:
                    const(w_tok[:, :, :], a["w_tok"])
                    const(ident[:, :], a["c_ident"])
                    const(embed[:, 0, :], a["pos"][0:P, :])
                    const(embed[0:IMG_ROWS1, 1, :], a["pos"][SECOND:SECOND + IMG_ROWS1, :])
                    const(hid[0:1, 0, :], a["cls"])
                    const(hid[1:P, 0, :], a["tok_b"].to_broadcast([P - 1, D]))
                    const(hid[0:IMG_ROWS1, 1, :], a["tok_b"].to_broadcast([IMG_ROWS1, D]))
                    const(w_o[:, :, :], a["w_o"])
                    const(w_2[:, 0:FC - 1, :], a["w_2"][0:(FC - 1) * P, :].rearrange("(c p) d -> p c d", p=P))
                    const(w_2[0:LAST, FC - 1, :], a["w_2"][(FC - 1) * P:HID, :])
                    sp.wait_ge(s_set, SET_B2)
                    const(b_2f[0:E1, :], a["b_2"])
                    const(b_2f[LO_ROW:LO_ROW + E1, :], a["b_2"])
                    const(b_13[:, :, :], a["b_13"])
                    const(rot_tab[:, :, :], a["c_rot"])
                    const(mask[:, :, :], a["c_mask"])
                    const(heads64[:, :], a["c_heads"])
                    const(sel_in, a["c_sel"])
                    const(tie_g[:, :], a["c_tie_g"].to_broadcast([P, G * G]))
                    const(tie_e[:, :], a["c_tie_e"].to_broadcast([P, E * E]))
                    const(gate_b[:, :], a["gate_b"].to_broadcast([P, E]))
                    const(gn[:, GN_IN, :], a["gn_wb"])
            assert n[0] == CONSTS

            def load(p):
                if later(p):
                    sp.wait_ge(s_tok, nth(1, p, -1))
                else:
                    sp.wait_ge(s_zero, 1)
                sp.dma_start(patch[:, :, 1:1 + PATCHES], a["patches"][bass.ds(p, 1), :, :, :].rearrange(
                    "a p c t -> (a p) c t")).then_inc(s_patch, 16)

            def embed_text(p):
                if later(p):
                    sp.wait_ge(s_hid2, nth(2, p, -1))
                for b in range(2):
                    sp.dma_start(hid[IMG_ROWS1:P, 2 * b + 1, :], a["txt"][bass.ds(p * 2 + b, 1), :, :].rearrange(
                        "b t d -> (b t) d")).then_inc(s_txt, 16)

            def finish(p, b):
                sp.wait_ge(s_out, nth(2, p, b))
                img = a["out"][bass.ds(p * 2 + b, 1), :, :].rearrange("a t d -> (a t) d")
                sp.dma_start(img[0:P, :], outp[:, 2 * b, :]).then_inc(s_store, 16)
                sp.dma_start(img[P:T, :], outp[P - SECOND:P, 2 * b + 1, :]).then_inc(s_store, 16)

            program(sp, {"load": load, "embed": embed_text, "finish": finish})
            sp.wait_ge(s_store, 64 * PAIRS)

        @block.gpsimd
        def _(pool):
            nc.gpsimd.memset(patch[:, :, 0:1], 0.0).then_inc(s_zero, 1)
            nc.gpsimd.memset(comb[:, :, E:E1], 1.0).then_inc(s_zero, 1)
            nc.gpsimd.memset(neg_half[:, :], -0.5).then_inc(s_zero, 1)
            nc.gpsimd.memset(zeros[:, :, :], 0.0).then_inc(s_zero, 1)
            pool.wait_ge(s_zero, 4)

            def norm1(p):
                pool.wait_ge(s_ln1, nth(LN_OPS, p, LN_OPS - 1))
                nc.gpsimd.tensor_tensor(rstd1[:, :], rstd1[:, :], neg_half[:, 0:CH], ALU.pow).then_inc(s_rstd1, 1)

            def project(p, n):
                if n < 2 * H:
                    pool.wait_ge(s_swap, 2 * nth(2 * H, p, n))
                    s = swap[:, n % 2, :].rearrange("p (b t) -> p b t", b=2)
                    k = 2 * (n % 2) + 1
                    nc.gpsimd.tensor_tensor(s, s, rot_tab[:, k:k + 1, :].to_broadcast([P, 2, T]),
                                            ALU.mult).then_inc(s_sin, 1)

            def group_norm(p):
                pool.wait_ge(s_gn, nth(GN_OPS, p, 12))
                nc.gpsimd.tensor_tensor(gn[:, GN_RSTD, :], gn[:, GN_RSTD, :], neg_half[:, 0:2 * HVC],
                                        ALU.pow).then_inc(s_gnrstd, 1)

            def attn_scale(p):
                for c in range(HVC):
                    pool.wait_ge(s_scaled, nth(2 * HVC, p, 2 * c + 1))
                    pool.wait_ge(s_gate, nth(HVC, p, c))
                    nc.gpsimd.tensor_tensor(ret(c), ret(c), gate(c), ALU.mult).then_inc(s_gated, 1)

            def norm2(p):
                pool.wait_ge(s_ln2, nth(LN_OPS, p, LN_OPS - 1))
                nc.gpsimd.tensor_tensor(rstd2[:, :], rstd2[:, :], neg_half[:, 0:CH], ALU.pow).then_inc(s_rstd2, 1)

            def residual(p):
                if later(p):
                    pool.wait_ge(s_store, 64 * nth(1, p, -1))
                nc.gpsimd.tensor_tensor(outp[:, :, :], hid2[:, :, :], zeros[:, :, :].to_broadcast([P, CH, D]),
                                        ALU.add).then_inc(s_res, 1)

            def weigh(p, c):
                r = ffn_rows(c)
                pool.wait_ge(s_glu, nth(FC, p, c))
                pool.wait_ge(s_weight, nth(FC, p, c))
                nc.gpsimd.tensor_tensor(gT[0:r, c, :], gT[0:r, c, :], glu[0:r, c % 2, 1, :],
                                        ALU.mult).then_inc(s_exout, 1)

            program(pool, {"norm1": norm1, "project": project, "group_norm": group_norm,
                           "attn_scale": attn_scale, "norm2": norm2, "residual": residual, "weigh": weigh})

        @block.scalar
        def _(act):
            for i in range(2 * len(PIECES)):
                lo, hi = PIECES[i // 2]
                dst = (wA_hi if i % 2 == 0 else wB_hi)[:, lo:hi]
                act.wait_ge(s_stage[i % 2], (16 if i % 2 == 0 else 32) * (i // 2 + 1))
                nc.scalar.activation(dst, stage[i % 2][:, 0:hi - lo], ACT.Copy).then_inc(s_whi, 1)
            act.wait_ge(s_const, 16 * CONSTS)
            act.wait_ge(s_set, SET_B2)
            nc.scalar.activation(b_2hi[:, :], b_2f, ACT.Copy).then_inc(s_sel, 1)
            nc.scalar.activation(sel[:, :, :].rearrange("p c r -> p (c r)"), sel_in, ACT.Copy).then_inc(s_sel, 1)

            def split1(p):
                act.wait_ge(s_x1T, nth(2, p, 0))
                if later(p):
                    act.wait_ge(s_gproj, nth(HVC, p, -1))
                nc.scalar.activation(x1A_hi[:, :], psA[:, 2, 0:TT], ACT.Copy).then_inc(s_x1hi, 1)
                act.wait_ge(s_x1T, nth(2, p, 1))
                nc.scalar.activation(x1B[0:DB, :], psA[0:DB, 3, 0:TT], ACT.Copy).then_inc(s_x1hi, 1)
                nc.scalar.activation(x1B_z[0:DB, :], psA[0:DB, 3, 0:TT], ACT.Copy).then_inc(s_x1hi, 1)

            def project(p, n):
                bank = psA[:, n % 4, :]
                act.wait_ge(s_proj, nth(QKV, p, n))
                if n < 2 * H:
                    if n >= 2 or later(p):
                        act.wait_ge(s_rot, nth(2 * H, p, n - 2))
                    nc.scalar.activation(swap[0:64, n % 2, :], bank[64:P, 0:TT], ACT.Copy).then_inc(s_swap, 1)
                    nc.scalar.activation(swap[64:P, n % 2, :], bank[0:64, 0:TT], ACT.Copy).then_inc(s_swap, 1)
                else:
                    if n == 2 * H and later(p):
                        act.wait_ge(s_pv, nth(2 * H, p, -1))
                    nc.scalar.activation(val[:, n - 2 * H, :], bank[:, 0:HV], ACT.Copy).then_inc(s_val, 1)

            def mix(p, h):
                if h % 2 == 1:
                    c = h // 2
                    act.wait_ge(s_pv, nth(2 * H, p, 2 * h + 1))
                    nc.scalar.activation(ret(c), psA[:, 3 - c % 2, 0:TT], ACT.Copy).then_inc(s_ret, 1)

            def attn_gate(p, c):
                act.wait_ge(s_gproj, nth(HVC, p, c))
                nc.scalar.activation(gate(c), psA[:, c, 0:TT], ACT.Tanh, scale=0.5).then_inc(s_tanh, 1)

            def split2(p):
                act.wait_ge(s_x2T, nth(2, p, 0))
                if later(p):
                    act.wait_ge(s_up, nth(4 * FC, p, -1))
                nc.scalar.activation(x2A_hi[:, :], psF[:, 2, 0:TT], ACT.Copy).then_inc(s_x2hi, 1)
                act.wait_ge(s_x2T, nth(2, p, 1))
                nc.scalar.activation(x2B[0:DB, :], psF[0:DB, 3, 0:TT], ACT.Copy).then_inc(s_x2hi, 1)
                nc.scalar.activation(x2B_z[DB:P, :], psF[0:DB, 3, 0:TT], ACT.Copy).then_inc(s_x2hi, 1)

            def logits(p):
                act.wait_ge(s_logit, nth(1, p, 0))
                if later(p):
                    act.wait_ge(s_glu, nth(FC, p, -1))
                nc.scalar.activation(th[0:E, :], psF[0:E, bank_of("logits"), 0:TT], ACT.Copy).then_inc(s_lgcol, 1)

            def route(p):
                act.wait_ge(s_top, nth(TOP_OPS, p, 1))
                nc.scalar.activation(lg[:, 1, :], lg[:, 0, :], ACT.Exp).then_inc(s_exp, 1)

            def combine(p):
                act.wait_ge(s_combT, nth(1, p, 0))
                if later(p):
                    act.wait_ge(s_down, nth(2, p, -1))
                nc.scalar.activation(combR[0:E1, :], psF[0:E1, bank_of("combine"), 0:TT], ACT.Copy).then_inc(s_combhi, 1)

            def spread(p, c):
                r = ffn_rows(c)
                act.wait_ge(s_spread, nth(FC, p, c))
                nc.scalar.activation(gT[0:r, c, :], psF[0:r, bank_of("spread", c), 0:TT], ACT.Copy).then_inc(s_weight, 1)

            def act_(p, c):
                r = ffn_rows(c)
                if c >= 2 or later(p):
                    act.wait_ge(s_exout, nth(FC, p, c - 2))
                for part in range(2):
                    act.wait_ge(s_up, nth(4 * FC, p, 4 * c + part))
                    nc.scalar.activation(glu[0:r, c % 2, part, :], psF[0:r, bank_of("up", c, part), 0:TT], ACT.Identity,
                                         bias=b_13[0:r, c, part:part + 1]).then_inc(s_up1, 1)

            def tanh(p, c):
                r = ffn_rows(c)
                if c == 0:
                    act.wait_ge(s_lgrow, nth(1, p, 0))
                act.wait_ge(s_clip, nth(2 * FC, p, 2 * c))
                if c >= 1 or later(p):
                    act.wait_ge(s_glu, nth(FC, p, c - 1))
                nc.scalar.activation(th[0:r, :], glu[0:r, c % 2, 0, :], ACT.Tanh, scale=ALPHA / 2).then_inc(s_sig, 1)

            program(act, {"split1": split1, "project": project, "mix": mix, "attn_gate": attn_gate,
                          "split2": split2, "logits": logits, "route": route, "combine": combine,
                          "spread": spread, "act": act_, "tanh": tanh})

        @block.vector
        def _(dve):
            nc.vector.memset(b_2f, 0.0).then_inc(s_set, 1)
            for rows in (combR[:, :], x1B_z[DB:P, :], x2B_z[0:DB, :], wB_lo[0:DB, W_F:FFC]):
                nc.vector.memset(rows.bitcast(mybir.dt.uint32), 0).then_inc(s_set, 1)
            for i in range(2 * len(PIECES)):
                lo, hi = PIECES[i // 2]
                st = stage[i % 2][:, 0:hi - lo]
                dve.wait_ge(s_whi, i + 1)
                if i % 2 == 0:
                    nc.vector.tensor_tensor(wA_lo[:, lo:hi], st, wA_hi[:, lo:hi].bitcast(F32),
                                            ALU.subtract).then_inc(s_wlo, 1)
                else:
                    r, off = (0, 0) if hi <= W_F else (DB, W_F)
                    nc.vector.tensor_tensor(wB_lo[r:r + DB, lo - off:hi - off], st[r:r + DB, :],
                                            wB_hi[r:r + DB, lo:hi].bitcast(F32), ALU.subtract).then_inc(s_wlo, 1)
            dve.wait_ge(s_const, 16 * CONSTS)
            nc.vector.tensor_tensor(embed[:, 0, :], embed[:, 0, :], hid[:, 0, :], ALU.add).then_inc(s_set, 1)
            nc.vector.tensor_tensor(embed[0:IMG_ROWS1, 1, :], embed[0:IMG_ROWS1, 1, :], hid[0:IMG_ROWS1, 1, :],
                                    ALU.add).then_inc(s_set, 1)
            nc.vector.tensor_scalar(gn_w[:, :], gn[:, GN_IN, 0:HVC], 0.5, None, ALU.mult).then_inc(s_set, 1)
            nc.vector.tensor_scalar(gn_b[:, :], gn[:, GN_IN, HVC:2 * HVC], 0.5, None, ALU.mult).then_inc(s_set, 1)
            dve.wait_ge(s_sel, 1)
            nc.vector.tensor_tensor(b_2lo[:, :], b_2f, b_2hi[:, :].bitcast(F32), ALU.subtract).then_inc(s_set, 1)
            dve.wait_ge(s_set, SET_ALL)

            hid4 = hid[:, :, :].rearrange("p (b k) d -> p b k d", k=2)

            def embed_image(p):
                dve.wait_ge(s_tok, nth(1, p, 0))
                nc.vector.tensor_tensor(hid4[:, :, 0, :], psA[:, 0:2, 0:D],
                                        embed[:, 0:1, :].to_broadcast([P, 2, D]), ALU.add).then_inc(s_hid, 1)
                nc.vector.tensor_tensor(hid4[0:IMG_ROWS1, :, 1, :], psA[0:IMG_ROWS1, 0:2, D:2 * D],
                                        embed[0:IMG_ROWS1, 1:2, :].to_broadcast([IMG_ROWS1, 2, D]),
                                        ALU.add).then_inc(s_hid, 1)

            def layer_norm(p, src, bn, mv, rstd, s_stat, s_rstd, s_done):
                for c in range(CH):
                    nc.vector.bn_stats(bn[:, c, :], src[:, c, :]).then_inc(s_stat, 1)
                dve.wait_ge(s_stat, nth(LN_OPS, p, CH - 1))
                nc.vector.memset(rstd[:, :], EPS)
                for c in range(CH):
                    nc.vector.bn_aggr(mv[:, c, :], bn[:, c, :]).then_inc(s_stat, 1)
                dve.wait_ge(s_stat, nth(LN_OPS, p, 2 * CH - 1))
                nc.vector.tensor_tensor(rstd[:, :], mv[:, :, 1], rstd[:, :], ALU.add).then_inc(s_stat, 1)
                dve.wait_ge(s_rstd, nth(1, p, 0))
                for c in range(CH):
                    nc.vector.tensor_scalar(normed[:, c, :], src[:, c, :], mv[:, c, 0:1], rstd[:, c:c + 1],
                                            ALU.subtract, ALU.mult).then_inc(s_done, 1)

            def norm1(p):
                dve.wait_ge(s_hid, nth(2, p, 1))
                dve.wait_ge(s_txt, 32 * nth(1, p, 0))
                if later(p):
                    dve.wait_ge(s_x2T, nth(2, p, -1))
                layer_norm(p, hid, bn1, mv1, rstd1, s_ln1, s_rstd1, s_norm1)

            def norm2(p):
                dve.wait_ge(s_x1T, nth(2, p, 1))
                dve.wait_ge(s_hid2, nth(2, p, 1))
                layer_norm(p, hid2, bn2, mv2, rstd2, s_ln2, s_rstd2, s_norm2)

            def split1(p):
                dve.wait_ge(s_x1hi, nth(3, p, 0))
                nc.vector.tensor_tensor(x1A_lo[:, :], psA[:, 2, 0:TT], x1A_hi[:, :].bitcast(F32),
                                        ALU.subtract).then_inc(s_x1lo, 1)
                dve.wait_ge(s_x1hi, nth(3, p, 2))
                nc.vector.tensor_tensor(x1B[DB:P, :], psA[0:DB, 3, 0:TT], x1B[0:DB, :].bitcast(F32),
                                        ALU.subtract).then_inc(s_x1lo, 1)

            def split2(p):
                dve.wait_ge(s_x2hi, nth(3, p, 0))
                nc.vector.tensor_tensor(x2A_lo[:, :], psF[:, 2, 0:TT], x2A_hi[:, :].bitcast(F32),
                                        ALU.subtract).then_inc(s_x2lo, 1)
                dve.wait_ge(s_x2hi, nth(3, p, 2))
                nc.vector.tensor_tensor(x2B[DB:P, :], psF[0:DB, 3, 0:TT], x2B[0:DB, :].bitcast(F32),
                                        ALU.subtract).then_inc(s_x2lo, 1)

            def add_sin(p, n):
                dve.wait_ge(s_cos, nth(2 * H, p, n))
                dve.wait_ge(s_sin, nth(2 * H, p, n))
                nc.vector.tensor_tensor(qk[:, n, :], qk[:, n, :], swap[:, n % 2, :], ALU.add).then_inc(s_rot, 1)

            def project(p, n):
                if 1 <= n <= 2 * H:
                    add_sin(p, n - 1)
                if n < 2 * H:
                    dve.wait_ge(s_swap, 2 * nth(2 * H, p, n))
                    if n == 0 and later(p):
                        dve.wait_ge(s_wo, nth(2, p, -1))
                    k = 2 * (n % 2)
                    nc.vector.tensor_tensor(qk[:, n, :].rearrange("p (b t) -> p b t", b=2),
                                            psA[:, n % 4, 0:TT].rearrange("p (b t) -> p b t", b=2),
                                            rot_tab[:, k:k + 1, :].to_broadcast([P, 2, T]),
                                            ALU.mult).then_inc(s_cos, 1)

            def score(p, h):
                for b in range(2):
                    n = 2 * h + b
                    dve.wait_ge(s_score, nth(2 * H, p, n))
                    if h > 0 or later(p):
                        dve.wait_ge(s_pv, nth(2 * H, p, n - 2))
                    nc.vector.tensor_tensor(prob[:, b, :], psA[:, b, 0:SC], mask[:, h, :], ALU.mult).then_inc(s_prob, 1)

            def mix(p, h):
                if h % 2 == 1:
                    c = h // 2
                    dve.wait_ge(s_ret, nth(HVC, p, c))
                    for b in range(2):
                        nc.vector.bn_stats(rbn[:, 2 * c + b, :], ret(c)[:, b * T:(b + 1) * T]).then_inc(s_gn, 1)

            def group_norm(p):
                k = [2 * HVC]

                def link(ins):
                    k[0] += 1
                    ins.then_inc(s_gn, 1)
                    dve.wait_ge(s_gn, nth(GN_OPS, p, k[0] - 1))

                dve.wait_ge(s_gn, nth(GN_OPS, p, 2 * HVC - 1))
                nc.vector.memset(gn[:, GN_RSTD, :], EPS)
                for i in range(2 * HVC):
                    last = nc.vector.bn_aggr(rmv[:, i, :], rbn[:, i, :])
                link(last)
                link(nc.vector.tensor_tensor(gn[:, GN_T, :], rmv[:, :, 0], rmv[:, :, 0], ALU.mult))
                link(nc.vector.tensor_tensor(rmv[:, :, 1], rmv[:, :, 1], gn[:, GN_T, :], ALU.add))
                dve.wait_ge(s_gnsum, nth(1, p, 0))
                link(nc.vector.tensor_copy(gn[:, GN_MEAN:GN_SQ + 1, :],
                                           psA[:, 3, 0:4 * HVC].rearrange("p (i s) -> p s i", s=2)))
                link(nc.vector.tensor_tensor(gn[:, GN_T, :], gn[:, GN_MEAN, :], gn[:, GN_MEAN, :], ALU.mult))
                link(nc.vector.tensor_tensor(gn[:, GN_SQ, :], gn[:, GN_SQ, :], gn[:, GN_T, :], ALU.subtract))
                link(nc.vector.tensor_tensor(gn[:, GN_RSTD, :], gn[:, GN_SQ, :], gn[:, GN_RSTD, :], ALU.add))
                assert k[0] == 13

            def attn_gate(p, c):
                dve.wait_ge(s_tanh, nth(HVC, p, c))
                nc.vector.scalar_tensor_tensor(gate(c), gate(c), 1.0, psA[:, c, 0:TT],
                                               ALU.add, ALU.mult).then_inc(s_gate, 1)

            def attn_scale(p):
                def by_chunk(row):
                    return gn[:, row, :].rearrange("p (c b) -> p c b", b=2)

                dve.wait_ge(s_gnrstd, nth(1, p, 0))
                nc.vector.tensor_tensor(by_chunk(GN_SCALE), by_chunk(GN_RSTD), gn_w[:, :, None].to_broadcast([P, HVC, 2]),
                                        ALU.mult).then_inc(s_gn, 1)
                dve.wait_ge(s_gn, nth(GN_OPS, p, 13))
                nc.vector.tensor_tensor(gn[:, GN_T, :], gn[:, GN_MEAN, :], gn[:, GN_SCALE, :], ALU.mult).then_inc(s_gn, 1)
                dve.wait_ge(s_gn, nth(GN_OPS, p, 14))
                nc.vector.tensor_tensor(by_chunk(GN_SHIFT), gn_b[:, :, None].to_broadcast([P, HVC, 2]), by_chunk(GN_T),
                                        ALU.subtract).then_inc(s_gn, 1)
                dve.wait_ge(s_gn, nth(GN_OPS, p, 15))
                for i in range(2 * HVC):
                    x = ret(i // 2)[:, (i % 2) * T:(i % 2 + 1) * T]
                    nc.vector.tensor_scalar(x, x, gn[:, GN_SCALE, i:i + 1], gn[:, GN_SHIFT, i:i + 1],
                                            ALU.mult, ALU.add).then_inc(s_scaled, 1)

            def attn_out(p):
                for b in range(2):
                    dve.wait_ge(s_wo, nth(2, p, b))
                    if b == 0 and later(p):
                        dve.wait_ge(s_res, nth(1, p, -1))
                    nc.vector.tensor_tensor(hid2[:, 2 * b:2 * b + 2, :],
                                            psA[:, b, 0:2 * D].rearrange("p (k d) -> p k d", k=2),
                                            hid[:, 2 * b:2 * b + 2, :], ALU.add).then_inc(s_hid2, 1)

            def route(p):
                k = [0]

                def link(ins):
                    k[0] += 1
                    ins.then_inc(s_top, 1)
                    dve.wait_ge(s_top, nth(TOP_OPS, p, k[0] - 1))

                def by_row(x, n):
                    return x.rearrange("p (c n) -> p c n", n=n)

                def rank(values, n, ties, out):
                    v = by_row(values, n)
                    other = v[:, :, None, :].to_broadcast([P, CH, n, n])
                    own = v[:, :, :, None].to_broadcast([P, CH, n, n])
                    a_ = cmp_a[:, 0:CH * n * n]
                    b_ = cmp_b[:, 0:CH * n * n]
                    a4 = a_.rearrange("p (c i j) -> p c i j", i=n, j=n)
                    b4 = b_.rearrange("p (c i j) -> p c i j", i=n, j=n)
                    link(nc.vector.tensor_tensor(a4, other, own, ALU.is_gt))
                    link(nc.vector.tensor_tensor(b4, other, own, ALU.is_equal))
                    link(nc.vector.tensor_tensor(by_row(b_, n * n), by_row(b_, n * n),
                                                 ties[:, None, :].to_broadcast([P, CH, n * n]), ALU.mult))
                    link(nc.vector.tensor_tensor(a_, a_, b_, ALU.add))
                    link(nc.vector.reduce_sum(out, a_.rearrange("p (i j) -> p i j", j=n), axis=AX_X))

                logits = psF[:, bank_of("route"), 0:CH * E]
                dve.wait_ge(s_lgrow, nth(1, p, 0))
                link(nc.vector.reduce_max(few[:, 0, 0:CH], by_row(logits, E), axis=AX_X))
                link(nc.vector.tensor_tensor(by_row(lg[:, 0, :], E), by_row(logits, E),
                                             few[:, 0, 0:CH, None].to_broadcast([P, CH, E]), ALU.subtract))
                dve.wait_ge(s_exp, nth(1, p, 0))
                link(nc.vector.reduce_sum(few[:, 1, 0:CH], by_row(lg[:, 1, :], E), axis=AX_X))
                link(nc.vector.reciprocal(few[:, 2, 0:CH], few[:, 1, 0:CH]))
                link(nc.vector.tensor_tensor(by_row(lg[:, 2, :], E), by_row(lg[:, 1, :], E),
                                             few[:, 2, 0:CH, None].to_broadcast([P, CH, E]), ALU.mult))
                link(nc.vector.tensor_tensor(by_row(lg[:, 3, :], E), by_row(lg[:, 2, :], E),
                                             gate_b[:, None, :].to_broadcast([P, CH, E]), ALU.add))
                pairs = lg[:, 3, :].rearrange("p (m two) -> p m two", two=2)
                link(nc.vector.tensor_tensor(few[:, 3, :], pairs[:, :, 0], pairs[:, :, 1], ALU.add))
                rank(few[:, 3, :], G, tie_g[:, :], few[:, 4, :])
                link(nc.vector.tensor_scalar(few[:, 5, :], few[:, 4, :], 2.0, -BIG, ALU.is_ge, ALU.mult))
                link(nc.vector.tensor_tensor(lg[:, 4, :].rearrange("p (m two) -> p m two", two=2), pairs,
                                             few[:, 5, :, None].to_broadcast([P, CH * G, 2]), ALU.add))
                rank(lg[:, 4, :], E, tie_e[:, :], lg[:, 0, :])
                if later(p):
                    dve.wait_ge(s_combT, nth(1, p, -1))
                nc.vector.scalar_tensor_tensor(comb[:, :, 0:E], by_row(lg[:, 0, :], E), 2.0, by_row(lg[:, 2, :], E),
                                               ALU.is_lt, ALU.mult).then_inc(s_top, 1)
                assert k[0] + 1 == TOP_OPS, k[0]

            def combine(p):
                dve.wait_ge(s_combhi, nth(1, p, 0))
                nc.vector.tensor_tensor(combR[LO_ROW:LO_ROW + E1, :], psF[0:E1, bank_of("combine"), 0:TT],
                                        combR[0:E1, :].bitcast(F32), ALU.subtract).then_inc(s_comblo, 1)

            def glu_(p, c):
                r = ffn_rows(c)
                odd = glu[0:r, c % 2, 1, :]
                dve.wait_ge(s_sig, nth(FC, p, c))
                dve.wait_ge(s_lin, nth(FC, p, c))
                nc.vector.scalar_tensor_tensor(odd, th[0:r, :], 1.0, odd, ALU.add, ALU.mult).then_inc(s_glu, 1)

            def act_(p, c):
                r = ffn_rows(c)
                even, odd = glu[0:r, c % 2, 0, :], glu[0:r, c % 2, 1, :]
                for part in range(2):
                    x = glu[0:r, c % 2, part, :]
                    dve.wait_ge(s_up, nth(4 * FC, p, 4 * c + 2 + part))
                    dve.wait_ge(s_up1, nth(2 * FC, p, 2 * c + part))
                    nc.vector.scalar_tensor_tensor(x, psF[0:r, bank_of("up", c, 2 + part), 0:TT],
                                                   b_13[0:r, c, 2 + part:3 + part], x,
                                                   ALU.add, ALU.mult).then_inc(s_prod, 1)
                dve.wait_ge(s_prod, nth(2 * FC, p, 2 * c))
                nc.vector.tensor_scalar(even, even, LIMIT, None, ALU.min).then_inc(s_clip, 1)
                dve.wait_ge(s_prod, nth(2 * FC, p, 2 * c + 1))
                nc.vector.tensor_scalar(odd, odd, LIMIT, -LIMIT, ALU.min, ALU.max).then_inc(s_clip, 1)
                dve.wait_ge(s_clip, nth(2 * FC, p, 2 * c + 1))
                nc.vector.scalar_tensor_tensor(odd, odd, 1.0, even, ALU.add, ALU.mult).then_inc(s_lin, 1)

            def finish(p, b):
                dve.wait_ge(s_down, nth(2, p, b))
                if b == 0:
                    dve.wait_ge(s_res, nth(1, p, 0))
                rows = outp[:, 2 * b:2 * b + 2, :]
                nc.vector.tensor_tensor(rows, psF[:, b, 0:2 * D].rearrange("p (k d) -> p k d", k=2), rows,
                                        ALU.add).then_inc(s_out, 1)

            program(dve, {"embed": embed_image, "norm1": norm1, "split1": split1, "project": project,
                          "score": score, "mix": mix, "group_norm": group_norm, "attn_gate": attn_gate,
                          "attn_scale": attn_scale, "attn_out": attn_out, "norm2": norm2, "split2": split2,
                          "route": route, "combine": combine, "act": act_, "glu": glu_, "finish": finish})

        @block.tensor
        def _(pe):
            pe.wait_ge(s_const, 16 * CONSTS)
            pe.wait_ge(s_zero, 4)
            pe.wait_ge(s_wlo, 2 * len(PIECES))
            pe.wait_ge(s_set, SET_ALL)
            pe.wait_ge(s_sel, 2)

            def weights_by_tokens(out, w0, m, xA_hi, xA_lo, xB, xB_z):
                w = slice(w0, w0 + m)
                lo = slice(w0, w0 + m) if w0 < W_F else slice(w0 - W_F, w0 - W_F + m)
                nc.tensor.matmul(out, wA_hi[:, w], xA_hi[:, :], start=True, stop=False)
                nc.tensor.matmul(out, wA_lo[:, w], xA_hi[:, :], start=False, stop=False)
                nc.tensor.matmul(out, wA_hi[:, w], xA_lo[:, :], start=False, stop=False)
                nc.tensor.matmul(out, wB_hi[:, w], xB[:, :], start=False, stop=False)
                return nc.tensor.matmul(out, wB_lo[:, lo], xB_z[:, :], start=False, stop=True)

            def tokens_by_weights(out, c, w0, m, xA_hi, xA_lo, xB, xB_z):
                w = slice(w0, w0 + m)
                t = slice(row_col(c), row_col(c) + P)
                nc.tensor.matmul(out, xA_hi[:, t], wA_hi[:, w], start=True, stop=False)
                nc.tensor.matmul(out, xA_hi[:, t], wA_lo[:, w], start=False, stop=False)
                nc.tensor.matmul(out, xA_lo[:, t], wA_hi[:, w], start=False, stop=False)
                nc.tensor.matmul(out, xB[:, t], wB_hi[:, w], start=False, stop=False)
                return nc.tensor.matmul(out, xB_z[:, t], wB_lo[:, w], start=False, stop=True)

            def embed_(p):
                pe.wait_ge(s_patch, 16 * nth(1, p, 0))
                if later(p):
                    pe.wait_ge(s_hid2, nth(2, p, -1))
                for b in range(2):
                    for k in range(2):
                        m, t0 = (P, 0) if k == 0 else (IMG_ROWS1, SECOND)
                        for c in range(PCH):
                            last = nc.tensor.matmul(psA[0:m, b, k * D:(k + 1) * D], patch[:, 2 * c + b, t0:t0 + m],
                                                    w_tok[:, c, :], start=(c == 0), stop=(c == PCH - 1))
                last.then_inc(s_tok, 1)

            def to_columns(bankA, bankB, s_done):
                for c in range(CH):
                    t = slice(row_col(c), row_col(c) + P)
                    last = nc.tensor.transpose(bankA[:, t], normed[:, c, 0:P], ident[:, :])
                last.then_inc(s_done, 1)
                for c in range(CH):
                    t = slice(row_col(c), row_col(c) + P)
                    last = nc.tensor.transpose(bankB[0:DB, t], normed[:, c, P:D], ident[:, :])
                last.then_inc(s_done, 1)

            def split1(p):
                pe.wait_ge(s_norm1, nth(CH, p, CH - 1))
                if later(p):
                    pe.wait_ge(s_gate, nth(HVC, p, -1))
                    pe.wait_ge(s_gn, nth(GN_OPS, p - 1, 9))
                to_columns(psA[:, 2, :], psA[:, 3, :], s_x1T)

            def project(p, n):
                bank = psA[:, n % 4, :]
                if n == 0:
                    pe.wait_ge(s_x1lo, nth(2, p, 1))
                    pe.wait_ge(s_hid, nth(2, p, 1))
                elif n >= 4:
                    pe.wait_ge(s_swap, 2 * nth(2 * H, p, n - 4))
                    pe.wait_ge(s_cos, nth(2 * H, p, n - 4))
                if n < 2 * H:
                    head, k = n // 2, n % 2
                    w0 = k * H * DQK + head * DQK
                    last = weights_by_tokens(bank[:, 0:TT], w0, P, x1A_hi, x1A_lo, x1B, x1B_z)
                else:
                    last = tokens_by_weights(bank[:, 0:HV], n - 2 * H, W_V, HV, x1A_hi, x1A_lo, x1B, x1B_z)
                last.then_inc(s_proj, 1)

            def score(p, h):
                pe.wait_ge(s_rot, nth(2 * H, p, 2 * h + 1))
                for b in range(2):
                    if h == 0:
                        pe.wait_ge(s_val, nth(CH, p, b))
                    else:
                        pe.wait_ge(s_prob, nth(2 * H, p, 2 * h - 2 + b))
                    t0 = b * T
                    q, k = qk[:, 2 * h, :], qk[:, 2 * h + 1, :]
                    nc.tensor.matmul(psA[:, b, 0:T], k[:, t0:t0 + P], q[:, t0:t0 + T], start=True, stop=True)
                    nc.tensor.matmul(psA[:, b, T:SC], k[:, t0 + SECOND:t0 + T], q[:, t0 + P:t0 + T],
                                     start=True, stop=True).then_inc(s_score, 1)

            def mix(p, h):
                c = h // 2
                bank = psA[:, 3 - c % 2, :]
                rows = slice(64 * (h % 2), 64 * (h % 2) + 64)
                v = slice(h * DV, (h + 1) * DV)
                if h % 2 == 0:
                    if c < 2:
                        pe.wait_ge(s_val, nth(CH, p, CH - 1))
                    else:
                        pe.wait_ge(s_ret, nth(HVC, p, c - 2))
                for b in range(2):
                    pe.wait_ge(s_prob, nth(2 * H, p, 2 * h + b))
                    nc.tensor.matmul(bank[rows, b * T:(b + 1) * T], val[:, 2 * b, v], prob[:, b, 0:T],
                                     start=True, stop=False)
                    nc.tensor.matmul(bank[rows, b * T + P:(b + 1) * T], val[:, 2 * b + 1, v], prob[:, b, T:SC],
                                     start=False, stop=True).then_inc(s_pv, 1)

            def head_sums(p):
                pe.wait_ge(s_ret, nth(HVC, p, HVC - 1))
                pe.wait_ge(s_gn, nth(GN_OPS, p, 8))
                nc.tensor.matmul(psA[:, 3, 0:4 * HVC], heads64[:, :], rmv[:, :, :].rearrange("p i s -> p (i s)"),
                                 start=True, stop=True).then_inc(s_gnsum, 1)

            def attn_gate(p, c):
                if c < 2:
                    pe.wait_ge(s_prob, nth(2 * H, p, 2 * H - 2 + c))
                else:
                    pe.wait_ge(s_ret, nth(HVC, p, 1))
                weights_by_tokens(psA[:, c, 0:TT], W_G + c * P, P, x1A_hi, x1A_lo, x1B, x1B_z).then_inc(s_gproj, 1)

            def attn_out(p):
                pe.wait_ge(s_gated, nth(HVC, p, HVC - 1))
                for b in range(2):
                    for k in range(2):
                        t0 = row_col(2 * b + k)
                        for c in range(HVC):
                            last = nc.tensor.matmul(psA[:, b, k * D:(k + 1) * D], ret(c)[:, t0:t0 + P], w_o[:, c, :],
                                                    start=(c == 0), stop=(c == HVC - 1))
                    last.then_inc(s_wo, 1)

            def split2(p):
                pe.wait_ge(s_norm2, nth(CH, p, CH - 1))
                if later(p):
                    pe.wait_ge(s_exout, nth(FC, p, -1))
                to_columns(psF[:, 2, :], psF[:, 3, :], s_x2T)

            def bank_for(p, *item):
                i = ROUND.index(item)
                if i < 2:
                    if later(p):
                        pe.wait_ge(s_out, nth(2, p, -2 + i))
                elif i == 2:
                    pe.wait_ge(s_x2lo, nth(2, p, 0))
                elif i == 3:
                    pe.wait_ge(s_x2lo, nth(2, p, 1))
                else:
                    kind, *at = ROUND[i - 4]
                    if kind == "logits":
                        pe.wait_ge(s_lgcol, nth(1, p, 0))
                    elif kind == "route":
                        pe.wait_ge(s_top, nth(TOP_OPS, p, 1))
                    elif kind == "combine":
                        pe.wait_ge(s_comblo, nth(1, p, 0))
                    elif kind == "spread":
                        pe.wait_ge(s_weight, nth(FC, p, at[0]))
                    elif at[1] < 2:
                        pe.wait_ge(s_up1, nth(2 * FC, p, 2 * at[0] + at[1]))
                    else:
                        pe.wait_ge(s_prod, nth(2 * FC, p, 2 * at[0] + at[1] - 2))
                return psF[:, i % 4, :]

            def logits(p):
                pe.wait_ge(s_x2lo, nth(2, p, 1))
                bank = bank_for(p, "logits")
                weights_by_tokens(bank[0:E, 0:TT], W_R, E, x2A_hi, x2A_lo, x2B, x2B_z).then_inc(s_logit, 1)

            def route(p):
                bank = bank_for(p, "route")
                pe.wait_ge(s_lgcol, nth(1, p, 0))
                for c in range(CH):
                    last = nc.tensor.matmul(bank[:, c * E:(c + 1) * E], th[0:E, row_col(c):row_col(c) + P],
                                            ident[0:E, 0:E], start=True, stop=True)
                last.then_inc(s_lgrow, 1)

            def combine(p):
                bank = bank_for(p, "combine")
                pe.wait_ge(s_top, nth(TOP_OPS, p, TOP_OPS - 1))
                for c in range(CH):
                    last = nc.tensor.transpose(bank[0:E1, row_col(c):row_col(c) + P], comb[:, c, :], ident[:, :])
                last.then_inc(s_combT, 1)

            def spread(p, c):
                r = ffn_rows(c)
                bank = bank_for(p, "spread", c)
                if c == 0:
                    pe.wait_ge(s_comblo, nth(1, p, 0))
                nc.tensor.matmul(bank[0:r, 0:TT], sel[0:LO_ROW + E1, c, 0:r], combR[0:LO_ROW + E1, :],
                                 start=True, stop=True).then_inc(s_spread, 1)

            def up(p, c):
                r = ffn_rows(c)
                for part in range(4):
                    bank = bank_for(p, "up", c, part)
                    weights_by_tokens(bank[0:r, 0:TT], up_col(c, part), r, x2A_hi, x2A_lo, x2B,
                                      x2B_z).then_inc(s_up, 1)

            def down(p, b):
                for k in range(2):
                    t0 = row_col(2 * b + k)
                    out = psF[:, b, k * D:(k + 1) * D]
                    cw = combR[0:LO_ROW + E1, t0:t0 + P]
                    if b == 0 and k == 0:
                        pe.wait_ge(s_weight, nth(FC, p, FC - 1))
                        pe.wait_ge(s_prod, nth(2 * FC, p, 2 * FC - 1))
                    nc.tensor.matmul(out, cw, b_2hi[:, :], start=True, stop=False)
                    nc.tensor.matmul(out, cw, b_2lo[:, :], start=False, stop=False)
                    for c in range(FC):
                        r = ffn_rows(c)
                        if b == 0 and k == 0:
                            pe.wait_ge(s_exout, nth(FC, p, c))
                        last = nc.tensor.matmul(out, gT[0:r, c, t0:t0 + P], w_2[0:r, c, :],
                                                start=False, stop=(c == FC - 1))
                last.then_inc(s_down, 1)

            program(pe, {"embed": embed_, "split1": split1, "project": project, "score": score, "mix": mix,
                         "head_sums": head_sums, "attn_gate": attn_gate, "attn_out": attn_out,
                         "split2": split2, "logits": logits, "route": route, "combine": combine,
                         "spread": spread, "up": up, "down": down})


def _tables():
    import numpy as np
    half = DQK // 2
    pos = np.arange(T, dtype=np.float32)
    inv_freq = np.float32(1.0) / np.float32(10000.0) ** (np.arange(half, dtype=np.float32) / np.float32(half))
    angles = (inv_freq[:, None] * pos[None, :]).astype(np.float32).astype(np.float64)
    zeta = (np.arange(half, dtype=np.float64) + half) / DQK
    rot = np.zeros((P, 4, T), np.float32)
    for i, sign in enumerate((1.0, -1.0)):
        decay = zeta[:, None] ** (sign * pos[None, :].astype(np.float64) / 512.0)
        cos, sin = np.cos(angles) * decay, np.sin(angles) * decay
        rot[:, 2 * i] = np.concatenate([cos, cos])
        rot[:, 2 * i + 1] = np.concatenate([-sin, sin])
    t = np.arange(T)
    diff = t[None, :] - t[:, None]
    mask = np.zeros((P, H, SC), np.float32)
    for h in range(H):
        gamma = 1.0 - 2.0 ** (-(5 + h))
        d = np.where(diff >= 0, gamma ** np.maximum(diff, 0), 0.0)
        d = d / np.sqrt(np.maximum(d.sum(axis=0, keepdims=True), 1e-6)) * DQK ** -0.5
        mask[:, h, 0:T] = d[0:P]
        mask[P - SECOND:, h, T:] = d[P:, P:]
    heads = np.kron(np.eye(2), np.full((64, 64), 1.0 / 64)).astype(np.float32)
    sel = np.zeros((P, FC * P), np.float32)
    for r in range(HID):
        sel[r // I, r] = sel[LO_ROW + r // I, r] = 0.5
    return {
        "c_ident": np.eye(P, dtype=np.float32), "c_rot": rot, "c_mask": mask, "c_heads": heads, "c_sel": sel,
        "c_tie_g": np.tril(np.ones((G, G), np.float32), -1).reshape(1, -1),
        "c_tie_e": np.tril(np.ones((E, E), np.float32), -1).reshape(1, -1),
    }


def kernel(x, txt, L0_tok_W, L0_tok_b, L0_tok_class_token, L0_tok_pos_embed, L0_attn_Wq, L0_attn_Wk, L0_attn_Wv,
           L0_attn_Wg, L0_attn_Wo, L0_attn_gn_weight, L0_attn_gn_bias, L0_ffn_gate_w, L0_ffn_gate_b, L0_ffn_W1,
           L0_ffn_B1, L0_ffn_W3, L0_ffn_B3, L0_ffn_W2, L0_ffn_B2, L0_ffn_Ws1, L0_ffn_Bs1, L0_ffn_Ws3, L0_ffn_Bs3,
           L0_ffn_Ws2, L0_ffn_Bs2):
    import numpy as np
    import concourse.bacc as bacc
    from concourse import mybir as _mybir
    from concourse.bass_utils import run_bass_kernel_spmd

    def f(v):
        return np.asarray(v)

    def experts(w, ws):
        return np.concatenate([f(w), f(ws)[None]]).transpose(1, 0, 2).reshape(D, HID, 2)

    up1, up3 = experts(L0_ffn_W1, L0_ffn_Ws1), experts(L0_ffn_W3, L0_ffn_Ws3)
    bias1 = np.concatenate([f(L0_ffn_B1), f(L0_ffn_Bs1)[None]]).reshape(HID, 2)
    bias3 = np.concatenate([f(L0_ffn_B3), f(L0_ffn_Bs3)[None]]).reshape(HID, 2)
    cols = [f(L0_attn_Wq), f(L0_attn_Wk), f(L0_attn_Wv), f(L0_attn_Wg), f(L0_ffn_gate_w).T]
    b_13 = np.zeros((P, FC, 4), np.float32)
    for c in range(FC):
        r = slice(c * P, c * P + ffn_rows(c))
        cols += [up1[:, r, 0], up1[:, r, 1], up3[:, r, 0], up3[:, r, 1]]
        b_13[0:ffn_rows(c), c, 0:2] = bias1[r]
        b_13[0:ffn_rows(c), c, 2:4] = bias3[r]
    n = 14
    ps = 16
    patches = f(x).reshape(PAIRS, 2, 3, n, ps, n, ps).transpose(0, 2, 4, 6, 1, 3, 5)
    patches = patches.reshape(PAIRS, PCH, P, 2, PATCHES).transpose(0, 2, 1, 3, 4).reshape(PAIRS, P, PCH * 2, PATCHES)
    ins = {
        "patches": patches,
        "txt": f(txt),
        "w_stack": np.concatenate(cols, axis=1),
        "w_tok": f(L0_tok_W).T.reshape(PCH, P, D).transpose(1, 0, 2),
        "tok_b": f(L0_tok_b).reshape(1, D),
        "cls": f(L0_tok_class_token),
        "pos": f(L0_tok_pos_embed),
        "w_o": f(L0_attn_Wo).reshape(HVC, P, D).transpose(1, 0, 2),
        "gn_wb": np.concatenate([f(L0_attn_gn_weight).reshape(HVC, P).T, f(L0_attn_gn_bias).reshape(HVC, P).T], axis=1),
        "gate_b": f(L0_ffn_gate_b).reshape(1, E),
        "w_2": np.concatenate([f(L0_ffn_W2).reshape(E * I, D), f(L0_ffn_Ws2)]),
        "b_2": np.concatenate([f(L0_ffn_B2), f(L0_ffn_Bs2).reshape(1, D)]),
        "b_13": b_13,
        **_tables(),
    }
    ins = {k: np.ascontiguousarray(v) for k, v in ins.items()}
    nc = bacc.Bacc("TRN2", target_bir_lowering=False, num_devices=1)
    aps = {k: nc.dram_tensor("in_" + k, v.shape, _mybir.dt.from_np(v.dtype), kind="ExternalInput").ap() for k, v in ins.items()}
    aps["out"] = nc.dram_tensor("out", (IMAGES, T, D), F32, kind="ExternalOutput").ap()
    fusion_kernel(nc, aps)
    r = run_bass_kernel_spmd(nc, [{"in_" + k: v for k, v in ins.items()}], core_ids=[0])
    return r.results[0]["out"]
```

```python
from contextlib import ExitStack

import concourse.bass as bass
from concourse import mybir

P = 128
F32 = mybir.dt.float32
F32R = mybir.dt.float32r
ALU = mybir.AluOpType
ACT = mybir.ActivationFunctionType
AX_X = mybir.AxisListType.X

IMAGES = 64
PAIRS = IMAGES // 2
D = 192
DB = D - P
PATCHES = 196
PDIM = 768
PCH = PDIM // P
TXT = 32
T = PATCHES + 1 + TXT
TT = 2 * T
SECOND = T - P
CH = 4
IMG_ROWS1 = P - TXT
H = 6
DQK = 128
DV = 64
HV = H * DV
HVC = HV // P
SC = T + (T - P)
E = 8
G = 4
I = 96
E1 = E + 1
HID = E1 * I
FC = -(-HID // P)
SHARED = HID - (FC - 1) * P
LIMIT = 7.0
ALPHA = 1.702
EPS = 1e-5
BIG = 1e30
LO_ROW = 32
HI_ROW = 64

W_V = 2 * H * DQK
W_G = W_V + HV
W_F = W_G + HV


def ffn_rows(c):
    return P if c > 0 else SHARED


def ffn_first(c):
    return max(0, c * P - (P - SHARED))


WCOLS = W_F + E + 4 * HID
FFC = WCOLS - W_F
PIECES = ([(i * W_F // 2, (i + 1) * W_F // 2) for i in range(2)]
          + [(W_F + i * 1156, min(W_F + (i + 1) * 1156, WCOLS)) for i in range(3)])
PIECE = max(b - a for a, b in PIECES)
ATTN_PIECES = 4


def stage_of(i):
    return i if i < ATTN_PIECES else ATTN_PIECES + (i - ATTN_PIECES) % 3


def loads_of(i):
    return 1 if i < ATTN_PIECES else (i - ATTN_PIECES) // 3 + 1


def up_col(c, part):
    return W_F + 4 * ffn_first(c) + part * ffn_rows(c) + (E if (c, part) > (0, 0) else 0)


EMBEDDING = {"load", "text", "embed", "tokens", "stats_1", "rstd_1", "norm_1", "turn_1", "hi_1", "lo_1"}
EXPERTS = {"route", "pick", "exp", "combine", "comb_hi", "comb_lo", "spread", "weight", "up", "bias", "logit_cols",
           "prod", "clip", "lin", "tanh", "glu", "weigh", "residual", "down", "finish", "store"}


def in_order(table):
    return [tuple(int(x) if x.isdigit() else x for x in word.split(".")) for word in table.split()]


TENSOR = in_order("""
    up.0.0  project.0  project.1  up.0.1  route  project.2  project.3  up.0.2  project.4  project.5  up.0.3
    up.1.0  project.6  up.1.1  up.1.2  project.7  up.1.3  project.8  up.2.0  project.9  project.10  project.11
    up.2.1  project.12  project.13  up.2.2  project.14  project.15  score.0.0  up.2.3  score.0.1  combine
    up.3.0  mix.0.0  mix.0.1  score.1.0  score.1.1  up.3.1  spread.1  mix.1.0  mix.1.1  score.2.0  score.2.1
    up.3.2  mix.2.0  mix.2.1  score.3.0  spread.2  score.3.1  spread.3  up.3.3  mix.3.0  mix.3.1  score.4.0
    score.4.1  up.4.0  mix.4.0  mix.4.1  score.5.0  score.5.1  up.4.1  mix.5.0  mix.5.1  spread.4  up.4.2
    gate_in.0  up.4.3  gate_in.1  head_sums  gate_in.2  up.5.0  spread.5  up.5.1  up.5.2  up.5.3  up.6.0
    embed.0  up.6.1  up.6.2  up.6.3  attn_out.0  attn_out.1  spread.6  embed.1  down.0.0  down.0.1  turn_2
    down.1.0  turn_1  down.1.1
""")
SCALAR = in_order("""
    change.0  logit_cols  change.1  bias.0.0  exp  change.2  bias.0.1  change.3  change.4  bias.1.0  change.5
    change.6  tanh.0  change.7  change.8  bias.1.1  change.9  change.10  change.11  value.0  value.1  bias.2.0
    value.2  bias.2.1  value.3  comb_hi  tanh.1  weight.1  retained.0  bias.3.0  bias.3.1  weight.2  tanh.2
    weight.3  retained.1  retained.2  bias.4.0  weight.4  gate_tanh.0  bias.4.1  tanh.3  gate_tanh.1  tanh.4
    gate_tanh.2  bias.5.0  bias.5.1  weight.5  scale_b.0  scale_b.1  bias.6.0  tanh.5  scale_b.2  bias.6.1
    tanh.6  weight.6  hi_2  hi_1
""")
VECTOR = in_order("""
    cos.0  pick.0  pick.1  sin.0  cos.1  pick.2  pick.3  sin.1  cos.2  pick.4  prod.0.0  pick.5  sin.2
    clip.0.0  cos.3  sin.3  pick.6  cos.4  prod.0.1  pick.7  pick.8  sin.4  pick.9  cos.5  clip.0.1  sin.5
    cos.6  pick.10  lin.0  sin.6  cos.7  pick.11  sin.7  cos.8  prod.1.0  pick.12  sin.8  pick.13  cos.9
    sin.9  cos.10  prod.1.1  cos.11  pick.14  glu.0  pick.15  clip.1.0  pick.16  clip.1.1  pick.17  masked.0.0
    masked.0.1  prod.2.0  lin.1  clip.2.0  prod.2.1  comb_lo  masked.1.0  masked.1.1  glu.1  clip.2.1
    masked.2.0  masked.2.1  row_stats.0  prod.3.0  lin.2  masked.3.0  masked.3.1  sin.10  clip.3.0  sin.11
    glu.2  masked.4.0  masked.4.1  prod.3.1  masked.5.0  masked.5.1  clip.3.1  row_stats.1  lin.3  row_stats.2
    moments.0  moments.1  moments.2  prod.4.0  clip.4.0  gate_mul.0  glu.3  variance.0  prod.4.1  variance.1
    clip.4.1  variance.2  lin.4  variance.3  gate_mul.1  gate_mul.2  glu.4  factors.0  factors.1  factors.2
    scale_a.0  prod.5.0  scale_a.1  clip.5.0  scale_a.2  prod.5.1  clip.5.1  lin.5  glu.5  prod.6.0  prod.6.1
    clip.6.0  add_attn.0  clip.6.1  lin.6  glu.6  add_attn.1  stats_2  tokens  norm_2  stats_1  norm_1  lo_2
    finish.0  lo_1  finish.1
""")
GPSIMD = in_order("""
    by_sin.0  by_sin.1  by_sin.2  by_sin.3  by_sin.4  by_sin.5  by_sin.6  by_sin.7  by_sin.8  by_sin.9
    weigh.1  by_sin.10  by_sin.11  residual  weigh.2  weigh.3  gn_rstd  weigh.4  gated.0  gated.1  gated.2
    weigh.5  weigh.6  rstd_2  rstd_1
""")
SYNC = in_order("""
    load  text  store.0  store.1
""")

ROUND = [step for step in TENSOR if step[0] in ("up", "route", "combine", "spread")]


def bank_of(*item):
    return ROUND.index(item) % 4


def row_col(c):
    return (c // 2) * T + (c % 2) * SECOND


def fusion_kernel(nc, a):
    ctx = ExitStack()
    with ctx:
        def sb(name, shape, dt=F32):
            return ctx.enter_context(nc.sbuf_tensor(name, shape, dt))

        def sem(name):
            return ctx.enter_context(nc.semaphore(name))

        wA_hi = sb("wA_hi", [P, WCOLS], F32R)
        wA_lo = sb("wA_lo", [P, WCOLS], F32R)
        wB_hi = sb("wB_hi", [P, WCOLS], F32R)
        wB_lo = sb("wB_lo", [P, FFC], F32R)
        w_tok = sb("w_tok", [P, PCH, D])
        w_o = sb("w_o", [P, HVC, D])
        w_2 = sb("w_2", [P, FC, D])
        b_13 = sb("b_13", [P, FC, 4])
        ident = sb("ident", [P, P])
        heads64 = sb("heads64", [P, P])
        rot_tab = sb("rot_tab", [P, 4, T])
        mask = sb("mask", [P, H, SC])
        sel = sb("sel", [P, FC - 1, P], F32R)
        tie_g = sb("tie_g", [P, G * G])
        tie_e = sb("tie_e", [P, E * E])
        embed = sb("embed", [P, 2, D])
        b_2 = sb("b_2", [HI_ROW + E1, D], F32R)
        gate_b = sb("gate_b", [P, E])
        gn_w = sb("gn_w", [P, HVC])
        gn_b = sb("gn_b", [P, HVC])
        neg_half = sb("neg_half", [P, 2 * H])
        zeros = sb("zeros", [P, 1, 1])

        patch = sb("patch", [P, PCH * 2, 1 + PATCHES])
        hid = sb("hid", [P, CH, D])
        normed = sb("normed", [P, CH, D])
        hid2 = sb("hid2", [P, CH, D])
        outp = sb("outp", [P, CH, D])
        bn1 = sb("bn1", [P, CH, 6])
        mv1 = sb("mv1", [P, CH, 2])
        rstd1 = sb("rstd1", [P, CH])
        bn2 = sb("bn2", [P, CH, 6])
        mv2 = sb("mv2", [P, CH, 2])
        rstd2 = sb("rstd2", [P, CH])
        x1A_hi = sb("x1A_hi", [P, TT], F32R)
        x1A_lo = sb("x1A_lo", [P, TT], F32R)
        x1B = sb("x1B", [P, TT], F32R)
        x1B_z = sb("x1B_z", [P, TT], F32R)
        x2A_hi = sb("x2A_hi", [P, TT], F32R)
        x2A_lo = sb("x2A_lo", [P, TT], F32R)
        x2B = sb("x2B", [P, TT], F32R)
        x2B_z = sb("x2B_z", [P, TT], F32R)
        swap = sb("swap", [P, 2, TT])
        qk = sb("qk", [P, 2 * H, TT])
        val = sb("val", [P, CH, HV])
        prob = sb("prob", [P, 2, SC])
        rbn = sb("rbn", [P, 2 * HVC, 6])
        rmv = sb("rmv", [P, 2 * HVC, 2])
        gn = sb("gn", [P, 8, 2 * HVC])
        lg = sb("lg", [P, 5, CH * E])
        few = sb("few", [P, 6, CH * G])
        cmp = prob[:, :, :].rearrange("p b s -> p (b s)")[:, 0:2 * CH * E * E]
        comb = sb("comb", [P, CH, E1])
        combR = sb("combR", [HI_ROW + E1, TT], F32R)
        gT = sb("gT", [P, FC, TT])
        glu = sb("glu", [P, 2, 2, TT])
        th = sb("th", [P, TT])
        qk_flat = qk[:, :, :].rearrange("p c t -> p (c t)")
        gT_flat = gT[:, :, :].rearrange("p c t -> p (c t)")
        glu_flat = glu[:, :, :, :].rearrange("p a b t -> p (a b t)")
        stage = ([qk_flat[:, i * PIECE:(i + 1) * PIECE] for i in range(ATTN_PIECES)]
                 + [gT_flat[:, 0:PIECE], gT_flat[:, PIECE:2 * PIECE], glu_flat[:, 0:PIECE]])
        sel_in = gT_flat[:, 2 * PIECE:2 * PIECE + (FC - 1) * P]
        b_2f = glu_flat[0:HI_ROW + E1, PIECE:PIECE + D]
        GN_IN, GN_MEAN, GN_SQ, GN_RSTD, GN_SCALE, GN_T, GN_SHIFT = range(7)

        def ret(c):
            return qk[:, 4 * c, :]

        def gate(c):
            return qk[:, 4 * c + 1, :]

        psA = ctx.enter_context(nc.psum_tensor("psA", [P, 4, 512], F32))
        psF = ctx.enter_context(nc.psum_tensor("psF", [P, 4, 512], F32))

        s_wtok = sem("s_wtok")
        s_tok_const = sem("s_tok_const")
        s_attn_const = sem("s_attn_const")
        s_ffn_const = sem("s_ffn_const")
        s_stage = [sem("s_stage%d" % i) for i in range(ATTN_PIECES + 3)]
        s_whi = sem("s_whi")
        s_wlo = sem("s_wlo")
        s_zero = sem("s_zero")
        s_set = sem("s_set")
        s_sel = sem("s_sel")
        s_patch = sem("s_patch")
        s_txt = sem("s_txt")
        s_tok = sem("s_tok")
        s_hid = sem("s_hid")
        s_ln1 = sem("s_ln1")
        s_rstd1 = sem("s_rstd1")
        s_norm1 = sem("s_norm1")
        s_x1T = sem("s_x1T")
        s_x1hi = sem("s_x1hi")
        s_x1lo = sem("s_x1lo")
        s_proj = sem("s_proj")
        s_swap = sem("s_swap")
        s_cos = sem("s_cos")
        s_sin = sem("s_sin")
        s_rot = sem("s_rot")
        s_val = sem("s_val")
        s_gproj = sem("s_gproj")
        s_tanh = sem("s_tanh")
        s_gate = sem("s_gate")
        s_score = sem("s_score")
        s_prob = sem("s_prob")
        s_pv = sem("s_pv")
        s_ret = sem("s_ret")
        s_gn = sem("s_gn")
        s_gnsum = sem("s_gnsum")
        s_gnrstd = sem("s_gnrstd")
        s_scaled = sem("s_scaled")
        s_scaled_b = sem("s_scaled_b")
        s_gated = sem("s_gated")
        s_wo = sem("s_wo")
        s_hid2 = sem("s_hid2")
        s_res = sem("s_res")
        s_ln2 = sem("s_ln2")
        s_rstd2 = sem("s_rstd2")
        s_norm2 = sem("s_norm2")
        s_x2T = sem("s_x2T")
        s_x2hi = sem("s_x2hi")
        s_x2lo = sem("s_x2lo")
        s_lgcol = sem("s_lgcol")
        s_lgrow = sem("s_lgrow")
        s_top = sem("s_top")
        s_exp = sem("s_exp")
        s_combT = sem("s_combT")
        s_combhi = sem("s_combhi")
        s_comblo = sem("s_comblo")
        s_spread = sem("s_spread")
        s_weight = sem("s_weight")
        s_up = sem("s_up")
        s_up1 = sem("s_up1")
        s_prod = sem("s_prod")
        s_clip = sem("s_clip")
        s_lin = sem("s_lin")
        s_sig = sem("s_sig")
        s_glu = sem("s_glu")
        s_exout = sem("s_exout")
        s_down = sem("s_down")
        s_out = sem("s_out")
        s_store = sem("s_store")

        QKV = 2 * H + CH
        LN_OPS = 2 * CH + 1
        GN_OPS = 16
        TOP_OPS = 18
        TOK_CONSTS, ATTN_CONSTS, FFN_CONSTS = 6, 5, 10
        SET_B2 = 1
        SET_TOK = 7
        SET_ATTN = 9
        SET_ALL = 11

        def nth(per_pair, p, k):
            return per_pair * p + (k + 1)

        def later(p):
            return not isinstance(p, int) or p > 0

        def program(eng, order, steps, before_attention, before_experts):
            def turn(p):
                for name, *args in order:
                    if name in EXPERTS:
                        if later(p):
                            steps[name](p - 1, *args)
                    elif name in EMBEDDING:
                        if not isinstance(p, int) or p < PAIRS - 1:
                            steps[name](p + 1, *args)
                    else:
                        steps[name](p, *args)

            for name, *args in order:
                if name in EMBEDDING:
                    steps[name](0, *args)
            before_attention()
            turn(0)
            before_experts()
            turn(1)
            with eng.Fori(2, PAIRS - 1) as p:
                turn(p)
            turn(PAIRS - 1)
            for name, *args in order:
                if name in EXPERTS:
                    steps[name](PAIRS - 1, *args)

        block = ctx.enter_context(nc.Block())

        @block.sync
        def _(sp):
            def const(s_loaded, dst, src):
                sp.dma_start(dst, src).then_inc(s_loaded, 16)

            def load_piece(i):
                lo, hi = PIECES[i // 2]
                st = stage[stage_of(i)][:, 0:hi - lo]
                if loads_of(i) > 1:
                    sp.wait_ge(s_wlo, i - 2)
                if i % 2 == 0:
                    sp.dma_start(st, a["w_stack"][0:P, lo:hi]).then_inc(s_stage[stage_of(i)], 16)
                else:
                    sp.dma_start(st[0:DB, :], a["w_stack"][P:D, lo:hi]).then_inc(s_stage[stage_of(i)], 16)
                    sp.dma_start(st[DB:P, :], a["w_stack"][P:D, lo:hi]).then_inc(s_stage[stage_of(i)], 16)

            load_piece(0)
            load_piece(1)
            sp.dma_start(w_tok[:, :, :], a["w_tok"]).then_inc(s_wtok, 16)

            def before_attention():
                const(s_tok_const, embed[:, 0, :], a["pos"][0:P, :])
                const(s_tok_const, embed[0:IMG_ROWS1, 1, :], a["pos"][SECOND:SECOND + IMG_ROWS1, :])
                const(s_tok_const, hid[0:1, 0, :], a["cls"])
                const(s_tok_const, hid[1:P, 0, :], a["tok_b"].to_broadcast([P - 1, D]))
                const(s_tok_const, hid[0:IMG_ROWS1, 1, :], a["tok_b"].to_broadcast([IMG_ROWS1, D]))
                const(s_tok_const, ident[:, :], a["c_ident"])

                for i in range(2, ATTN_PIECES + 3):
                    load_piece(i)
                const(s_attn_const, gn[:, GN_IN, :], a["gn_wb"])
                const(s_attn_const, rot_tab[:, :, :], a["c_rot"])
                for i in range(ATTN_PIECES + 3, 2 * len(PIECES)):
                    load_piece(i)
                const(s_attn_const, mask[:, :, :], a["c_mask"])
                const(s_attn_const, heads64[:, :], a["c_heads"])
                const(s_attn_const, w_o[:, :, :], a["w_o"])
                sp.wait_ge(s_set, SET_B2)
                for row in (0, LO_ROW, HI_ROW):
                    const(s_ffn_const, b_2f[row:row + E1, :], a["b_2"])
                const(s_ffn_const, b_13[:, :, :], a["b_13"])
                const(s_ffn_const, sel_in, a["c_sel"])
                const(s_ffn_const, tie_g[:, :], a["c_tie_g"].to_broadcast([P, G * G]))
                const(s_ffn_const, tie_e[:, :], a["c_tie_e"].to_broadcast([P, E * E]))
                const(s_ffn_const, gate_b[:, :], a["gate_b"].to_broadcast([P, E]))
                const(s_ffn_const, w_2[0:SHARED, 0, :], a["w_2"][0:SHARED, :])
                const(s_ffn_const, w_2[:, 1:FC, :], a["w_2"][SHARED:HID, :].rearrange("(c p) d -> p c d", p=P))

            def before_experts():
                pass

            def load(p):
                if later(p):
                    sp.wait_ge(s_tok, nth(1, p, -1))
                else:
                    sp.wait_ge(s_zero, 1)
                sp.dma_start(patch[:, :, 1:1 + PATCHES], a["patches"][bass.ds(p, 1), :, :, :].rearrange(
                    "a p c t -> (a p) c t")).then_inc(s_patch, 16)

            def text(p):
                if later(p):
                    sp.wait_ge(s_hid2, nth(2, p, -1))
                for b in range(2):
                    sp.dma_start(hid[IMG_ROWS1:P, 2 * b + 1, :], a["txt"][bass.ds(p * 2 + b, 1), :, :].rearrange(
                        "b t d -> (b t) d")).then_inc(s_txt, 16)

            def store(p, b):
                sp.wait_ge(s_out, nth(2, p, b))
                img = a["out"][bass.ds(p * 2 + b, 1), :, :].rearrange("a t d -> (a t) d")
                sp.dma_start(img[0:P, :], outp[:, 2 * b, :]).then_inc(s_store, 16)
                sp.dma_start(img[P:T, :], outp[P - SECOND:P, 2 * b + 1, :]).then_inc(s_store, 16)

            program(sp, SYNC, {"load": load, "text": text, "store": store}, before_attention, before_experts)
            sp.wait_ge(s_store, 64 * PAIRS)

        @block.gpsimd
        def _(pool):
            nc.gpsimd.memset(patch[:, :, 0:1], 0.0).then_inc(s_zero, 1)
            nc.gpsimd.memset(comb[:, :, E:E1], 1.0).then_inc(s_zero, 1)
            nc.gpsimd.memset(neg_half[:, :], -0.5).then_inc(s_zero, 1)
            nc.gpsimd.memset(zeros[:, :, :], 0.0).then_inc(s_zero, 1)
            pool.wait_ge(s_zero, 4)

            def before_attention():
                pool.wait_ge(s_attn_const, 16 * ATTN_CONSTS)

            def before_experts():
                pass

            def rstd_1(p):
                pool.wait_ge(s_ln1, nth(LN_OPS, p, LN_OPS - 1))
                nc.gpsimd.tensor_tensor(rstd1[:, :], rstd1[:, :], neg_half[:, 0:CH], ALU.pow).then_inc(s_rstd1, 1)

            def by_sin(p, n):
                pool.wait_ge(s_swap, 2 * nth(2 * H, p, n))
                s = swap[:, n % 2, :].rearrange("p (b t) -> p b t", b=2)
                k = 2 * (n % 2) + 1
                nc.gpsimd.tensor_tensor(s, s, rot_tab[:, k:k + 1, :].to_broadcast([P, 2, T]),
                                        ALU.mult).then_inc(s_sin, 1)

            def gn_rstd(p):
                pool.wait_ge(s_gn, nth(GN_OPS, p, 12))
                nc.gpsimd.tensor_tensor(gn[:, GN_RSTD, :], gn[:, GN_RSTD, :], neg_half[:, 0:2 * HVC],
                                        ALU.pow).then_inc(s_gnrstd, 1)

            def gated(p, c):
                pool.wait_ge(s_scaled, nth(HVC, p, c))
                pool.wait_ge(s_scaled_b, nth(HVC, p, c))
                pool.wait_ge(s_gate, nth(HVC, p, c))
                nc.gpsimd.tensor_tensor(ret(c), ret(c), gate(c), ALU.mult).then_inc(s_gated, 1)

            def rstd_2(p):
                pool.wait_ge(s_ln2, nth(LN_OPS, p, LN_OPS - 1))
                nc.gpsimd.tensor_tensor(rstd2[:, :], rstd2[:, :], neg_half[:, 0:CH], ALU.pow).then_inc(s_rstd2, 1)

            def residual(p):
                if later(p):
                    pool.wait_ge(s_store, 64 * nth(1, p, -1))
                nc.gpsimd.tensor_tensor(outp[:, :, :], hid2[:, :, :], zeros[:, :, :].to_broadcast([P, CH, D]),
                                        ALU.add).then_inc(s_res, 1)

            def weigh(p, c):
                r = ffn_rows(c)
                pool.wait_ge(s_glu, nth(FC, p, c))
                pool.wait_ge(s_weight, nth(FC - 1, p, c - 1))
                nc.gpsimd.tensor_tensor(gT[0:r, c, :], gT[0:r, c, :], glu[0:r, c % 2, 1, :],
                                        ALU.mult).then_inc(s_exout, 1)

            program(pool, GPSIMD, {"rstd_1": rstd_1, "by_sin": by_sin, "gn_rstd": gn_rstd, "gated": gated,
                                   "rstd_2": rstd_2, "residual": residual, "weigh": weigh},
                    before_attention, before_experts)

        @block.scalar
        def _(act):
            def split_piece(i):
                lo, hi = PIECES[i // 2]
                dst = (wA_hi if i % 2 == 0 else wB_hi)[:, lo:hi]
                transfers = 3 if loads_of(i) == 2 else 1 + i % 2
                act.wait_ge(s_stage[stage_of(i)], 16 * transfers)
                nc.scalar.activation(dst, stage[stage_of(i)][:, 0:hi - lo], ACT.Copy).then_inc(s_whi, 1)

            for i in range(ATTN_PIECES + 3):
                split_piece(i)

            def before_attention():
                for i in range(ATTN_PIECES + 3, 2 * len(PIECES)):
                    split_piece(i)
                act.wait_ge(s_wlo, ATTN_PIECES)

            def before_experts():
                act.wait_ge(s_ffn_const, 16 * FFN_CONSTS)
                act.wait_ge(s_set, SET_B2)
                nc.scalar.activation(b_2[:, :], b_2f, ACT.Copy).then_inc(s_sel, 1)
                nc.scalar.activation(sel[:, :, :].rearrange("p c r -> p (c r)"), sel_in, ACT.Copy).then_inc(s_sel, 1)
                act.wait_ge(s_sel, 2)
                act.wait_ge(s_wlo, 2 * len(PIECES))
                act.wait_ge(s_set, SET_ALL)

            def hi_1(p):
                act.wait_ge(s_x1T, nth(2, p, 0))
                if later(p):
                    act.wait_ge(s_gproj, nth(HVC, p, -1))
                nc.scalar.activation(x1A_hi[:, :], psA[:, 2, 0:TT], ACT.Copy).then_inc(s_x1hi, 1)
                act.wait_ge(s_x1T, nth(2, p, 1))
                nc.scalar.activation(x1B[0:DB, :], psA[0:DB, 3, 0:TT], ACT.Copy).then_inc(s_x1hi, 1)
                nc.scalar.activation(x1B_z[0:DB, :], psA[0:DB, 3, 0:TT], ACT.Copy).then_inc(s_x1hi, 1)

            def change(p, n):
                bank = psA[:, n % 4, :]
                act.wait_ge(s_proj, nth(QKV, p, n))
                if n >= 2 or later(p):
                    act.wait_ge(s_rot, nth(2 * H, p, n - 2))
                nc.scalar.activation(swap[0:64, n % 2, :], bank[64:P, 0:TT], ACT.Copy).then_inc(s_swap, 1)
                nc.scalar.activation(swap[64:P, n % 2, :], bank[0:64, 0:TT], ACT.Copy).then_inc(s_swap, 1)

            def value(p, c):
                act.wait_ge(s_proj, nth(QKV, p, 2 * H + c))
                if c == 0 and later(p):
                    act.wait_ge(s_pv, nth(2 * H, p, -1))
                nc.scalar.activation(val[:, c, :], psA[:, c, 0:HV], ACT.Copy).then_inc(s_val, 1)

            def retained(p, c):
                act.wait_ge(s_pv, nth(2 * H, p, 4 * c + 3))
                nc.scalar.activation(ret(c), psA[:, 3 - c % 2, 0:TT], ACT.Copy).then_inc(s_ret, 1)

            def gate_tanh(p, c):
                act.wait_ge(s_gproj, nth(HVC, p, c))
                nc.scalar.activation(gate(c), psA[:, c, 0:TT], ACT.Tanh, scale=0.5).then_inc(s_tanh, 1)

            def scale_b(p, c):
                if c == 0:
                    act.wait_ge(s_gn, nth(GN_OPS, p, GN_OPS - 1))
                x = ret(c)[:, T:TT]
                i = 2 * c + 1
                nc.scalar.activation(x, x, ACT.Identity, bias=gn[:, GN_SHIFT, i:i + 1],
                                     scale=gn[:, GN_SCALE, i:i + 1]).then_inc(s_scaled_b, 1)

            def hi_2(p):
                act.wait_ge(s_x2T, nth(2, p, 0))
                if later(p):
                    act.wait_ge(s_up, nth(4 * FC, p, -1))
                nc.scalar.activation(x2A_hi[:, :], psF[:, 2, 0:TT], ACT.Copy).then_inc(s_x2hi, 1)
                act.wait_ge(s_x2T, nth(2, p, 1))
                nc.scalar.activation(x2B[0:DB, :], psF[0:DB, 3, 0:TT], ACT.Copy).then_inc(s_x2hi, 1)
                nc.scalar.activation(x2B_z[DB:P, :], psF[0:DB, 3, 0:TT], ACT.Copy).then_inc(s_x2hi, 1)

            def logit_cols(p):
                act.wait_ge(s_up, nth(4 * FC, p, 0))
                if later(p):
                    act.wait_ge(s_glu, nth(FC, p, -1))
                nc.scalar.activation(th[SHARED:SHARED + E, :], psF[SHARED:SHARED + E, bank_of("up", 0, 0), 0:TT],
                                     ACT.Copy).then_inc(s_lgcol, 1)

            def exp(p):
                act.wait_ge(s_top, nth(TOP_OPS, p, 1))
                nc.scalar.activation(lg[:, 1, :], lg[:, 0, :], ACT.Exp).then_inc(s_exp, 1)

            def comb_hi(p):
                act.wait_ge(s_combT, nth(1, p, 0))
                if later(p):
                    act.wait_ge(s_down, nth(2, p, -1))
                for row in (0, HI_ROW):
                    nc.scalar.activation(combR[row:row + E1, :], psF[0:E1, bank_of("combine"), 0:TT],
                                         ACT.Copy).then_inc(s_combhi, 1)

            def weight(p, c):
                act.wait_ge(s_spread, nth(FC - 1, p, c - 1))
                nc.scalar.activation(gT[:, c, :], psF[:, bank_of("spread", c), 0:TT], ACT.Copy).then_inc(s_weight, 1)

            def bias(p, c, part):
                r = ffn_rows(c)
                if part == 0:
                    if c == 2:
                        act.wait_ge(s_glu, nth(FC, p, 0))
                    elif c > 2 or (c == 0 and later(p)):
                        act.wait_ge(s_exout, nth(FC - 1, p, max(c - 3, -1)))
                act.wait_ge(s_up, nth(4 * FC, p, 4 * c + part))
                nc.scalar.activation(glu[0:r, c % 2, part, :], psF[0:r, bank_of("up", c, part), 0:TT], ACT.Identity,
                                     bias=b_13[0:r, c, part:part + 1]).then_inc(s_up1, 1)

            def tanh(p, c):
                r = ffn_rows(c)
                if c == 1:
                    act.wait_ge(s_lgrow, nth(1, p, 0))
                act.wait_ge(s_clip, nth(2 * FC, p, 2 * c))
                if c >= 1 or later(p):
                    act.wait_ge(s_glu, nth(FC, p, c - 1))
                nc.scalar.activation(th[0:r, :], glu[0:r, c % 2, 0, :], ACT.Tanh, scale=ALPHA / 2).then_inc(s_sig, 1)

            program(act, SCALAR, {"hi_1": hi_1, "change": change, "value": value, "retained": retained,
                                  "gate_tanh": gate_tanh, "scale_b": scale_b, "hi_2": hi_2, "logit_cols": logit_cols,
                                  "exp": exp, "comb_hi": comb_hi, "weight": weight, "bias": bias, "tanh": tanh},
                    before_attention, before_experts)

        @block.vector
        def _(dve):
            nc.vector.memset(b_2f, 0.0).then_inc(s_set, 1)
            for rows in (combR[:, :], x1B_z[DB:P, :], x2B_z[0:DB, :], wB_lo[0:DB, W_F:FFC]):
                nc.vector.memset(rows.bitcast(mybir.dt.uint32), 0).then_inc(s_set, 1)
            def split_piece(i):
                lo, hi = PIECES[i // 2]
                st = stage[stage_of(i)][:, 0:hi - lo]
                dve.wait_ge(s_whi, i + 1)
                if i % 2 == 0:
                    nc.vector.tensor_tensor(wA_lo[:, lo:hi], st, wA_hi[:, lo:hi].bitcast(F32),
                                            ALU.subtract).then_inc(s_wlo, 1)
                else:
                    r, off = (0, 0) if hi <= W_F else (DB, W_F)
                    nc.vector.tensor_tensor(wB_lo[r:r + DB, lo - off:hi - off], st[r:r + DB, :],
                                            wB_hi[r:r + DB, lo:hi].bitcast(F32), ALU.subtract).then_inc(s_wlo, 1)

            split_piece(0)
            split_piece(1)
            dve.wait_ge(s_tok_const, 16 * TOK_CONSTS)
            nc.vector.tensor_tensor(embed[:, 0, :], embed[:, 0, :], hid[:, 0, :], ALU.add).then_inc(s_set, 1)
            nc.vector.tensor_tensor(embed[0:IMG_ROWS1, 1, :], embed[0:IMG_ROWS1, 1, :], hid[0:IMG_ROWS1, 1, :],
                                    ALU.add).then_inc(s_set, 1)
            for i in range(2, ATTN_PIECES + 3):
                split_piece(i)
            dve.wait_ge(s_set, SET_TOK)

            def before_attention():
                for i in range(ATTN_PIECES + 3, 2 * len(PIECES)):
                    split_piece(i)
                dve.wait_ge(s_attn_const, 16 * ATTN_CONSTS)
                nc.vector.tensor_scalar(gn_w[:, :], gn[:, GN_IN, 0:HVC], 0.5, None, ALU.mult).then_inc(s_set, 1)
                nc.vector.tensor_scalar(gn_b[:, :], gn[:, GN_IN, HVC:2 * HVC], 0.5, None, ALU.mult).then_inc(s_set, 1)
                dve.wait_ge(s_wlo, 2 * len(PIECES))
                dve.wait_ge(s_set, SET_ATTN)

            def before_experts():
                dve.wait_ge(s_ffn_const, 16 * FFN_CONSTS)
                nc.vector.tensor_scalar(w_2[0:SHARED, 0, :], w_2[0:SHARED, 0, :], 0.5, None, ALU.mult).then_inc(s_set, 1)
                dve.wait_ge(s_sel, 1)
                lows = slice(HI_ROW, HI_ROW + E1)
                nc.vector.tensor_tensor(b_2[lows, :], b_2f[lows, :], b_2[lows, :].bitcast(F32),
                                        ALU.subtract).then_inc(s_set, 1)
                dve.wait_ge(s_set, SET_ALL)

            hid4 = hid[:, :, :].rearrange("p (b k) d -> p b k d", k=2)

            def tokens(p):
                dve.wait_ge(s_tok, nth(1, p, 0))
                if later(p):
                    dve.wait_ge(s_hid2, nth(2, p, -1))
                nc.vector.tensor_tensor(hid4[:, :, 0, :], psA[:, 2:4, 0:D],
                                        embed[:, 0:1, :].to_broadcast([P, 2, D]), ALU.add).then_inc(s_hid, 1)
                nc.vector.tensor_tensor(hid4[0:IMG_ROWS1, :, 1, :], psA[0:IMG_ROWS1, 2:4, D:2 * D],
                                        embed[0:IMG_ROWS1, 1:2, :].to_broadcast([IMG_ROWS1, 2, D]),
                                        ALU.add).then_inc(s_hid, 1)

            def norm_stats(p, src, bn, mv, rstd, s_stat):
                for c in range(CH):
                    nc.vector.bn_stats(bn[:, c, :], src[:, c, :]).then_inc(s_stat, 1)
                dve.wait_ge(s_stat, nth(LN_OPS, p, CH - 1))
                nc.vector.memset(rstd[:, :], EPS)
                for c in range(CH):
                    nc.vector.bn_aggr(mv[:, c, :], bn[:, c, :]).then_inc(s_stat, 1)
                dve.wait_ge(s_stat, nth(LN_OPS, p, 2 * CH - 1))
                nc.vector.tensor_tensor(rstd[:, :], mv[:, :, 1], rstd[:, :], ALU.add).then_inc(s_stat, 1)

            def normalise(p, src, mv, rstd, s_rstd, s_done):
                dve.wait_ge(s_rstd, nth(1, p, 0))
                for c in range(CH):
                    nc.vector.tensor_scalar(normed[:, c, :], src[:, c, :], mv[:, c, 0:1], rstd[:, c:c + 1],
                                            ALU.subtract, ALU.mult).then_inc(s_done, 1)

            def stats_1(p):
                dve.wait_ge(s_hid, nth(2, p, 1))
                dve.wait_ge(s_txt, 32 * nth(1, p, 0))
                norm_stats(p, hid, bn1, mv1, rstd1, s_ln1)

            def norm_1(p):
                if later(p):
                    dve.wait_ge(s_x2T, nth(2, p, -1))
                normalise(p, hid, mv1, rstd1, s_rstd1, s_norm1)

            def stats_2(p):
                dve.wait_ge(s_hid2, nth(2, p, 1))
                norm_stats(p, hid2, bn2, mv2, rstd2, s_ln2)

            def norm_2(p):
                dve.wait_ge(s_x1T, nth(2, p, 1))
                normalise(p, hid2, mv2, rstd2, s_rstd2, s_norm2)

            def lo_1(p):
                dve.wait_ge(s_x1hi, nth(3, p, 0))
                nc.vector.tensor_tensor(x1A_lo[:, :], psA[:, 2, 0:TT], x1A_hi[:, :].bitcast(F32),
                                        ALU.subtract).then_inc(s_x1lo, 1)
                dve.wait_ge(s_x1hi, nth(3, p, 2))
                nc.vector.tensor_tensor(x1B[DB:P, :], psA[0:DB, 3, 0:TT], x1B[0:DB, :].bitcast(F32),
                                        ALU.subtract).then_inc(s_x1lo, 1)

            def lo_2(p):
                dve.wait_ge(s_x2hi, nth(3, p, 0))
                nc.vector.tensor_tensor(x2A_lo[:, :], psF[:, 2, 0:TT], x2A_hi[:, :].bitcast(F32),
                                        ALU.subtract).then_inc(s_x2lo, 1)
                dve.wait_ge(s_x2hi, nth(3, p, 2))
                nc.vector.tensor_tensor(x2B[DB:P, :], psF[0:DB, 3, 0:TT], x2B[0:DB, :].bitcast(F32),
                                        ALU.subtract).then_inc(s_x2lo, 1)

            def cos(p, n):
                dve.wait_ge(s_swap, 2 * nth(2 * H, p, n))
                if n == 0 and later(p):
                    dve.wait_ge(s_wo, nth(2, p, -1))
                k = 2 * (n % 2)
                nc.vector.tensor_tensor(qk[:, n, :].rearrange("p (b t) -> p b t", b=2),
                                        psA[:, n % 4, 0:TT].rearrange("p (b t) -> p b t", b=2),
                                        rot_tab[:, k:k + 1, :].to_broadcast([P, 2, T]), ALU.mult).then_inc(s_cos, 1)

            def sin(p, n):
                dve.wait_ge(s_cos, nth(2 * H, p, n))
                dve.wait_ge(s_sin, nth(2 * H, p, n))
                nc.vector.tensor_tensor(qk[:, n, :], qk[:, n, :], swap[:, n % 2, :], ALU.add).then_inc(s_rot, 1)

            def masked(p, h, b):
                n = 2 * h + b
                dve.wait_ge(s_score, nth(2 * H, p, n))
                if h > 0 or later(p):
                    dve.wait_ge(s_pv, nth(2 * H, p, n - 2))
                nc.vector.tensor_tensor(prob[:, b, :], psA[:, b, 0:SC], mask[:, h, :], ALU.mult).then_inc(s_prob, 1)

            def row_stats(p, c):
                dve.wait_ge(s_ret, nth(HVC, p, c))
                for b in range(2):
                    nc.vector.bn_stats(rbn[:, 2 * c + b, :], ret(c)[:, b * T:(b + 1) * T]).then_inc(s_gn, 1)

            def moments(p, k):
                dve.wait_ge(s_gn, nth(GN_OPS, p, 2 * HVC + k - 1))
                if k == 0:
                    nc.vector.memset(gn[:, GN_RSTD, :], EPS)
                    for i in range(2 * HVC):
                        ins = nc.vector.bn_aggr(rmv[:, i, :], rbn[:, i, :])
                elif k == 1:
                    ins = nc.vector.tensor_tensor(gn[:, GN_T, :], rmv[:, :, 0], rmv[:, :, 0], ALU.mult)
                else:
                    ins = nc.vector.tensor_tensor(rmv[:, :, 1], rmv[:, :, 1], gn[:, GN_T, :], ALU.add)
                ins.then_inc(s_gn, 1)

            def variance(p, k):
                dve.wait_ge(s_gn, nth(GN_OPS, p, 2 * HVC + 3 + k - 1))
                if k == 0:
                    dve.wait_ge(s_gnsum, nth(1, p, 0))
                    ins = nc.vector.tensor_copy(gn[:, GN_MEAN:GN_SQ + 1, :],
                                                psA[:, 3, 0:4 * HVC].rearrange("p (i s) -> p s i", s=2))
                elif k == 1:
                    ins = nc.vector.tensor_tensor(gn[:, GN_T, :], gn[:, GN_MEAN, :], gn[:, GN_MEAN, :], ALU.mult)
                elif k == 2:
                    ins = nc.vector.tensor_tensor(gn[:, GN_SQ, :], gn[:, GN_SQ, :], gn[:, GN_T, :], ALU.subtract)
                else:
                    ins = nc.vector.tensor_tensor(gn[:, GN_RSTD, :], gn[:, GN_SQ, :], gn[:, GN_RSTD, :], ALU.add)
                ins.then_inc(s_gn, 1)

            def gate_mul(p, c):
                dve.wait_ge(s_tanh, nth(HVC, p, c))
                nc.vector.scalar_tensor_tensor(gate(c), gate(c), 1.0, psA[:, c, 0:TT],
                                               ALU.add, ALU.mult).then_inc(s_gate, 1)

            def factors(p, k):
                def by_chunk(row):
                    return gn[:, row, :].rearrange("p (c b) -> p c b", b=2)

                dve.wait_ge(s_gn, nth(GN_OPS, p, 13 + k - 1))
                if k == 0:
                    dve.wait_ge(s_gnrstd, nth(1, p, 0))
                    ins = nc.vector.tensor_tensor(by_chunk(GN_SCALE), by_chunk(GN_RSTD),
                                                  gn_w[:, :, None].to_broadcast([P, HVC, 2]), ALU.mult)
                elif k == 1:
                    ins = nc.vector.tensor_tensor(gn[:, GN_T, :], gn[:, GN_MEAN, :], gn[:, GN_SCALE, :], ALU.mult)
                else:
                    ins = nc.vector.tensor_tensor(by_chunk(GN_SHIFT), gn_b[:, :, None].to_broadcast([P, HVC, 2]),
                                                  by_chunk(GN_T), ALU.subtract)
                ins.then_inc(s_gn, 1)

            def scale_a(p, c):
                if c == 0:
                    dve.wait_ge(s_gn, nth(GN_OPS, p, GN_OPS - 1))
                x = ret(c)[:, 0:T]
                nc.vector.tensor_scalar(x, x, gn[:, GN_SCALE, 2 * c:2 * c + 1], gn[:, GN_SHIFT, 2 * c:2 * c + 1],
                                        ALU.mult, ALU.add).then_inc(s_scaled, 1)

            def add_attn(p, b):
                dve.wait_ge(s_wo, nth(2, p, b))
                if b == 0 and later(p):
                    dve.wait_ge(s_res, nth(1, p, -1))
                nc.vector.tensor_tensor(hid2[:, 2 * b:2 * b + 2, :],
                                        psA[:, b, 0:2 * D].rearrange("p (k d) -> p k d", k=2),
                                        hid[:, 2 * b:2 * b + 2, :], ALU.add).then_inc(s_hid2, 1)

            def by_row(x, n):
                return x.rearrange("p (c n) -> p c n", n=n)

            def rank(values, n, ties, out, k):
                v = by_row(values, n)
                other = v[:, :, None, :].to_broadcast([P, CH, n, n])
                own = v[:, :, :, None].to_broadcast([P, CH, n, n])
                both = cmp[:, 0:2 * CH * n * n].rearrange("p (c i two j) -> p c i two j", i=n, two=2, j=n)
                if k == 0:
                    return nc.vector.tensor_tensor(both[:, :, :, 0, :], other, own, ALU.is_gt)
                if k == 1:
                    return nc.vector.tensor_tensor(both[:, :, :, 1, :], other, own, ALU.is_equal)
                if k == 2:
                    return nc.vector.tensor_tensor(both[:, :, :, 1, :], both[:, :, :, 1, :],
                                                   ties.rearrange("p (i j) -> p i j", j=n)[:, None, :, :].to_broadcast(
                                                       [P, CH, n, n]), ALU.mult)
                return nc.vector.reduce_sum(out, cmp[:, 0:2 * CH * n * n].rearrange("p (i m) -> p i m", m=2 * n), axis=AX_X)

            def pick(p, k):
                logits = psF[:, bank_of("route"), 0:CH * E]
                two = lg[:, 3, :].rearrange("p (m two) -> p m two", two=2)
                if k == 0:
                    dve.wait_ge(s_lgrow, nth(1, p, 0))
                else:
                    dve.wait_ge(s_top, nth(TOP_OPS, p, k - 1))
                if k == 0:
                    ins = nc.vector.reduce_max(few[:, 0, 0:CH], by_row(logits, E), axis=AX_X)
                elif k == 1:
                    ins = nc.vector.tensor_tensor(by_row(lg[:, 0, :], E), by_row(logits, E),
                                                  few[:, 0, 0:CH, None].to_broadcast([P, CH, E]), ALU.subtract)
                elif k == 2:
                    dve.wait_ge(s_exp, nth(1, p, 0))
                    ins = nc.vector.reduce_sum(few[:, 1, 0:CH], by_row(lg[:, 1, :], E), axis=AX_X)
                elif k == 3:
                    ins = nc.vector.reciprocal(few[:, 2, 0:CH], few[:, 1, 0:CH])
                elif k == 4:
                    ins = nc.vector.tensor_tensor(by_row(lg[:, 2, :], E), by_row(lg[:, 1, :], E),
                                                  few[:, 2, 0:CH, None].to_broadcast([P, CH, E]), ALU.mult)
                elif k == 5:
                    ins = nc.vector.tensor_tensor(by_row(lg[:, 3, :], E), by_row(lg[:, 2, :], E),
                                                  gate_b[:, None, :].to_broadcast([P, CH, E]), ALU.add)
                elif k == 6:
                    ins = nc.vector.tensor_tensor(few[:, 3, :], two[:, :, 0], two[:, :, 1], ALU.add)
                elif k < 11:
                    ins = rank(few[:, 3, :], G, tie_g[:, :], few[:, 4, :], k - 7)
                elif k == 11:
                    ins = nc.vector.tensor_scalar(few[:, 5, :], few[:, 4, :], 2.0, -BIG, ALU.is_ge, ALU.mult)
                elif k == 12:
                    ins = nc.vector.tensor_tensor(lg[:, 4, :].rearrange("p (m two) -> p m two", two=2), two,
                                                  few[:, 5, :, None].to_broadcast([P, CH * G, 2]), ALU.add)
                elif k < 17:
                    ins = rank(lg[:, 4, :], E, tie_e[:, :], lg[:, 0, :], k - 13)
                else:
                    if later(p):
                        dve.wait_ge(s_combT, nth(1, p, -1))
                    ins = nc.vector.scalar_tensor_tensor(comb[:, :, 0:E], by_row(lg[:, 0, :], E), 2.0,
                                                         by_row(lg[:, 2, :], E), ALU.is_lt, ALU.mult)
                ins.then_inc(s_top, 1)

            def comb_lo(p):
                dve.wait_ge(s_combhi, nth(2, p, 1))
                nc.vector.tensor_tensor(combR[LO_ROW:LO_ROW + E1, :], psF[0:E1, bank_of("combine"), 0:TT],
                                        combR[0:E1, :].bitcast(F32), ALU.subtract).then_inc(s_comblo, 1)

            def glu_(p, c):
                r = ffn_rows(c)
                odd = glu[0:r, c % 2, 1, :]
                dve.wait_ge(s_sig, nth(FC, p, c))
                dve.wait_ge(s_lin, nth(FC, p, c))
                if c == 0 and later(p):
                    dve.wait_ge(s_down, nth(2, p, -1))
                nc.vector.scalar_tensor_tensor(gT[0:r, 0, :] if c == 0 else odd, th[0:r, :], 1.0, odd,
                                               ALU.add, ALU.mult).then_inc(s_glu, 1)

            def prod(p, c, part):
                r = ffn_rows(c)
                x = glu[0:r, c % 2, part, :]
                dve.wait_ge(s_up, nth(4 * FC, p, 4 * c + 2 + part))
                dve.wait_ge(s_up1, nth(2 * FC, p, 2 * c + part))
                nc.vector.scalar_tensor_tensor(x, psF[0:r, bank_of("up", c, 2 + part), 0:TT],
                                               b_13[0:r, c, 2 + part:3 + part], x,
                                               ALU.add, ALU.mult).then_inc(s_prod, 1)

            def clip(p, c, part):
                r = ffn_rows(c)
                x = glu[0:r, c % 2, part, :]
                dve.wait_ge(s_prod, nth(2 * FC, p, 2 * c + part))
                if part == 0:
                    nc.vector.tensor_scalar(x, x, LIMIT, None, ALU.min).then_inc(s_clip, 1)
                else:
                    nc.vector.tensor_scalar(x, x, LIMIT, -LIMIT, ALU.min, ALU.max).then_inc(s_clip, 1)

            def lin(p, c):
                r = ffn_rows(c)
                even, odd = glu[0:r, c % 2, 0, :], glu[0:r, c % 2, 1, :]
                dve.wait_ge(s_clip, nth(2 * FC, p, 2 * c + 1))
                nc.vector.scalar_tensor_tensor(odd, odd, 1.0, even, ALU.add, ALU.mult).then_inc(s_lin, 1)

            def finish(p, b):
                dve.wait_ge(s_down, nth(2, p, b))
                if b == 0:
                    dve.wait_ge(s_res, nth(1, p, 0))
                rows = outp[:, 2 * b:2 * b + 2, :]
                nc.vector.tensor_tensor(rows, psF[:, b, 0:2 * D].rearrange("p (k d) -> p k d", k=2), rows,
                                        ALU.add).then_inc(s_out, 1)

            program(dve, VECTOR, {"tokens": tokens, "stats_1": stats_1, "norm_1": norm_1, "lo_1": lo_1, "cos": cos,
                                  "sin": sin, "masked": masked, "row_stats": row_stats, "moments": moments,
                                  "variance": variance, "gate_mul": gate_mul, "factors": factors,
                                  "scale_a": scale_a, "add_attn": add_attn, "stats_2": stats_2, "norm_2": norm_2,
                                  "lo_2": lo_2, "pick": pick, "comb_lo": comb_lo, "prod": prod, "clip": clip,
                                  "lin": lin, "glu": glu_, "finish": finish},
                    before_attention, before_experts)

        @block.tensor
        def _(pe):
            pe.wait_ge(s_wtok, 16)
            pe.wait_ge(s_zero, 4)

            def before_attention():
                pe.wait_ge(s_attn_const, 16 * ATTN_CONSTS)
                pe.wait_ge(s_wlo, 2 * len(PIECES))

            def before_experts():
                pe.wait_ge(s_ffn_const, 16 * FFN_CONSTS)
                pe.wait_ge(s_wlo, 2 * len(PIECES))
                pe.wait_ge(s_set, SET_ALL)
                pe.wait_ge(s_sel, 2)

            def weights_by_tokens(out, w0, m, xA_hi, xA_lo, xB, xB_z):
                w = slice(w0, w0 + m)
                lo = slice(w0, w0 + m) if w0 < W_F else slice(w0 - W_F, w0 - W_F + m)
                nc.tensor.matmul(out, wA_hi[:, w], xA_hi[:, :], start=True, stop=False)
                nc.tensor.matmul(out, wA_lo[:, w], xA_hi[:, :], start=False, stop=False)
                nc.tensor.matmul(out, wA_hi[:, w], xA_lo[:, :], start=False, stop=False)
                nc.tensor.matmul(out, wB_hi[:, w], xB[:, :], start=False, stop=False)
                return nc.tensor.matmul(out, wB_lo[:, lo], xB_z[:, :], start=False, stop=True)

            def tokens_by_weights(out, c, w0, m, xA_hi, xA_lo, xB, xB_z):
                w = slice(w0, w0 + m)
                t = slice(row_col(c), row_col(c) + P)
                nc.tensor.matmul(out, xA_hi[:, t], wA_hi[:, w], start=True, stop=False)
                nc.tensor.matmul(out, xA_hi[:, t], wA_lo[:, w], start=False, stop=False)
                nc.tensor.matmul(out, xA_lo[:, t], wA_hi[:, w], start=False, stop=False)
                nc.tensor.matmul(out, xB[:, t], wB_hi[:, w], start=False, stop=False)
                return nc.tensor.matmul(out, xB_z[:, t], wB_lo[:, w], start=False, stop=True)

            def embed_(p, b):
                if b == 0:
                    pe.wait_ge(s_patch, 16 * nth(1, p, 0))
                    if later(p):
                        pe.wait_ge(s_gate, nth(HVC, p, -1))
                if b == 1 and later(p):
                    pe.wait_ge(s_gn, nth(GN_OPS, p - 1, 9))
                for k in range(2):
                    m, t0 = (P, 0) if k == 0 else (IMG_ROWS1, SECOND)
                    for c in range(PCH):
                        last = nc.tensor.matmul(psA[0:m, 2 + b, k * D:(k + 1) * D], patch[:, 2 * c + b, t0:t0 + m],
                                                w_tok[:, c, :], start=(c == 0), stop=(c == PCH - 1))
                if b == 1:
                    last.then_inc(s_tok, 1)

            def to_columns(bankA, bankB, s_done):
                for c in range(CH):
                    t = slice(row_col(c), row_col(c) + P)
                    last = nc.tensor.transpose(bankA[:, t], normed[:, c, 0:P], ident[:, :])
                last.then_inc(s_done, 1)
                for c in range(CH):
                    t = slice(row_col(c), row_col(c) + P)
                    last = nc.tensor.transpose(bankB[0:DB, t], normed[:, c, P:D], ident[:, :])
                last.then_inc(s_done, 1)

            def turn_1(p):
                pe.wait_ge(s_norm1, nth(CH, p, CH - 1))
                pe.wait_ge(s_hid, nth(2, p, 1))
                if not later(p):
                    pe.wait_ge(s_tok_const, 16 * TOK_CONSTS)
                    pe.wait_ge(s_set, SET_TOK)
                to_columns(psA[:, 2, :], psA[:, 3, :], s_x1T)

            def project(p, n):
                bank = psA[:, n % 4, :]
                if n == 0:
                    pe.wait_ge(s_x1lo, nth(2, p, 1))
                    if later(p):
                        pe.wait_ge(s_hid2, nth(2, p, -1))
                elif n >= 4:
                    pe.wait_ge(s_swap, 2 * nth(2 * H, p, n - 4))
                    pe.wait_ge(s_cos, nth(2 * H, p, n - 4))
                if n < 2 * H:
                    head, k = n // 2, n % 2
                    w0 = k * H * DQK + head * DQK
                    last = weights_by_tokens(bank[:, 0:TT], w0, P, x1A_hi, x1A_lo, x1B, x1B_z)
                else:
                    last = tokens_by_weights(bank[:, 0:HV], n - 2 * H, W_V, HV, x1A_hi, x1A_lo, x1B, x1B_z)
                last.then_inc(s_proj, 1)

            def score(p, h, b):
                if b == 0:
                    pe.wait_ge(s_rot, nth(2 * H, p, 2 * h + 1))
                if h == 0:
                    pe.wait_ge(s_val, nth(CH, p, b))
                else:
                    pe.wait_ge(s_prob, nth(2 * H, p, 2 * h - 2 + b))
                t0 = b * T
                q, k = qk[:, 2 * h, :], qk[:, 2 * h + 1, :]
                nc.tensor.matmul(psA[:, b, 0:T], k[:, t0:t0 + P], q[:, t0:t0 + T], start=True, stop=True)
                nc.tensor.matmul(psA[:, b, T:SC], k[:, t0 + SECOND:t0 + T], q[:, t0 + P:t0 + T],
                                 start=True, stop=True).then_inc(s_score, 1)

            def mix(p, h, b):
                c = h // 2
                bank = psA[:, 3 - c % 2, :]
                rows = slice(64 * (h % 2), 64 * (h % 2) + 64)
                v = slice(h * DV, (h + 1) * DV)
                if h % 2 == 0 and b == 0:
                    if c < 2:
                        pe.wait_ge(s_val, nth(CH, p, CH - 1))
                    else:
                        pe.wait_ge(s_ret, nth(HVC, p, c - 2))
                pe.wait_ge(s_prob, nth(2 * H, p, 2 * h + b))
                nc.tensor.matmul(bank[rows, b * T:(b + 1) * T], val[:, 2 * b, v], prob[:, b, 0:T],
                                 start=True, stop=False)
                nc.tensor.matmul(bank[rows, b * T + P:(b + 1) * T], val[:, 2 * b + 1, v], prob[:, b, T:SC],
                                 start=False, stop=True).then_inc(s_pv, 1)

            def head_sums(p):
                pe.wait_ge(s_ret, nth(HVC, p, HVC - 1))
                pe.wait_ge(s_gn, nth(GN_OPS, p, 8))
                nc.tensor.matmul(psA[:, 3, 0:4 * HVC], heads64[:, :], rmv[:, :, :].rearrange("p i s -> p (i s)"),
                                 start=True, stop=True).then_inc(s_gnsum, 1)

            def gate_in(p, c):
                if c < 2:
                    pe.wait_ge(s_prob, nth(2 * H, p, 2 * H - 2 + c))
                else:
                    pe.wait_ge(s_ret, nth(HVC, p, 1))
                weights_by_tokens(psA[:, c, 0:TT], W_G + c * P, P, x1A_hi, x1A_lo, x1B, x1B_z).then_inc(s_gproj, 1)

            def attn_out(p, b):
                pe.wait_ge(s_gated, nth(HVC, p, HVC - 1))
                for k in range(2):
                    t0 = row_col(2 * b + k)
                    for c in range(HVC):
                        last = nc.tensor.matmul(psA[:, b, k * D:(k + 1) * D], ret(c)[:, t0:t0 + P], w_o[:, c, :],
                                                start=(c == 0), stop=(c == HVC - 1))
                last.then_inc(s_wo, 1)

            def turn_2(p):
                pe.wait_ge(s_norm2, nth(CH, p, CH - 1))
                if later(p):
                    pe.wait_ge(s_exout, nth(FC - 1, p, -1))
                to_columns(psF[:, 2, :], psF[:, 3, :], s_x2T)

            def bank_for(p, *item):
                i = ROUND.index(item)
                if i == 0:
                    pe.wait_ge(s_x2lo, nth(2, p, 1))
                if i < 2:
                    if later(p):
                        pe.wait_ge(s_out, nth(2, p, -2 + i))
                elif i == 2:
                    pe.wait_ge(s_x2lo, nth(2, p, 0))
                elif i == 3:
                    pe.wait_ge(s_x2lo, nth(2, p, 1))
                else:
                    emptied(p, *ROUND[i - 4])
                return psF[:, i % 4, :]

            def emptied(p, kind, *at):
                if kind == "route":
                    pe.wait_ge(s_top, nth(TOP_OPS, p, 1))
                elif kind == "combine":
                    pe.wait_ge(s_comblo, nth(1, p, 0))
                elif kind == "spread":
                    pe.wait_ge(s_weight, nth(FC - 1, p, at[0] - 1))
                elif at[1] < 2:
                    pe.wait_ge(s_up1, nth(2 * FC, p, 2 * at[0] + at[1]))
                else:
                    pe.wait_ge(s_prod, nth(2 * FC, p, 2 * at[0] + at[1] - 2))

            def route(p):
                bank = bank_for(p, "route")
                rows = slice(SHARED, SHARED + E)
                pe.wait_ge(s_lgcol, nth(1, p, 0))
                nc.tensor.matmul(bank[:, 0:E], th[rows, 0:P], ident[rows, rows], start=True, stop=True)
                for c in range(1, CH):
                    last = nc.tensor.transpose(bank[:, c * E:(c + 1) * E], th[rows, row_col(c):row_col(c) + P],
                                               ident[rows, rows])
                last.then_inc(s_lgrow, 1)

            def combine(p):
                bank = bank_for(p, "combine")
                pe.wait_ge(s_top, nth(TOP_OPS, p, TOP_OPS - 1))
                for c in range(CH):
                    last = nc.tensor.transpose(bank[0:E1, row_col(c):row_col(c) + P], comb[:, c, :], ident[:, :])
                last.then_inc(s_combT, 1)

            def spread(p, c):
                bank = bank_for(p, "spread", c)
                if c == 1:
                    pe.wait_ge(s_comblo, nth(1, p, 0))
                nc.tensor.matmul(bank[:, 0:TT], sel[0:LO_ROW + E1, c - 1, :], combR[0:LO_ROW + E1, :],
                                 start=True, stop=True).then_inc(s_spread, 1)

            def up(p, c, part):
                r = ffn_rows(c) + (E if (c, part) == (0, 0) else 0)
                bank = bank_for(p, "up", c, part)
                weights_by_tokens(bank[0:r, 0:TT], up_col(c, part), r, x2A_hi, x2A_lo, x2B,
                                  x2B_z).then_inc(s_up, 1)

            def down(p, b, k):
                t0 = row_col(2 * b + k)
                out = psF[:, b, k * D:(k + 1) * D]
                if k == 0:
                    emptied(p, *[item for i, item in enumerate(ROUND) if i % 4 == b][-1])
                nc.tensor.matmul(out, combR[:, t0:t0 + P], b_2[:, :], start=True, stop=False)
                for c in range(FC):
                    r = ffn_rows(c)
                    if b == 0 and k == 0:
                        if c == 0:
                            pe.wait_ge(s_glu, nth(FC, p, 0))
                        else:
                            pe.wait_ge(s_exout, nth(FC - 1, p, c - 1))
                    last = nc.tensor.matmul(out, gT[0:r, c, t0:t0 + P], w_2[0:r, c, :],
                                            start=False, stop=(c == FC - 1))
                if k == 1:
                    last.then_inc(s_down, 1)

            program(pe, TENSOR, {"embed": embed_, "turn_1": turn_1, "project": project, "score": score, "mix": mix,
                                 "head_sums": head_sums, "gate_in": gate_in, "attn_out": attn_out,
                                 "turn_2": turn_2, "route": route, "combine": combine,
                                 "spread": spread, "up": up, "down": down},
                    before_attention, before_experts)


def _tables():
    import numpy as np
    half = DQK // 2
    pos = np.arange(T, dtype=np.float32)
    inv_freq = np.float32(1.0) / np.float32(10000.0) ** (np.arange(half, dtype=np.float32) / np.float32(half))
    angles = (inv_freq[:, None] * pos[None, :]).astype(np.float32).astype(np.float64)
    zeta = (np.arange(half, dtype=np.float64) + half) / DQK
    rot = np.zeros((P, 4, T), np.float32)
    for i, sign in enumerate((1.0, -1.0)):
        decay = zeta[:, None] ** (sign * pos[None, :].astype(np.float64) / 512.0)
        cos, sin = np.cos(angles) * decay, np.sin(angles) * decay
        rot[:, 2 * i] = np.concatenate([cos, cos])
        rot[:, 2 * i + 1] = np.concatenate([-sin, sin])
    t = np.arange(T)
    diff = t[None, :] - t[:, None]
    mask = np.zeros((P, H, SC), np.float32)
    for h in range(H):
        gamma = 1.0 - 2.0 ** (-(5 + h))
        d = np.where(diff >= 0, gamma ** np.maximum(diff, 0), 0.0)
        d = d / np.sqrt(np.maximum(d.sum(axis=0, keepdims=True), 1e-6)) * DQK ** -0.5
        mask[:, h, 0:T] = d[0:P]
        mask[P - SECOND:, h, T:] = d[P:, P:]
    heads = np.kron(np.eye(2), np.full((64, 64), 1.0 / 64)).astype(np.float32)
    sel = np.zeros((P, (FC - 1) * P), np.float32)
    for r in range(E * I):
        sel[r // I, r] = sel[LO_ROW + r // I, r] = 0.5
    return {
        "c_ident": np.eye(P, dtype=np.float32), "c_rot": rot, "c_mask": mask, "c_heads": heads, "c_sel": sel,
        "c_tie_g": np.tril(np.ones((G, G), np.float32), -1).reshape(1, -1),
        "c_tie_e": np.tril(np.ones((E, E), np.float32), -1).reshape(1, -1),
    }


def kernel(x, txt, L0_tok_W, L0_tok_b, L0_tok_class_token, L0_tok_pos_embed, L0_attn_Wq, L0_attn_Wk, L0_attn_Wv,
           L0_attn_Wg, L0_attn_Wo, L0_attn_gn_weight, L0_attn_gn_bias, L0_ffn_gate_w, L0_ffn_gate_b, L0_ffn_W1,
           L0_ffn_B1, L0_ffn_W3, L0_ffn_B3, L0_ffn_W2, L0_ffn_B2, L0_ffn_Ws1, L0_ffn_Bs1, L0_ffn_Ws3, L0_ffn_Bs3,
           L0_ffn_Ws2, L0_ffn_Bs2):
    import numpy as np
    import concourse.bacc as bacc
    from concourse import mybir as _mybir
    from concourse.bass_utils import run_bass_kernel_spmd

    def f(v):
        return np.asarray(v)

    def experts(w, ws):
        return np.concatenate([f(ws)[None], f(w)]).transpose(1, 0, 2).reshape(D, HID, 2)

    up1, up3 = experts(L0_ffn_W1, L0_ffn_Ws1), experts(L0_ffn_W3, L0_ffn_Ws3)
    bias1 = np.concatenate([f(L0_ffn_Bs1)[None], f(L0_ffn_B1)]).reshape(HID, 2)
    bias3 = np.concatenate([f(L0_ffn_Bs3)[None], f(L0_ffn_B3)]).reshape(HID, 2)
    cols = [f(L0_attn_Wq), f(L0_attn_Wk), f(L0_attn_Wv), f(L0_attn_Wg)]
    b_13 = np.zeros((P, FC, 4), np.float32)
    for c in range(FC):
        r = slice(ffn_first(c), ffn_first(c) + ffn_rows(c))
        cols += [up1[:, r, 0]] + ([f(L0_ffn_gate_w).T] if c == 0 else []) + [up1[:, r, 1], up3[:, r, 0], up3[:, r, 1]]
        b_13[0:ffn_rows(c), c, 0:2] = bias1[r]
        b_13[0:ffn_rows(c), c, 2:4] = bias3[r]
    n = 14
    ps = 16
    patches = f(x).reshape(PAIRS, 2, 3, n, ps, n, ps).transpose(0, 2, 4, 6, 1, 3, 5)
    patches = patches.reshape(PAIRS, PCH, P, 2, PATCHES).transpose(0, 2, 1, 3, 4).reshape(PAIRS, P, PCH * 2, PATCHES)
    ins = {
        "patches": patches,
        "txt": f(txt),
        "w_stack": np.concatenate(cols, axis=1),
        "w_tok": f(L0_tok_W).T.reshape(PCH, P, D).transpose(1, 0, 2),
        "tok_b": f(L0_tok_b).reshape(1, D),
        "cls": f(L0_tok_class_token),
        "pos": f(L0_tok_pos_embed),
        "w_o": f(L0_attn_Wo).reshape(HVC, P, D).transpose(1, 0, 2),
        "gn_wb": np.concatenate([f(L0_attn_gn_weight).reshape(HVC, P).T, f(L0_attn_gn_bias).reshape(HVC, P).T], axis=1),
        "gate_b": f(L0_ffn_gate_b).reshape(1, E),
        "w_2": np.concatenate([f(L0_ffn_Ws2), f(L0_ffn_W2).reshape(E * I, D)]),
        "b_2": np.concatenate([f(L0_ffn_B2), f(L0_ffn_Bs2).reshape(1, D)]),
        "b_13": b_13,
        **_tables(),
    }
    ins = {k: np.ascontiguousarray(v) for k, v in ins.items()}
    nc = bacc.Bacc("TRN2", target_bir_lowering=False, num_devices=1)
    aps = {k: nc.dram_tensor("in_" + k, v.shape, _mybir.dt.from_np(v.dtype), kind="ExternalInput").ap() for k, v in ins.items()}
    aps["out"] = nc.dram_tensor("out", (IMAGES, T, D), F32, kind="ExternalOutput").ap()
    fusion_kernel(nc, aps)
    r = run_bass_kernel_spmd(nc, [{"in_" + k: v for k, v in ins.items()}], core_ids=[0])
    return r.results[0]["out"]
```
